# Optimizing a Trainium2 kernel written in Bass

```python
import numpy as np
import jax
import jax.numpy as jnp

def _softmax(x, axis=-1):
    return jax.nn.softmax(x, axis=axis)

def _gelu(x):
    return jax.nn.gelu(x, approximate=True)

def _silu(x):
    return jax.nn.silu(x)

def _sigmoid(x):
    return jax.nn.sigmoid(x)

def _layernorm(x, axis=-1, eps=1e-05):
    m = jnp.mean(x, axis=axis, keepdims=True)
    v = jnp.var(x, axis=axis, keepdims=True)
    return (x - m) / jnp.sqrt(v + eps)

def _scatter_add(tgt, idx, src, axis=0):
    return tgt.at[idx].add(src)

def _segment_sum(src, seg, n):
    return jax.ops.segment_sum(src, seg, n)
kernel_name = 'mk_prb_d1_jaxref_r4_9857e3'

def setup_inputs(seed: int=0):
    np.random.seed(seed)
    _w = jnp.asarray

    def _L0_attn_setup():
        import jax, jax.numpy as jnp
        import numpy as np
        import math
        DIM, NHEAD, WINDOW = (256, 16, 128)
        DK = DIM // NHEAD
        key = jax.random.key(seed)
        k1, k2, k3 = jax.random.split(key, 3)
        x = jax.random.normal(k1, (4, 512, DIM), dtype=jnp.float32)
        w_qkv = jax.random.normal(k2, (3 * DIM, DIM), dtype=jnp.float32) * (1.0 / math.sqrt(DIM))
        w_proj = jax.random.normal(k3, (DIM, DIM), dtype=jnp.float32) * (1.0 / math.sqrt(DIM))
        return {'x': x, 'w_qkv': w_qkv, 'w_proj': w_proj}
    _L0_attn_in = _L0_attn_setup()

    def _L0_ffn_setup():
        import jax, jax.numpy as jnp
        import numpy as np
        B, S, H, I, E, K = (2, 128, 256, 128, 64, 8)
        key = jax.random.key(seed)
        ks = jax.random.split(key, 8)
        return {'hidden_states': jax.random.normal(ks[0], (B, S, H), dtype=jnp.float32), 'router_w': jax.random.normal(ks[1], (H, E), dtype=jnp.float32) * 0.02, 'shared_gate_w': jax.random.normal(ks[2], (H, I), dtype=jnp.float32) * 0.02, 'shared_up_w': jax.random.normal(ks[3], (H, I), dtype=jnp.float32) * 0.02, 'shared_down_w': jax.random.normal(ks[4], (I, H), dtype=jnp.float32) * 0.02, 'expert_gate_k': jax.random.normal(ks[5], (E, H, I), dtype=jnp.float32) * 0.02, 'expert_up_k': jax.random.normal(ks[6], (E, H, I), dtype=jnp.float32) * 0.02, 'expert_down_k': jax.random.normal(ks[7], (E, I, H), dtype=jnp.float32) * 0.02}
    _L0_ffn_in = _L0_ffn_setup()
    _d = {'L0_attn_x': _L0_attn_in['x'], 'L0_attn_w_qkv': _L0_attn_in['w_qkv'], 'L0_attn_w_proj': _L0_attn_in['w_proj'], 'L0_ffn_router_w': _L0_ffn_in['router_w'], 'L0_ffn_shared_gate_w': _L0_ffn_in['shared_gate_w'], 'L0_ffn_shared_up_w': _L0_ffn_in['shared_up_w'], 'L0_ffn_shared_down_w': _L0_ffn_in['shared_down_w'], 'L0_ffn_expert_gate_k': _L0_ffn_in['expert_gate_k'], 'L0_ffn_expert_up_k': _L0_ffn_in['expert_up_k'], 'L0_ffn_expert_down_k': _L0_ffn_in['expert_down_k']}
    _x0 = _d['L0_attn_x']
    _d['L0_attn_x'] = jax.random.normal(jax.random.fold_in(jax.random.key(seed), 1), (4, 1024, 256), dtype=_x0.dtype)
    del _x0
    return _d

def reference(L0_attn_x, L0_attn_w_qkv, L0_attn_w_proj, L0_ffn_router_w, L0_ffn_shared_gate_w, L0_ffn_shared_up_w, L0_ffn_shared_down_w, L0_ffn_expert_gate_k, L0_ffn_expert_up_k, L0_ffn_expert_down_k):

    def _L0_attn_ref(x, w_qkv, w_proj):
        import jax, jax.numpy as jnp
        import numpy as np
        import math
        DIM, NHEAD, WINDOW = (256, 16, 128)
        DK = DIM // NHEAD
        B, T, C = x.shape
        qkv = jnp.einsum('btc,oc->bto', x, w_qkv)
        q, k, v = jnp.split(qkv, 3, axis=-1)

        def heads(t):
            return t.reshape(B, T, NHEAD, DK).transpose(0, 2, 1, 3)
        q, k, v = (heads(q), heads(k), heads(v))
        attn = jnp.einsum('bhqd,bhkd->bhqk', q, k) / math.sqrt(DK)
        idx = jnp.arange(T)
        mask = jnp.abs(idx[None, :] - idx[:, None]) > WINDOW
        attn = jnp.where(mask[None, None], -1000000000.0, attn)
        p = jax.nn.softmax(attn, axis=-1)
        out = jnp.einsum('bhqk,bhkd->bhqd', p, v)
        out = out.transpose(0, 2, 1, 3).reshape(B, T, C)
        return jnp.einsum('btc,oc->bto', out, w_proj)

    def _L0_ffn_ref(hidden_states, router_w, shared_gate_w, shared_up_w, shared_down_w, expert_gate_k, expert_up_k, expert_down_k):
        import jax, jax.numpy as jnp
        import numpy as np
        B, S, H, I, E, K = (2, 128, 256, 128, 64, 8)
        logits = jnp.einsum('bsh,he->bse', hidden_states.astype(jnp.float32), router_w)
        affinity = jax.nn.sigmoid(logits)
        top_scores, top_idx = jax.lax.top_k(affinity, K)
        top_w = top_scores / (jnp.sum(top_scores, axis=-1, keepdims=True) + 1e-09)
        one_hot = jax.nn.one_hot(top_idx, E, dtype=top_w.dtype)
        router_mask = jnp.einsum('bske,bsk->bse', one_hot, top_w).astype(hidden_states.dtype)
        shared = jnp.einsum('bsi,ih->bsh', jax.nn.silu(hidden_states @ shared_gate_w) * (hidden_states @ shared_up_w), shared_down_w)
        gate_out = jnp.einsum('bsh,ehi->bsei', hidden_states, expert_gate_k)
        up_out = jnp.einsum('bsh,ehi->bsei', hidden_states, expert_up_k)
        expert_act = jax.nn.silu(gate_out) * up_out
        routed = jnp.einsum('bsei,eih->bsh', expert_act * router_mask[..., None], expert_down_k)
        return shared + routed
    x = L0_attn_x
    xn = _layernorm(x, axis=-1)
    x = x + _L0_attn_ref(xn, L0_attn_w_qkv, L0_attn_w_proj) + _L0_ffn_ref(xn, L0_ffn_router_w, L0_ffn_shared_gate_w, L0_ffn_shared_up_w, L0_ffn_shared_down_w, L0_ffn_expert_gate_k, L0_ffn_expert_up_k, L0_ffn_expert_down_k)
    return x

_drawn_inputs = setup_inputs


def setup_inputs(seed=0):
    import zlib

    import numpy as np

    out = dict(_drawn_inputs(seed))
    spreads = {}
    factors = {'L0_ffn_router_w': 8.0,
     'L0_ffn_shared_gate_w': 4.846,
     'L0_ffn_shared_up_w': 4.784,
     'L0_ffn_shared_down_w': 4.809,
     'L0_ffn_expert_gate_k': 8.0,
     'L0_ffn_expert_up_k': 8.0,
     'L0_ffn_expert_down_k': 8.0}
    for name, (base, spread) in spreads.items():
        noise = np.random.default_rng([zlib.crc32(name.encode()), seed]).standard_normal(out[name].shape)
        drawn = base * np.exp(spread * noise) if base else spread * noise
        out[name] = jnp.asarray(drawn.astype(out[name].dtype))
    for name, factor in factors.items():
        out[name] = (out[name] * factor).astype(out[name].dtype)
    return out
```

```python
from contextlib import ExitStack
from itertools import count

import numpy as np
import concourse.bass as bass
from concourse import mybir

F32 = mybir.dt.float32
BF16 = mybir.dt.bfloat16
I32 = mybir.dt.int32
ALU = mybir.AluOpType
ACT = mybir.ActivationFunctionType
AX = mybir.AxisListType

P = 128
B, T, D = 4, 1024, 256
NTOK = B * T
NTILE = NTOK // P
NH, DK = 16, 16
TT = T // P
NE, K, I = 64, 8, 128
EPS = 1e-5
NEG = -1.0e30

CH = 512
NCH = NTOK // CH
TPC = CH // P

NSPLIT = 3
KS = 6 * DK
KM = KS + 2
NU = B * NH
HG = 4
NG = NU // HG

NB_ROUTED = (NTOK * K) // P + NE
NB = NB_ROUTED + NTILE
W_COL, ID_COL = D, D + NE + 1
ROW = D + NE + 2
WCOLS = 2 * 2 * I + D
NACC = 4
XR = 16
WR = 8
MB = 3
E_F, NEW_F, WAT_F = 0, 1, 2
NFIELD = 3


class Chain:

    def __init__(self, engine, semaphore, base=0):
        self.engine, self.semaphore, self.base, self.n = engine, semaphore, base, 0

    def done(self, instruction):
        instruction.then_inc(self.semaphore, 1)
        self.n += 1

    def wait(self):
        self.engine.wait_ge(self.semaphore, self.base + self.n)


def project_and_route(nc, ctx, x, w_qk, w_vr, c_f32, c_ids, keep):
    qk_d, rows_d, slots_d, meta_d, acc_d = keep["dram"]
    ident, cb, v_sb, meta, idx8, zeros, banks, fill_done = keep["sbuf"]
    ident_b, before, ones_b = (cb[:, k * P:(k + 1) * P] for k in range(3))

    def sb(name, shape, dt=F32):
        return ctx.enter_context(nc.sbuf_tensor(name, shape, dt))

    def sem(name):
        return ctx.enter_context(nc.semaphore(name))

    consts = sb("consts_f32", [P, 6 * P + 2 * MB])
    wqk = sb("wqk", [P, 2, 2 * D])
    wvr = sb("wvr", [P, 2, D + NE])
    xin = sb("xin", [P, 2, TPC, D])
    xn = sb("xn", [P, 2, TPC, D])
    xT = sb("xT", [P, 2, 2, CH])
    stats = sb("stats", [P, TPC, 6])
    small = sb("small", [P, 10, TPC])
    parts = sb("parts", [P, 2, 4, NSPLIT, CH], BF16)
    rest = sb("rest", [P, 2, CH])
    rows = sb("rows", [P, NTILE, ROW])
    ids = sb("ids", [P, NTILE + 1], I32)
    template = sb("template", [P, ROW])
    logits = sb("logits", [P, NTILE, NE])
    aff = sb("aff", [P, NTILE, NE])
    work = sb("work", [P, NTILE, NE])
    chosen = sb("chosen", [P, NTILE, NE], BF16)
    base = sb("base", [P, NTILE + 1, NE])
    top8 = sb("top8", [P, NTILE, K])
    rsum = sb("rsum", [P, NTILE])
    blk = sb("blk", [P, 8, NE])
    blk_i = sb("blk_i", [P, NE], I32)
    junk = sb("junk", [P, NE])
    cols = sb("cols", [P, 4, MB])
    meta_c = sb("meta_c", [P, NFIELD, MB], I32)

    consts_in, weights_in = sem("consts_in"), sem("weights_in")
    x_in = [sem("x_in0"), sem("x_in1")]
    consts_ready = sem("consts_ready")
    dve_a = sem("dve_a")
    tick = sem("project_tick")
    var_ready, std_ready, xn_ready = sem("var_ready"), sem("std_ready"), sem("xn_ready")
    xn_free_pool, xn_free_pe = sem("xn_free_pool"), sem("xn_free_pe")
    xTp_ready = sem("xTp_ready")
    xT0_ready, xT1_ready = sem("xT0_ready"), sem("xT1_ready")
    qk_ready, hi_ready, rest_ready, mid_ready, lo_ready = (
        sem("qk_ready"), sem("hi_ready"), sem("rest_ready"), sem("mid_ready"), sem("lo_ready"))
    parts_out = [sem("parts_out0"), sem("parts_out1")]
    parts_free = sem("parts_free")
    vr_ready, vr_free = sem("vr_ready"), sem("vr_free")
    XT0 = 8

    with nc.Block() as block:
        @block.sync
        def _(sp):
            sp.dma_start(consts[:, :], c_f32).then_inc(consts_in, 16)
            sp.dma_start(ids[:, :], c_ids).then_inc(consts_in, 16)

            def load(c, j):
                sp.dma_start(xin[:, j, :, :], x[bass.ds(c * TPC, TPC), :, :].rearrange("n p c -> p n c")
                             ).then_inc(x_in[j], 16)

            load(0, 0)
            load(1, 1)
            sp.dma_start(wqk[:, :, :], w_qk).then_inc(weights_in, 16)
            sp.dma_start(wvr[:, :, :], w_vr).then_inc(weights_in, 16)
            sp.sem_inc(parts_free, 2)

            def step(b, more):
                for j in range(2):
                    if more:
                        sp.wait_ge(xn_ready, b * 2 + j + 1)
                        load(b * 2 + j + 2, j)
                    sp.wait_ge(lo_ready, b * 8 + 4 * j + 6)
                    for o in range(4):
                        dst = qk_d[o // 2, :, bass.ds(b * D + (o % 2) * P, P), j * CH:(j + 1) * CH]
                        sp.dma_start(dst.rearrange("s p t -> p s t"),
                                     parts[:, j, o, :, :]).then_inc(parts_out[j], 16)
                    sp.wait_ge(parts_out[j], b * 64 + 64)
                    sp.sem_inc(parts_free, 1)

            with sp.Fori(0, NCH // 2 - 1) as b:
                step(b, True)
            step(NCH // 2 - 1, False)

        @block.scalar
        def _(act):
            act.wait_ge(consts_ready, 3)
            n = NB_ROUTED // 8
            for k in range(8):
                act.dma_start(slots_d[k * n * P:(k + 1) * n * P, :].rearrange("(n p) c -> p n c", p=P),
                              template[:, :].unsqueeze(1).to_broadcast([P, n, ROW])).then_inc(fill_done, 16)
            for k in range(NACC):
                act.dma_start(acc_d[k][0:NTOK, :].rearrange("(p m n) c -> p m (n c)", p=P, n=4),
                              zeros[:, :].unsqueeze(1).to_broadcast([P, 8, 1024])).then_inc(fill_done, 16)
                act.dma_start(acc_d[k][NTOK:NTOK + P, :], zeros[:, 0:D]).then_inc(fill_done, 16)
            act.sem_inc(vr_free, 2)
            with act.Fori(0, NCH // 2) as b:
                for j in range(2):
                    c = b * 2 + j
                    act.wait_ge(var_ready, c + 1)
                    nc.scalar.activation(small[:, 4, :], small[:, 3, :], ACT.Sqrt).then_inc(std_ready, 1)
                    act.wait_ge(vr_ready, c * 4 + XT0 - 4)
                    act.wait_ge(xTp_ready, c + 1)
                    nc.scalar.copy(xT[:, j, 0, :], banks[0][:, :]).then_inc(xT0_ready, 1)
                    act.wait_ge(parts_free, c + 1)
                    for o in range(4):
                        act.wait_ge(qk_ready, c * 4 + o + 1)
                        nc.scalar.activation(parts[:, j, o, 0, :], banks[2 + o % 2][:, :], ACT.Copy,
                                             scale=0.25 if o < 2 else 1.0).then_inc(hi_ready, 1)
                    for t in range(TPC):
                        act.wait_ge(vr_ready, c * 4 + XT0 + t + 1)
                        nc.scalar.copy(v_sb[:, bass.ds(b * NH, NH), j * TPC + t, :],
                                       banks[4 + t % 2][:, 0:D].rearrange("p (h d) -> p h d", h=NH))
                        nc.scalar.copy(logits[:, bass.ds(c * TPC + t, 1), :],
                                       banks[4 + t % 2][:, D:D + NE]).then_inc(vr_free, 1)

        @block.gpsimd
        def _(pool):
            pool.sem_inc(xn_free_pool, 2)
            pool.sem_inc(lo_ready, 2)
            with pool.Fori(0, NCH // 2) as b:
                for j in range(2):
                    c = b * 2 + j
                    pool.wait_ge(xn_ready, c + 1)
                    pool.sem_inc(tick, 1)
                    nc.gpsimd.tensor_copy(rows[:, bass.ds(c * TPC, TPC), 0:D],
                                          xn[:, j, :, :]).then_inc(xn_free_pool, 1)
                    for o in range(4):
                        pool.wait_ge(rest_ready, c * 4 + o + 3)
                        pool.sem_inc(tick, 1)
                        nc.gpsimd.tensor_copy(parts[:, j, o, 1, :], rest[:, o % 2, :]).then_inc(mid_ready, 1)
                        pool.wait_ge(mid_ready, c * 4 + o + 1)
                        nc.gpsimd.tensor_tensor(parts[:, j, o, 2, :], rest[:, o % 2, :], parts[:, j, o, 1, :],
                                                ALU.subtract).then_inc(lo_ready, 1)

        @block.vector
        def _(dve):
            dve.wait_ge(consts_in, 32)
            nc.vector.memset(zeros[:, :], 0.0).then_inc(consts_ready, 1)
            nc.vector.memset(template[:, 0:ID_COL], 0.0).then_inc(consts_ready, 1)
            nc.vector.tensor_copy(template[:, ID_COL:ROW].bitcast(I32), ids[:, NTILE:NTILE + 1]
                                  ).then_inc(consts_ready, 1)
            nc.vector.tensor_copy(ident[:, :], consts[:, 0:P]).then_inc(consts_ready, 1)
            nc.vector.tensor_copy(cb[:, :], consts[:, P:6 * P]).then_inc(consts_ready, 1)
            nc.vector.tensor_copy(rows[:, :, ID_COL].bitcast(I32), ids[:, 0:NTILE]).then_inc(consts_ready, 1)
            nc.vector.memset(rows[:, :, ID_COL - 1], 1.0).then_inc(consts_ready, 1)
            dve.sem_inc(rest_ready, 2)
            with dve.Fori(0, NCH // 2) as b:
                for j in range(2):
                    c = b * 2 + j
                    chain = Chain(dve, dve_a, c * 15)
                    dve.wait_ge(x_in[j], b * 16 + 16)
                    for t in range(TPC):
                        chain.done(nc.vector.bn_stats(stats[:, t, :], xin[:, j, t, :]))
                    chain.wait()
                    chain.done(nc.vector.tensor_tensor(small[:, 0, :], stats[:, :, 1], stats[:, :, 4], ALU.add))
                    chain.done(nc.vector.tensor_tensor(small[:, 1, :], stats[:, :, 1], stats[:, :, 4],
                                                       ALU.subtract))
                    chain.done(nc.vector.tensor_tensor(small[:, 2, :], stats[:, :, 2], stats[:, :, 5], ALU.add))
                    chain.wait()
                    chain.done(nc.vector.tensor_scalar(small[:, 5, :], small[:, 0, :], 0.5, None, ALU.mult))
                    chain.done(nc.vector.tensor_tensor(small[:, 1, :], small[:, 1, :], small[:, 1, :], ALU.mult))
                    chain.done(nc.vector.tensor_scalar(small[:, 2, :], small[:, 2, :], 1.0 / D, EPS,
                                                       ALU.mult, ALU.add))
                    chain.wait()
                    nc.vector.scalar_tensor_tensor(small[:, 3, :], small[:, 1, :], 0.25, small[:, 2, :],
                                                   ALU.mult, ALU.add).then_inc(var_ready, 1)
                    dve.wait_ge(std_ready, c + 1)
                    chain.done(nc.vector.reciprocal(small[:, 6, :], small[:, 4, :]))
                    chain.wait()
                    chain.done(nc.vector.tensor_tensor(small[:, 7, :], small[:, 6, :], small[:, 6, :], ALU.mult))
                    chain.wait()
                    chain.done(nc.vector.tensor_tensor(small[:, 8, :], small[:, 7, :], small[:, 3, :], ALU.mult))
                    chain.wait()
                    chain.done(nc.vector.tensor_scalar(small[:, 7, :], small[:, 8, :], -0.5, 1.5,
                                                       ALU.mult, ALU.add))
                    chain.wait()
                    chain.done(nc.vector.tensor_tensor(small[:, 9, :], small[:, 6, :], small[:, 7, :], ALU.mult))
                    chain.wait()
                    assert chain.n == 15
                    dve.wait_ge(xn_free_pool, c + 1)
                    dve.wait_ge(xn_free_pe, c + 1)
                    for t in range(TPC):
                        last = nc.vector.tensor_scalar(xn[:, j, t, :], xin[:, j, t, :], small[:, 5, t:t + 1],
                                                       small[:, 9, t:t + 1], ALU.subtract, ALU.mult)
                    last.then_inc(xn_ready, 1)
                    dve.wait_ge(vr_ready, c * 4 + XT0 - 4)
                    dve.wait_ge(xTp_ready, c + 1)
                    nc.vector.tensor_copy(xT[:, j, 1, :], banks[1][:, :]).then_inc(xT1_ready, 1)
                    for o in range(4):
                        dve.wait_ge(hi_ready, c * 4 + o + 1)
                        dve.wait_ge(lo_ready, c * 4 + o + 1)
                        nc.vector.scalar_tensor_tensor(rest[:, o % 2, :], banks[2 + o % 2][:, :],
                                                       0.25 if o < 2 else 1.0, parts[:, j, o, 0, :],
                                                       ALU.mult, ALU.subtract).then_inc(rest_ready, 1)

        @block.tensor
        def _(pe):
            pe.sem_inc(xn_free_pe, 2)
            pe.sem_inc(vr_ready, XT0)
            pe.wait_ge(consts_ready, 7)
            pe.wait_ge(weights_in, 32)

            def transposes(c, j):
                pe.wait_ge(xn_ready, c + 1)
                for t in range(TPC):
                    for h in range(2):
                        last = nc.tensor.transpose(banks[h][:, t * P:(t + 1) * P],
                                                   xn[:, j, t, h * P:(h + 1) * P], ident[:, :])
                last.then_inc(xTp_ready, 1)

            def products(c, j):
                pe.wait_ge(xT0_ready, c + 1)
                pe.wait_ge(xT1_ready, c + 1)
                pe.sem_inc(xn_free_pe, 1)
                for o in range(4):
                    pe.wait_ge(rest_ready, c * 4 + o + 1)
                    for h in range(2):
                        last = nc.tensor.matmul(banks[2 + o % 2][:, :], wqk[:, h, o * P:(o + 1) * P],
                                                xT[:, j, h, :], start=(h == 0), stop=(h == 1))
                    last.then_inc(qk_ready, 1)
                for t in range(TPC):
                    pe.wait_ge(vr_free, c * 4 + t + 1)
                    for h in range(2):
                        last = nc.tensor.matmul(banks[4 + t % 2][:, 0:D + NE], xT[:, j, h, t * P:(t + 1) * P],
                                                wvr[:, h, :], start=(h == 0), stop=(h == 1))
                    last.then_inc(vr_ready, 1)

            with pe.Fori(0, NCH // 2) as b:
                for j in range(2):
                    transposes(b * 2 + j, j)
                    products(b * 2 + j, j)

    dve_r = sem("dve_r")
    ex_ready, chosen_ready, count_ready = sem("ex_ready"), sem("chosen_ready"), sem("count_ready")
    rows_ready, rows_out, meta_ready, meta_out, meta_in = (
        sem("rows_ready"), sem("rows_out"), sem("meta_ready"), sem("meta_out"), sem("meta_in"))

    with nc.Block() as block:
        @block.scalar
        def _(act):
            nc.scalar.activation(aff[:, :, :], logits[:, :, :], ACT.Exp, scale=-1.0).then_inc(ex_ready, 1)

        @block.tensor
        def _(pe):
            pe.wait_ge(chosen_ready, 1)
            for k in range(4):
                m = chosen[:, 8 * k:8 * k + 8, :].rearrange("p n e -> p (n e)")
                nc.tensor.matmul(banks[4 + k][:, :], ones_b, m, start=True, stop=True)
                last = nc.tensor.matmul(banks[k][:, :], before, m, start=True, stop=True)
            last.then_inc(count_ready, 1)

        @block.sync
        def _(sp):
            sp.wait_ge(rows_ready, 1)
            sp.dma_start(rows_d.rearrange("(n p) c -> p n c", p=P), rows[:, :, :]).then_inc(rows_out, 16)
            sp.dma_start(slots_d[NB_ROUTED * P:NB * P, :].rearrange("(n p) c -> p n c", p=P),
                         rows[:, :, :]).then_inc(rows_out, 16)
            sp.wait_ge(meta_ready, 1)
            sp.dma_start(meta_d.rearrange("f (c p) -> p f c", p=P), meta_c[:, :, :],
                         allow_slow_non_contiguous=True).then_inc(meta_out, 16)
            sp.wait_ge(meta_out, 16)
            sp.dma_start(meta[:, :, :], meta_d.unsqueeze(0)).then_inc(meta_in, 16)
            sp.wait_ge(rows_out, 32)
            sp.wait_ge(meta_in, 16)

        @block.vector
        def _(dve):
            chain = Chain(dve, dve_r)
            dve.wait_ge(ex_ready, 1)
            chain.done(nc.vector.tensor_scalar(work[:, :, :], aff[:, :, :], 1.0, None, ALU.add))
            chain.wait()
            chain.done(nc.vector.reciprocal(aff[:, :, :], work[:, :, :]))
            chain.wait()
            for n in range(NTILE):
                chain.done(nc.vector.max(top8[:, n, :], aff[:, n, :]))
            chain.wait()
            for n in range(NTILE):
                chain.done(nc.vector.match_replace(work[:, n, :], top8[:, n, :], aff[:, n, :], -1.0))
            chain.wait()
            nc.vector.tensor_scalar(chosen[:, :, :], work[:, :, :], 0.0, None, ALU.is_lt).then_inc(chosen_ready, 1)
            chain.done(nc.vector.tensor_reduce(rsum[:, :], top8[:, :, :], AX.X, ALU.add))
            chain.wait()
            chain.done(nc.vector.tensor_scalar(rsum[:, :], rsum[:, :], 1e-9, None, ALU.add))
            chain.wait()
            chain.done(nc.vector.reciprocal(junk[:, 0:NTILE], rsum[:, :]))
            dve.wait_ge(chosen_ready, 1)
            chain.done(nc.vector.tensor_tensor(work[:, :, :], aff[:, :, :], chosen[:, :, :], ALU.mult))
            chain.wait()
            nc.vector.tensor_tensor(rows[:, :, W_COL:W_COL + NE], work[:, :, :],
                                    junk[:, 0:NTILE].unsqueeze(2).to_broadcast([P, NTILE, NE]),
                                    ALU.mult).then_inc(rows_ready, 1)
            dve.wait_ge(count_ready, 1)
            chain.done(nc.vector.memset(base[:, 0, :], 0.0))
            for n in range(NTILE):
                chain.wait()
                chain.done(nc.vector.tensor_tensor(base[:, n + 1, :], base[:, n, :],
                                                   banks[4 + n // 8][:, (n % 8) * NE:(n % 8 + 1) * NE], ALU.add))
            chain.wait()
            chain.done(nc.vector.tensor_scalar(blk_i[:, :], base[:, NTILE, :], float(P - 1), None, ALU.add))
            chain.wait()
            chain.done(nc.vector.tensor_scalar(blk_i[:, :], blk_i[:, :], 7, None, ALU.logical_shift_right))
            chain.wait()
            nblk, ends, starts, some, one = (blk[:, k, :] for k in range(5))
            chain.done(nc.vector.tensor_copy(nblk, blk_i[:, :]))
            chain.done(nc.vector.memset(one, 1.0))
            chain.wait()
            chain.done(nc.vector.tensor_tensor_scan(ends, one, nblk, 0.0, ALU.mult, ALU.add))
            chain.done(nc.vector.tensor_scalar(some, nblk, 0.0, None, ALU.is_gt))
            chain.wait()
            chain.done(nc.vector.tensor_tensor(starts, ends, nblk, ALU.subtract))
            chain.wait()
            chain.done(nc.vector.tensor_scalar(starts, starts, float(P), 1.0, ALU.mult, ALU.add))
            chain.wait()
            chain.done(nc.vector.tensor_tensor(base[:, 0:NTILE, :], base[:, 0:NTILE, :],
                                               starts.unsqueeze(1).to_broadcast([P, NTILE, NE]), ALU.add))
            chain.wait()
            for k in range(4):
                chain.done(nc.vector.tensor_tensor(
                    work[:, 8 * k:8 * k + 8, :].rearrange("p n e -> p (n e)"), banks[k][:, :],
                    base[:, 8 * k:8 * k + 8, :].rearrange("p n e -> p (n e)"), ALU.add))
            chain.wait()
            chain.done(nc.vector.tensor_tensor(work[:, :, :], work[:, :, :], chosen[:, :, :], ALU.mult))
            chain.wait()
            for n in range(NTILE):
                chain.done(nc.vector.max(top8[:, n, :], work[:, n, :]))
            chain.wait()
            chain.done(nc.vector.tensor_scalar(idx8[:, :, :], top8[:, :, :], -1.0, None, ALU.add))
            for c in range(MB):
                for f, of, col in ((0, one, c), (1, some, c), (2, some, MB + c)):
                    chain.done(nc.vector.scalar_tensor_tensor(
                        junk[:, :], ends, consts[:, 6 * P + col:6 * P + col + 1], of, ALU.is_le, ALU.mult,
                        accum_out=cols[:, f, c:c + 1]))
                    chain.wait()
            chain.done(nc.vector.tensor_tensor(cols[:, 3, :], cols[:, 1, :], cols[:, 2, :], ALU.subtract))
            chain.wait()
            chain.done(nc.vector.memset(cols[0:1, 3, 0:1], 1.0))
            chain.done(nc.vector.tensor_copy(meta_c[:, E_F, :], cols[:, 0, :]))
            chain.done(nc.vector.tensor_copy(meta_c[:, WAT_F, :], cols[:, 1, :]))
            chain.wait()
            chain.done(nc.vector.tensor_copy(meta_c[:, NEW_F, :], cols[:, 3, :]))
            chain.done(nc.vector.tensor_scalar(meta_c[:, WAT_F, :], meta_c[:, WAT_F, :], WR - 1, None,
                                               ALU.bitwise_and))
            chain.wait()
            chain.done(nc.vector.tensor_scalar(meta_c[:, WAT_F, :], meta_c[:, WAT_F, :], WCOLS, None, ALU.mult))
            chain.wait()
            dve.sem_inc(meta_ready, 1)


def attend(nc, ctx, keep, onorm):
    qk_d, rows_d, slots_d, meta_d, acc_d = keep["dram"]
    ident, cb, v_sb, meta, idx8, zeros, banks, fill_done = keep["sbuf"]
    ident_b, mask_prev, mask_next = (cb[:, k * P:(k + 1) * P] for k in (0, 3, 4))

    def sb(name, shape, dt=F32):
        return ctx.enter_context(nc.sbuf_tensor(name, shape, dt))

    def sem(name):
        return ctx.enter_context(nc.semaphore(name))

    def sems(name, n):
        return [sem(f"{name}{i}") for i in range(n)]

    qT = sb("qT", [KM, HG, T], BF16)
    kT = sb("kT", [KM, HG, T], BF16)
    va = sb("va", [P, HG, TT, 32])
    nmax = sb("nmax", [P, HG, TT])
    nmax_b = sb("nmax_b", [P, HG, 2, TT], BF16)
    nmaxT = sb("nmaxT", [2 * TT, HG, P], BF16)
    pT = sb("pT", [P, 4, 3 * P])
    oT = sb("oT", [P, T])
    rec = sb("rec", [P, TT // 2, HG])
    row_ring = sb("row_ring", [P, 2, ROW])
    idx_ring = sb("idx_ring", [P, 2, K], I32)

    S1, S2, OB = 0, 2, 5
    misc = banks[7]
    misc_b = misc.bitcast(BF16)
    both_o = keep["psum"][:, OB:OB + 2, :]
    PAIRS = [(0, 7), (1, 2), (3, 4), (5, 6)]

    va_const, va_ready = sem("va_const"), sem("va_ready")
    qk_in, nrow_in = sems("qk_in", HG), sems("nrow_in", HG)
    s1_ready, s1_free = sem("s1_ready"), sem("s1_free")
    hi_done, nmax_ready, misc_ready, misc_free, rec_ready = (
        sem("hi_done"), sem("nmax_ready"), sem("misc_ready"), sem("misc_free"), sem("rec_ready"))
    s2_ready, p_ready, pv_done, o_read = sem("s2_ready"), sem("p_ready"), sem("pv_done"), sem("o_read")
    rows_in, scattered = sems("rows_in", 2), sems("scattered", 2)
    idx_ready, pool_tick = sem("idx_ready"), sem("pool_tick")

    def is_first(g):
        return isinstance(g, int) and g == 0

    def maxima_write(g, hh):
        return 1 + hh if is_first(g) else g * 6 - 1 + (0, 2, 4, 5)[hh]

    def outputs_write(g, half):
        return g * 6 - 1 + (1, 3)[half]

    def window(i):
        return max(i - 1, 0), min(i + 2, TT)

    with nc.Block() as block:
        @block.sync
        def _(sp):
            def load(u, hh):
                rows = bass.ds(u * DK, DK)
                for lo, n, s in ((0, 3, 0), (3, 2, 1), (5, 1, 2)):
                    sp.dma_start(qT[lo * DK:(lo + n) * DK, hh, :],
                                 qk_d[0, s:s + 1, rows, :].to_broadcast([n, DK, T])).then_inc(qk_in[hh], 16)
                for lo, n in ((0, 3), (3, 2), (5, 1)):
                    sp.dma_start(kT[lo * DK:(lo + n) * DK, hh, :], qk_d[1, 0:n, rows, :]).then_inc(qk_in[hh], 16)

            def maxima(hh, write):
                sp.wait_ge(misc_free, write + 1)
                for s in range(2):
                    dst = qT[KS + s:KS + s + 1, hh, :].rearrange("o (t q) -> o t q", t=TT)
                    sp.dma_start(dst, nmaxT[s * TT:(s + 1) * TT, hh, :]).then_inc(nrow_in[hh], 16)

            def group(g, last):
                for hh in range(HG):
                    if not (last and hh == HG - 1):
                        maxima((hh + 1) % HG, maxima_write(g, hh))
                    if not (last and hh > 0):
                        if not is_first(g) or hh > 0:
                            sp.wait_ge(pv_done, g * (HG * TT) + hh * TT)
                        load(g * HG + hh + 3, (hh + 3) % HG)

            for hh in range(3):
                load(hh, hh)
            maxima(0, 0)
            group(0, False)
            with sp.Fori(1, NG - 1) as g:
                group(g, False)
            group(NG - 1, True)

        @block.tensor
        def _(pe):
            pe.wait_ge(va_const, 3)

            def masks(bank, i, n):
                if i > 0:
                    last = nc.tensor.matmul(banks[bank][:, 0:P], ident_b, mask_prev, start=False,
                                            stop=(i == TT - 1), skip_group_check=True)
                if i < TT - 1:
                    last = nc.tensor.matmul(banks[bank][:, n - P:n], ident_b, mask_next, start=False, stop=True,
                                            skip_group_check=True)
                return last

            def scores_q(g, ahead, k):
                hh = ahead % HG
                pe.wait_ge(s1_free, g * (HG * 4) + (ahead * 4 + k + 1))
                for bank, i in enumerate(PAIRS[k]):
                    lo, hi = window(i)
                    nc.tensor.matmul(banks[S1 + bank][:, 0:(hi - lo) * P], qT[0:KS, hh, i * P:(i + 1) * P],
                                     kT[0:KS, hh, lo * P:hi * P], start=True, stop=False, skip_group_check=True)
                    last = masks(S1 + bank, i, (hi - lo) * P)
                last.then_inc(s1_ready, 1)

            def scores_k(g, hh, j):
                lo, hi = window(j)
                back = {0: 1, 1: 1, 2: 4}.get(j, 2)
                if not is_first(g) or hh > 0 or j > 2:
                    pe.wait_ge(p_ready, g * (HG * TT) + (hh * TT + j - back))
                nc.tensor.matmul(banks[S2 + j % 3][:, 0:(hi - lo) * P], kT[0:KM, hh, j * P:(j + 1) * P],
                                 qT[0:KM, hh, lo * P:hi * P], start=True, stop=False, skip_group_check=True)
                masks(S2 + j % 3, j, (hi - lo) * P).then_inc(s2_ready, 1)

            def values(g, hh, j):
                lo, hi = window(j)
                pe.wait_ge(p_ready, g * (HG * TT) + (hh * TT + j + 1))
                for bank in range(2):
                    a, b = max(lo, 4 * bank), min(hi, 4 * bank + 4)
                    if a < b:
                        last = nc.tensor.matmul(
                            banks[OB + bank][32 * hh:32 * hh + 32, (a - 4 * bank) * P:(b - 4 * bank) * P],
                            va[:, hh, j, :], pT[:, j % 4, (a - lo) * P:(b - lo) * P],
                            start=(j == (0, 3)[bank]), stop=(j == (4, 7)[bank]), skip_group_check=True)
                last.then_inc(pv_done, 1)

            def turn_maxima(g, ahead, write):
                pe.wait_ge(nmax_ready, g * HG + (ahead + 1))
                if not (isinstance(write, int) and write == 0):
                    pe.wait_ge(misc_free, write)
                nc.tensor.transpose(misc_b[0:2 * TT, 0:P],
                                    nmax_b[:, ahead % HG, :, :].rearrange("p s t -> p (s t)"),
                                    ident_b).then_inc(misc_ready, 1)

            def turn_outputs(g, half):
                pe.wait_ge(o_read, g)
                pe.wait_ge(misc_free, outputs_write(g, half))
                for t in range(4):
                    last = nc.tensor.transpose(misc[:, t * P:(t + 1) * P],
                                               oT[:, (4 * half + t) * P:(4 * half + t + 1) * P], ident[:, :])
                last.then_inc(misc_ready, 1)

            def group(g, last):
                for hh in range(HG):
                    if not (last and hh == HG - 1):
                        turn_maxima(g, hh + 1, maxima_write(g, hh))
                    pe.wait_ge(va_ready, g * HG + (hh + 1))
                    pe.wait_ge(nrow_in[hh], g * 32 + 32)
                    for j in range(TT):
                        scores_k(g, hh, j)
                        if j % 2 == 1 and not (last and hh > 1):
                            if j == 1:
                                pe.wait_ge(qk_in[(hh + 2) % HG], g * 96 + (96 if hh < 2 else 192))
                            scores_q(g, hh + 2, j // 2)
                        if j == 4 and hh < 2 and not is_first(g):
                            turn_outputs(g, hh)
                        if j == 1 and hh == 0 and not is_first(g):
                            pe.wait_ge(o_read, g)
                        if j > 0:
                            values(g, hh, j - 1)
                    values(g, hh, TT - 1)

            for hh in range(2):
                pe.wait_ge(qk_in[hh], 96)
                for k in range(4):
                    scores_q(0, hh, k)
            turn_maxima(0, 0, 0)
            group(0, False)
            with pe.Fori(1, NG - 1) as g:
                group(g, False)
            group(NG - 1, True)
            for half in range(2):
                pe.wait_ge(o_read, NG)
                pe.wait_ge(misc_free, NG * 6 - 2 + half)
                for t in range(4):
                    last = nc.tensor.transpose(misc[:, t * P:(t + 1) * P],
                                               oT[:, (4 * half + t) * P:(4 * half + t + 1) * P], ident[:, :])
                last.then_inc(misc_ready, 1)

        @block.scalar
        def _(act):
            def group(g, last):
                for hh in range(HG):
                    for j in range(TT):
                        lo, hi = window(j)
                        n = hh * TT + j
                        if not is_first(g) or n > 3:
                            act.wait_ge(pv_done, g * (HG * TT) + (n - 3))
                        act.wait_ge(s2_ready, g * (HG * TT) + (n + 1))
                        nc.scalar.activation(pT[:, j % 4, 0:(hi - lo) * P], banks[S2 + j % 3][:, 0:(hi - lo) * P],
                                             ACT.Exp).then_inc(p_ready, 1)
                act.wait_ge(pv_done, g * (HG * TT) + HG * TT)
                nc.scalar.copy(oT.rearrange("p (b q) -> p b q", b=2), both_o).then_inc(o_read, 1)

            group(0, False)
            with act.Fori(1, NG - 1) as g:
                group(g, False)
            group(NG - 1, True)

        @block.vector
        def _(dve):
            nc.vector.memset(va[:, :, :, DK + 1:32], 0.0).then_inc(va_const, 1)
            nc.vector.memset(va[:, :, :, DK:DK + 1], 1.0).then_inc(va_const, 1)
            nc.vector.memset(kT[KS:KM, :, :], 1.0).then_inc(va_const, 1)
            dve.sem_inc(s1_free, 1)

            def maxima(g, ahead, k):
                hh = ahead % HG
                dve.wait_ge(s1_ready, g * (HG * 4) + (ahead * 4 + k + 1))
                i0, i1 = PAIRS[k]
                nc.vector.tensor_reduce(nmax[:, hh, i0:i1 + 1:i1 - i0],
                                        keep["psum"][:, S1:S1 + 2, 0:(2 if k == 0 else 3) * P],
                                        AX.X, ALU.max, negate=True).then_inc(s1_free, 1)

            def split_maxima(g, ahead):
                hh = ahead % HG
                dve.wait_ge(s1_free, g * (HG * 4) + (ahead * 4 + 5))
                nc.vector.tensor_copy(nmax_b[:, hh, 0, :], nmax[:, hh, :]).then_inc(hi_done, 1)
                dve.wait_ge(hi_done, g * HG + (ahead + 1))
                nc.vector.tensor_tensor(nmax_b[:, hh, 1, :], nmax[:, hh, :], nmax_b[:, hh, 0, :],
                                        ALU.subtract).then_inc(nmax_ready, 1)

            def copy_maxima(hh, write):
                dve.wait_ge(misc_ready, write + 1)
                nc.vector.tensor_copy(nmaxT[:, hh, :], misc_b[0:2 * TT, 0:P]).then_inc(misc_free, 1)

            def copy_values(g, ahead):
                nc.vector.tensor_copy(va[:, ahead % HG, :, 0:DK],
                                      v_sb[:, bass.ds(g * HG + ahead, 1), :, :].rearrange("p o t d -> p (o t) d")
                                      ).then_inc(va_ready, 1)

            def normalise(g, half, write, done):
                dve.wait_ge(misc_ready, write + 1)
                o = misc.rearrange("p (t h c) -> p t h c", t=TT // 2, h=HG)
                nc.vector.reciprocal(rec[:, :, :], o[:, :, :, DK]).then_inc(rec_ready, 1)
                dve.wait_ge(rec_ready, done)
                dst = onorm[:, bass.ds(g * TT + half * (TT // 2), TT // 2), :]
                nc.vector.tensor_tensor(dst.rearrange("p t (h d) -> p t h d", h=HG), o[:, :, :, 0:DK],
                                        rec[:, :, :].unsqueeze(3).to_broadcast([P, TT // 2, HG, DK]),
                                        ALU.mult).then_inc(misc_free, 1)

            def group(g, last):
                for hh in range(HG):
                    if not (last and hh == HG - 1):
                        copy_maxima((hh + 1) % HG, maxima_write(g, hh))
                        if not is_first(g) or hh == 3:
                            dve.wait_ge(pv_done, g * (HG * TT) + (hh - 2) * TT)
                        copy_values(g, hh + 1)
                    for k in range(4):
                        if not (last and hh > 1):
                            maxima(g, hh + 2, k)
                        if k == 1 and hh < 2 and not is_first(g):
                            normalise(g - 1, hh, outputs_write(g, hh), g * 2 - 1 + hh)
                    if not (last and hh > 1):
                        split_maxima(g, hh + 2)

            copy_values(0, 0)
            for hh in range(2):
                for k in range(4):
                    maxima(0, hh, k)
                split_maxima(0, hh)
            copy_maxima(0, 0)
            group(0, False)
            with dve.Fori(1, NG - 1) as g:
                group(g, False)
            group(NG - 1, True)
            for half in range(2):
                normalise(NG - 1, half, NG * 6 - 2 + half, NG * 2 - 1 + half)

        @block.gpsimd
        def _(pool):
            def load(n, j):
                pool.dma_start(row_ring[:, j, :], rows_d[bass.ds(n * P, P), :]).then_inc(rows_in[j], 16)

            def step(i, j, last):
                n = i * 2 + j
                pool.wait_ge(rows_in[j], i * 16 + 16)
                pool.sem_inc(pool_tick, 1)
                nc.gpsimd.tensor_copy(idx_ring[:, j, :].unsqueeze(1), idx8[:, bass.ds(n, 1), :]
                                      ).then_inc(idx_ready, 1)
                pool.wait_ge(idx_ready, n + 1)
                pool.sem_inc(pool_tick, 1)
                for k in range(K):
                    nc.gpsimd.indirect_dma_start(
                        out=slots_d, out_offset=bass.IndirectOffsetOnAxis(ap=idx_ring[:, j, k:k + 1], axis=0),
                        in_=row_ring[:, j, :], in_offset=None).then_inc(scattered[j], 16)
                if not last:
                    if j == 1:
                        pool.wait_ge(scattered[0], i * (16 * K) + 16 * K)
                    elif not is_first(i):
                        pool.wait_ge(scattered[1], i * (16 * K))
                    if j == 1 or not is_first(i):
                        pool.sem_inc(pool_tick, 1)
                    load(n + 1, 1 - j)

            pool.wait_ge(fill_done, 16 * (8 + 2 * NACC))
            load(0, 0)
            step(0, 0, False)
            step(0, 1, False)
            with pool.Fori(1, NTILE // 2 - 1) as i:
                step(i, 0, False)
                step(i, 1, False)
            step(NTILE // 2 - 1, 0, False)
            step(NTILE // 2 - 1, 1, True)
            for j in range(2):
                pool.wait_ge(scattered[j], 16 * K * (NTILE // 2))


def merge(nc, ctx, keep, onorm, x, w_proj, res):
    ident, banks = keep["sbuf"][0], keep["sbuf"][6]

    def sb(name, shape, dt=F32):
        return ctx.enter_context(nc.sbuf_tensor(name, shape, dt))

    def sem(name):
        return ctx.enter_context(nc.semaphore(name))

    wp = sb("wp", [P, 2, D])
    stage = sb("stage", [P, 2, D])
    oT2 = sb("oT2", [P, 2, 2, P])
    m_in, stage_ready, turned, turned_read, proj_ready, proj_read = (
        sem("m_in"), sem("stage_ready"), sem("turned"), sem("turned_read"), sem("proj_ready"), sem("proj_read"))

    tick = sem("merge_tick")

    with nc.Block() as block:
        @block.sync
        def _(sp):
            sp.dma_start(wp[:, :, :], w_proj).then_inc(m_in, 16)
            sp.dma_start(res[:, :, :], x.rearrange("n p c -> p n c")).then_inc(m_in, 16)

        @block.gpsimd
        def _(pool):
            pool.sem_inc(turned, 2)
            with pool.Fori(0, B) as b:
                for t in range(TT):
                    pool.wait_ge(turned, b * TT + t + 1)
                    pool.sem_inc(tick, 1)
                    src = onorm[:, bass.ds(b * (4 * TT), 4 * TT), :].rearrange("p (g t) c -> p g t c", g=4)[:, :, t, :]
                    nc.gpsimd.tensor_copy(stage[:, t % 2, :].rearrange("p (g c) -> p g c", g=4), src
                                          ).then_inc(stage_ready, 1)

        @block.tensor
        def _(pe):
            pe.wait_ge(m_in, 32)
            with pe.Fori(0, B) as b:
                for t in range(TT):
                    n = b * TT + t
                    pe.wait_ge(stage_ready, n + 1)
                    for h in range(2):
                        last = nc.tensor.transpose(banks[t % 2][:, h * P:(h + 1) * P],
                                                   stage[:, t % 2, h * P:(h + 1) * P], ident[:, :])
                    last.then_inc(turned, 1)
                    pe.wait_ge(turned_read, n + 1)
                    pe.wait_ge(proj_read, n + 1)
                    for h in range(2):
                        last = nc.tensor.matmul(banks[2 + t % 2][:, 0:D], oT2[:, t % 2, h, :], wp[:, h, :],
                                                start=(h == 0), stop=(h == 1))
                    last.then_inc(proj_ready, 1)

        @block.scalar
        def _(act):
            with act.Fori(0, B) as b:
                for t in range(TT):
                    act.wait_ge(turned, b * TT + t + 3)
                    nc.scalar.copy(oT2[:, t % 2, :, :].rearrange("p h q -> p (h q)"), banks[t % 2][:, 0:D]
                                   ).then_inc(turned_read, 1)

        @block.vector
        def _(dve):
            dve.sem_inc(proj_read, 2)
            dve.wait_ge(m_in, 32)
            with dve.Fori(0, B) as b:
                for t in range(TT):
                    dve.wait_ge(proj_ready, b * TT + t + 1)
                    r = res[:, bass.ds(b * TT + t, 1), :].rearrange("p o c -> p (o c)")
                    nc.vector.tensor_tensor(r, banks[2 + t % 2][:, 0:D], r, ALU.add).then_inc(proj_read, 1)


def experts(nc, ctx, keep, w_exp):
    qk_d, rows_d, slots_d, meta_d, acc_d = keep["dram"]
    ident, cb, v_sb, meta, idx8, zeros, banks, fill_done = keep["sbuf"]

    def sb(name, shape, dt=F32):
        return ctx.enter_context(nc.sbuf_tensor(name, shape, dt))

    def sem(name):
        return ctx.enter_context(nc.semaphore(name))

    def sems(name, n):
        return [sem(f"{name}{i}") for i in range(n)]

    xb = sb("xb", [P, XR, ROW])
    wb = sb("wb", [P, WR * WCOLS])
    xT = sb("xTe", [P, 2, 2, P])
    gate = sb("gate", [P, 2, I])
    a_sb = sb("a_sb", [P, 2, I])
    aT = sb("aT", [P, 2, P])
    ys = sb("ys", [P, NACC, D])

    x_in, w_in, added = sems("xb_in", XR), sems("wb_in", WR), sems("added", NACC)
    px_ready, xT_ready, gu_ready, gate_ready, act_ready = (
        sem("px_ready"), sem("xTe_ready"), sem("gu_ready"), sem("gate_ready"), sem("act_ready"))
    pa_ready, aT_ready, y_ready, ys_ready = sem("pa_ready"), sem("aT_ready"), sem("y_ready"), sem("ys_ready")
    acc_free, tick = sem("acc_free"), sem("tick")
    PX, GU, PA, Y = 0, 2, 4, 6
    LAST = NB // XR - 1
    assert NB % XR == 0 and LAST > 1

    def first(i):
        return isinstance(i, int) and i == 0

    def exists(i, r):
        return not (isinstance(i, int) and i == LAST) or r < XR

    def every(engine, step):
        step(0)
        with engine.Fori(1, LAST) as i:
            step(i)
        step(LAST)

    number = count()

    def fields(engine, n, i, r, f, most):
        regs = [engine.alloc_register(f"field{f}_{next(number)}") for k in range(n)]
        engine.load(regs, meta[0:1, f, bass.ds(i * XR + r, n)])
        return [bass.RuntimeValue.of_register_unchecked(reg, min_val=0, max_val=most) for reg in regs]

    with nc.Block() as block:
        @block.sync
        def _(sp):
            def half(i, h):
                e = fields(sp, 8, i, 8 * h, E_F, NE)
                new = fields(sp, 8, i, 8 * h, NEW_F, 1)
                at = fields(sp, 8, i, 8 * h, WAT_F, (WR - 1) * WCOLS)
                for k in range(8):
                    r = 8 * h + k
                    if not first(i):
                        sp.wait_ge(acc_free, i * XR + (r - XR + NACC + 1))
                    sp.dma_start(xb[:, r, :], slots_d[bass.ds(i * (XR * P) + r * P, P), :]).then_inc(x_in[r], 16)
                    if not first(i) or r >= WR:
                        sp.wait_ge(y_ready, i * XR + (r - WR + 1))
                    sp.dma_start(wb[:, bass.ds(at[k], WCOLS)],
                                 w_exp[bass.ds(e[k], 1), :, :].rearrange("e p n -> p (e n)"),
                                 cond=new[k]).then_inc(w_in[r % WR], 16)

            def step(i):
                for h in range(XR // 8):
                    half(i, h)

            every(sp, step)

        @block.tensor
        def _(pe):
            def turn_x(i, r):
                pe.wait_ge(x_in[r % XR], i * 16 + 16 * (r // XR + 1))
                if not first(i) or r > 1:
                    pe.wait_ge(xT_ready, i * XR + (r - 1))
                for h in range(2):
                    last = nc.tensor.transpose(banks[PX + r % 2][:, h * P:(h + 1) * P],
                                               xb[:, r % XR, h * P:(h + 1) * P], ident[:, :])
                last.then_inc(px_ready, 1)

            def gate_up(i, r, at):
                pe.wait_ge(w_in[r % WR], i * (16 * XR // WR) + 16 * (r // WR + 1))
                pe.wait_ge(xT_ready, i * XR + r + 1)
                for h in range(2):
                    last = nc.tensor.matmul(banks[GU + r % 2][:, 0:2 * I], xT[:, r % 2, h, :],
                                            wb[:, bass.ds(at + h * 2 * I, 2 * I)],
                                            start=(h == 0), stop=(h == 1))
                last.then_inc(gu_ready, 1)

            def turn_a(i, r):
                pe.wait_ge(act_ready, i * XR + r + 1)
                nc.tensor.transpose(banks[PA + r % 2][:, 0:P], a_sb[:, r % 2, :], ident[:, :]).then_inc(pa_ready, 1)

            def down(i, r, at):
                if not first(i) or r > 1:
                    pe.wait_ge(ys_ready, i * XR + (r - 1))
                pe.wait_ge(aT_ready, i * XR + r + 1)
                nc.tensor.matmul(banks[Y + r % 2][:, 0:D], aT[:, r % 2, :], wb[:, bass.ds(at + 4 * I, D)],
                                 start=True, stop=True).then_inc(y_ready, 1)

            def step(i):
                for r in range(XR):
                    k = r % 8
                    if k == 0:
                        at = fields(pe, 10 if exists(i, r + 9) else 8, i, r, WAT_F, (WR - 1) * WCOLS)
                    if exists(i, r + 3):
                        turn_x(i, r + 3)
                    if exists(i, r + 2):
                        gate_up(i, r + 2, at[k + 2])
                    if exists(i, r + 1):
                        turn_a(i, r + 1)
                    down(i, r, at[k])

            at = fields(pe, 2, 0, 0, WAT_F, (WR - 1) * WCOLS)
            turn_x(0, 0)
            turn_x(0, 1)
            gate_up(0, 0, at[0])
            turn_x(0, 2)
            gate_up(0, 1, at[1])
            turn_a(0, 0)
            every(pe, step)

        @block.scalar
        def _(act):
            def copy_x(i, r):
                if not first(i) or r > 1:
                    act.wait_ge(gu_ready, i * XR + (r - 1))
                act.wait_ge(px_ready, i * XR + r + 1)
                nc.scalar.copy(xT[:, r % 2, :, :].rearrange("p h q -> p (h q)"), banks[PX + r % 2][:, 0:D]
                               ).then_inc(xT_ready, 1)

            def silu(i, r):
                if not first(i) or r > 1:
                    act.wait_ge(act_ready, i * XR + (r - 1))
                act.wait_ge(gu_ready, i * XR + r + 1)
                nc.scalar.activation(gate[:, r % 2, :], banks[GU + r % 2][:, 0:I], ACT.Silu).then_inc(gate_ready, 1)

            def step(i):
                for r in range(XR):
                    if exists(i, r + 3):
                        copy_x(i, r + 3)
                    if exists(i, r + 2):
                        silu(i, r + 2)

            copy_x(0, 0)
            copy_x(0, 1)
            silu(0, 0)
            copy_x(0, 2)
            silu(0, 1)
            every(act, step)

        @block.vector
        def _(dve):
            def product(i, r, e):
                dve.wait_ge(gate_ready, i * XR + r + 1)
                if not first(i) or r > 1:
                    dve.wait_ge(pa_ready, i * XR + (r - 1))
                nc.vector.scalar_tensor_tensor(a_sb[:, r % 2, :], gate[:, r % 2, :],
                                               xb[:, r % XR, bass.ds(e + W_COL, 1)],
                                               banks[GU + r % 2][:, I:2 * I], ALU.mult, ALU.mult
                                               ).then_inc(act_ready, 1)

            def copy_a(i, r):
                if not first(i) or r > 1:
                    dve.wait_ge(y_ready, i * XR + (r - 1))
                dve.wait_ge(pa_ready, i * XR + r + 1)
                nc.vector.tensor_copy(aT[:, r % 2, :], banks[PA + r % 2][:, 0:P]).then_inc(aT_ready, 1)

            def step(i):
                for r in range(XR):
                    k = r % 8
                    if k == 0:
                        e = fields(dve, 10 if exists(i, r + 9) else 8, i, r, E_F, NE)
                    if exists(i, r + 1):
                        copy_a(i, r + 1)
                    if exists(i, r + 2):
                        product(i, r + 2, e[k + 2])
                    dve.wait_ge(acc_free, i * XR + r + 1)
                    dve.wait_ge(y_ready, i * XR + r + 1)
                    nc.vector.tensor_copy(ys[:, r % NACC, :], banks[Y + r % 2][:, 0:D]).then_inc(ys_ready, 1)

            e = fields(dve, 2, 0, 0, E_F, NE)
            product(0, 0, e[0])
            product(0, 1, e[1])
            copy_a(0, 0)
            every(dve, step)

        @block.gpsimd
        def _(pool):
            def step(i):
                for r in range(XR):
                    if not first(i) or r >= NACC:
                        pool.wait_ge(added[r % NACC], i * (16 * XR // NACC) + 16 * (r // NACC))
                    pool.sem_inc(acc_free, 1)
                    pool.wait_ge(ys_ready, i * XR + r + 1)
                    pool.sem_inc(tick, 1)
                    nc.gpsimd.indirect_dma_start(
                        out=acc_d[r % NACC],
                        out_offset=bass.IndirectOffsetOnAxis(ap=xb[:, r, ID_COL:ROW].bitcast(I32), axis=0),
                        in_=ys[:, r % NACC, :], in_offset=None, compute_op=ALU.add).then_inc(added[r % NACC], 16)

            every(pool, step)
            for r in range(NACC):
                pool.wait_ge(added[r], 16 * (NB // NACC))


def total(nc, ctx, keep, res, out):
    acc_d = keep["dram"][4]

    def sem(name):
        return ctx.enter_context(nc.semaphore(name))

    parts = ctx.enter_context(nc.sbuf_tensor("acc_parts", [P, 2, NACC, TPC, D], F32))
    parts_in = [sem("acc_in0"), sem("acc_in1")]
    half_ready, sum_chain, sum_ready, stored = sem("half_ready"), sem("sum_chain"), sem("sum_ready"), sem("stored")

    with nc.Block() as block:
        @block.sync
        def _(sp):
            def load(c, j):
                for k in range(NACC):
                    sp.dma_start(parts[:, j, k, :, :],
                                 acc_d[k][bass.ds(c * CH, CH), :].rearrange("(n p) c -> p n c", p=P)
                                 ).then_inc(parts_in[j], 16)

            load(0, 0)
            load(1, 1)
            with sp.Fori(0, NCH // 2 - 1) as i:
                for j in range(2):
                    sp.wait_ge(sum_ready, i * 2 + j + 1)
                    load(i * 2 + j + 2, j)

        @block.gpsimd
        def _(pool):
            with pool.Fori(0, NCH // 2) as i:
                for j in range(2):
                    pool.wait_ge(parts_in[j], i * (16 * NACC) + 16 * NACC)
                    nc.gpsimd.tensor_tensor(parts[:, j, 2, :, :], parts[:, j, 2, :, :], parts[:, j, 3, :, :],
                                            ALU.add).then_inc(half_ready, 1)

        @block.vector
        def _(dve):
            with dve.Fori(0, NCH // 2) as i:
                for j in range(2):
                    c = i * 2 + j
                    r = res[:, bass.ds(c * TPC, TPC), :]
                    dve.wait_ge(parts_in[j], i * (16 * NACC) + 16 * NACC)
                    nc.vector.tensor_tensor(parts[:, j, 0, :, :], parts[:, j, 0, :, :], parts[:, j, 1, :, :],
                                            ALU.add).then_inc(sum_chain, 1)
                    dve.wait_ge(sum_chain, c * 2 + 1)
                    dve.wait_ge(half_ready, c + 1)
                    nc.vector.tensor_tensor(parts[:, j, 0, :, :], parts[:, j, 0, :, :], parts[:, j, 2, :, :],
                                            ALU.add).then_inc(sum_chain, 1)
                    dve.wait_ge(sum_chain, c * 2 + 2)
                    nc.vector.tensor_tensor(r, r, parts[:, j, 0, :, :], ALU.add).then_inc(sum_ready, 1)

        @block.scalar
        def _(act):
            with act.Fori(0, NCH) as c:
                act.wait_ge(sum_ready, c + 1)
                act.dma_start(out[bass.ds(c * TPC, TPC), :, :].rearrange("n p c -> p n c"),
                              res[:, bass.ds(c * TPC, TPC), :]).then_inc(stored, 16)
            act.wait_ge(stored, 16 * NCH)


def build(nc, x, w_qk, w_vr, w_proj, w_exp, c_f32, c_ids, out):
    with ExitStack() as ctx:
        def sb(name, shape, dt=F32):
            return ctx.enter_context(nc.sbuf_tensor(name, shape, dt))

        def dram(name, shape, dt=F32):
            return nc.dram_tensor(name, shape, dt, kind="Internal").ap()

        psum = ctx.enter_context(nc.psum_tensor("psum", [P, 8, 512], F32))
        keep = {
            "dram": (dram("qk_parts", (2, NSPLIT, B * D, T), BF16), dram("token_rows", (NTOK, ROW)),
                     dram("slot_rows", (NB * P, ROW)), dram("block_table", (NFIELD, MB * P), I32),
                     [dram(f"acc{i}", (NTOK + P, D)) for i in range(NACC)]),
            "psum": psum,
            "sbuf": (sb("ident", [P, P]), sb("consts_bf16", [P, 5 * P], BF16), sb("v_sb", [P, NU, TT, DK]),
                     sb("block_table_row", [1, NFIELD, MB * P], I32), sb("slots_of_tokens", [P, NTILE, K], I32),
                     sb("zeros", [P, 1024]), [psum[:, i, :] for i in range(8)],
                     ctx.enter_context(nc.semaphore("fill_done"))),
        }
        with ExitStack() as inner:
            project_and_route(nc, inner, x, w_qk, w_vr, c_f32, c_ids, keep)
        res = sb("res", [P, NTILE, D])
        with ExitStack() as inner:
            onorm = inner.enter_context(nc.sbuf_tensor("onorm", [P, NG * TT, HG * DK], F32))
            with ExitStack() as deeper:
                attend(nc, deeper, keep, onorm)
            with ExitStack() as deeper:
                merge(nc, deeper, keep, onorm, x, w_proj, res)
        with ExitStack() as inner:
            experts(nc, inner, keep, w_exp)
        with ExitStack() as inner:
            total(nc, inner, keep, res, out)


def constants():
    r, c = np.arange(P)[:, None], np.arange(P)[None, :]
    f = np.zeros((P, 6 * P + 2 * MB), np.float32)
    f[:, 0:P] = r == c
    f[:, P:2 * P] = r == c
    f[:, 2 * P:3 * P] = r < c
    f[:, 3 * P:4 * P] = 1.0
    f[:, 4 * P:5 * P] = np.where(r > c, NEG, 0.0)
    f[:, 5 * P:6 * P] = np.where(c > r, NEG, 0.0)
    f[:, 6 * P:6 * P + MB] = r + P * np.arange(MB)[None, :]
    f[:, 6 * P + MB:] = f[:, 6 * P:6 * P + MB] - 1
    ids = np.zeros((P, NTILE + 1), np.int32)
    ids[:, :] = r + P * np.arange(NTILE + 1)[None, :]
    return f, ids


def kernel(L0_attn_x, L0_attn_w_qkv, L0_attn_w_proj, L0_ffn_router_w, L0_ffn_shared_gate_w,
           L0_ffn_shared_up_w, L0_ffn_shared_down_w, L0_ffn_expert_gate_k, L0_ffn_expert_up_k,
           L0_ffn_expert_down_k):
    import concourse.bacc as bacc
    from concourse.bass_utils import run_bass_kernel_spmd

    def halves(w):
        return np.ascontiguousarray(w.reshape(2, P, -1).transpose(1, 0, 2))

    w_qkv = np.asarray(L0_attn_w_qkv)
    gates = np.concatenate([np.asarray(L0_ffn_expert_gate_k), np.asarray(L0_ffn_shared_gate_w)[None]])
    ups = np.concatenate([np.asarray(L0_ffn_expert_up_k), np.asarray(L0_ffn_shared_up_w)[None]])
    downs = np.concatenate([np.asarray(L0_ffn_expert_down_k), np.asarray(L0_ffn_shared_down_w)[None]])
    gu = np.concatenate([gates, ups], axis=2).reshape(NE + 1, 2, P, 2 * I).transpose(0, 2, 1, 3)
    c_f32, c_ids = constants()
    arrays = {
        "x": np.ascontiguousarray(np.asarray(L0_attn_x).reshape(NTILE, P, D)),
        "w_qk": halves(w_qkv[0:2 * D].T),
        "w_vr": halves(np.concatenate([w_qkv[2 * D:3 * D].T, np.asarray(L0_ffn_router_w)], axis=1)),
        "w_proj": halves(np.asarray(L0_attn_w_proj).T),
        "w_exp": np.ascontiguousarray(np.concatenate([gu.reshape(NE + 1, P, 4 * I), downs], axis=2)),
        "c_f32": c_f32,
        "c_ids": c_ids,
    }
    nc = bacc.Bacc("TRN2", target_bir_lowering=False, num_devices=1)
    ins = [nc.dram_tensor("in_" + k, a.shape, mybir.dt.from_np(a.dtype), kind="ExternalInput").ap()
           for k, a in arrays.items()]
    out = nc.dram_tensor("out", (NTILE, P, D), F32, kind="ExternalOutput").ap()
    build(nc, *ins, out)
    r = run_bass_kernel_spmd(nc, [{"in_" + k: a for k, a in arrays.items()}], core_ids=[0])
    return r.results[0]["out"].reshape(B, T, D)
```

```python
from contextlib import ExitStack
from itertools import count

import numpy as np
import concourse.bass as bass
from concourse import mybir

F32 = mybir.dt.float32
BF16 = mybir.dt.bfloat16
I32 = mybir.dt.int32
ALU = mybir.AluOpType
ACT = mybir.ActivationFunctionType
AX = mybir.AxisListType

P = 128
B, T, D = 4, 1024, 256
NTOK = B * T
NTILE = NTOK // P
NH, DK = 16, 16
TT = T // P
NE, K, I = 64, 8, 128
EPS = 1e-5
NEG = -1.0e30

CH = 512
NCH = NTOK // CH
TPC = CH // P

NSPLIT = 3
SLOTS = ((0, 3, 0), (3, 2, 1), (5, 1, 2)), ((0, 3, 0), (3, 2, 0), (5, 1, 0))
KS = 6 * DK
KM = KS + 2
NU = B * NH
HG = 4
NG = NU // HG

NB_ROUTED = (NTOK * K) // P + NE
EMPTY = NB_ROUTED
W_COL, ID_COL = D, D + NE
ROW = D + NE + 1
WCOLS = 2 * 2 * I + D
NACC = 4
XR = 16
WR = 8
MB = 3
E_F, AT_F, LOAD_F, SRC_F = range(4)
NFIELD = 4
NEW_BIT, PLACE_BIT = 7, 8


class Chain:

    def __init__(self, engine, semaphore, base=0):
        self.engine, self.semaphore, self.base, self.n = engine, semaphore, base, 0

    def done(self, instruction):
        instruction.then_inc(self.semaphore, 1)
        self.n += 1

    def wait(self):
        self.engine.wait_ge(self.semaphore, self.base + self.n)


def project_and_route(nc, ctx, x, w_qk, w_vr, c_f32, c_ids, keep):
    qk_d, rows_d, slots_d, meta_d, acc_d = keep["dram"]
    ident, cb, v_sb, meta, idx8, zeros, banks, fill_done = keep["sbuf"]
    ident_b, before, ones_b = (cb[:, k * P:(k + 1) * P] for k in range(3))

    def sb(name, shape, dt=F32):
        return ctx.enter_context(nc.sbuf_tensor(name, shape, dt))

    def sem(name):
        return ctx.enter_context(nc.semaphore(name))

    consts = sb("consts_f32", [P, 6 * P + 2 * MB])
    wqk = sb("wqk", [P, 2, 2 * D])
    wvr = sb("wvr", [P, 2, D + NE])
    xin = sb("xin", [P, 2, TPC, D])
    xn = sb("xn", [P, 2, TPC, D])
    xT = sb("xT", [P, 2, 2, CH])
    stats = sb("stats", [P, TPC, 6])
    small = sb("small", [P, 10, TPC])
    parts = sb("parts", [P, 2, 4, NSPLIT, CH], BF16)
    rest = sb("rest", [P, 2, CH])
    rows = sb("rows", [P, NTILE, ROW])
    ids = sb("ids", [P, NTILE + 1], I32)
    template = sb("template", [P, ROW])
    logits = sb("logits", [P, NTILE, NE])
    aff = sb("aff", [P, NTILE, NE])
    work = sb("work", [P, NTILE, NE])
    chosen = sb("chosen", [P, NTILE, NE], BF16)
    base = sb("base", [P, NTILE + 1, NE])
    top8 = sb("top8", [P, NTILE, K])
    rsum = sb("rsum", [P, NTILE])
    blk = sb("blk", [P, 8, NE])
    blk_i = sb("blk_i", [P, NE], I32)
    blk_table = sb("blk_table", [P, 2, NE], I32)
    junk = sb("junk", [P, NE])
    cols = sb("cols", [P, 7, MB])
    meta_c = sb("meta_c", [P, NFIELD, MB], I32)

    consts_in, weights_in = sem("consts_in"), sem("weights_in")
    x_in = [sem("x_in0"), sem("x_in1")]
    consts_ready = sem("consts_ready")
    dve_a = sem("dve_a")
    tick = sem("project_tick")
    var_ready, std_ready, xn_ready = sem("var_ready"), sem("std_ready"), sem("xn_ready")
    xn_free_pool, xn_free_pe = sem("xn_free_pool"), sem("xn_free_pe")
    xTp_ready = sem("xTp_ready")
    xT0_ready, xT1_ready = sem("xT0_ready"), sem("xT1_ready")
    qk_ready, hi_ready, rest_ready, mid_ready, lo_ready = (
        sem("qk_ready"), sem("hi_ready"), sem("rest_ready"), sem("mid_ready"), sem("lo_ready"))
    parts_out = [sem("parts_out0"), sem("parts_out1")]
    parts_free = sem("parts_free")
    vr_ready, vr_free = sem("vr_ready"), sem("vr_free")
    XT0 = 8

    with nc.Block() as block:
        @block.sync
        def _(sp):
            sp.dma_start(consts[:, :], c_f32).then_inc(consts_in, 16)
            sp.dma_start(ids[:, :], c_ids).then_inc(consts_in, 16)

            def load(c, j):
                sp.dma_start(xin[:, j, :, :], x[bass.ds(c * TPC, TPC), :, :].rearrange("n p c -> p n c")
                             ).then_inc(x_in[j], 16)

            load(0, 0)
            load(1, 1)
            sp.dma_start(wqk[:, :, :], w_qk).then_inc(weights_in, 16)
            sp.dma_start(wvr[:, :, :], w_vr).then_inc(weights_in, 16)
            sp.sem_inc(parts_free, 2)

            def step(b, more):
                for j in range(2):
                    if more:
                        sp.wait_ge(xn_ready, b * 2 + j + 1)
                        load(b * 2 + j + 2, j)
                    sp.wait_ge(lo_ready, b * 8 + 4 * j + 6)
                    for o in range(4):
                        dst = qk_d[o // 2, :, bass.ds(b * D + (o % 2) * P, P), j * CH:(j + 1) * CH
                                   ].rearrange("s p t -> p s t")
                        for slot, n, part in SLOTS[o // 2]:
                            src = parts[:, j, o, part:part + 1, :].to_broadcast([P, n, CH]) if o < 2 else \
                                parts[:, j, o, part:part + n, :]
                            sp.dma_start(dst[:, slot:slot + n, :], src).then_inc(parts_out[j], 16)
                    sp.wait_ge(parts_out[j], b * (16 * 12) + 16 * 12)
                    sp.sem_inc(parts_free, 1)

            with sp.Fori(0, NCH // 2 - 1) as b:
                step(b, True)
            step(NCH // 2 - 1, False)

        @block.scalar
        def _(act):
            act.sem_inc(vr_free, 2)
            with act.Fori(0, NCH // 2) as b:
                for j in range(2):
                    c = b * 2 + j
                    act.wait_ge(var_ready, c + 1)
                    nc.scalar.activation(small[:, 4, :], small[:, 3, :], ACT.Sqrt).then_inc(std_ready, 1)
                    act.wait_ge(vr_ready, c * 4 + XT0 - 4)
                    act.wait_ge(xTp_ready, c + 1)
                    nc.scalar.copy(xT[:, j, 0, :], banks[0][:, :]).then_inc(xT0_ready, 1)
                    act.wait_ge(parts_free, c + 1)
                    for o in range(5):
                        if o < 4:
                            act.wait_ge(qk_ready, c * 4 + o + 1)
                            nc.scalar.activation(parts[:, j, o, 0, :], banks[2 + o % 2][:, :], ACT.Copy,
                                                 scale=0.25 if o < 2 else 1.0).then_inc(hi_ready, 1)
                        if o > 0:
                            act.wait_ge(rest_ready, c * 4 + o + 2)
                            nc.scalar.copy(parts[:, j, o - 1, 1, :], rest[:, (o - 1) % 2, :]
                                           ).then_inc(mid_ready, 1)
                    for t in range(TPC):
                        act.wait_ge(vr_ready, c * 4 + XT0 + t + 1)
                        nc.scalar.copy(v_sb[:, bass.ds(b * NH, NH), j * TPC + t, :],
                                       banks[4 + t % 2][:, 0:D].rearrange("p (h d) -> p h d", h=NH))
                        nc.scalar.copy(logits[:, bass.ds(c * TPC + t, 1), :],
                                       banks[4 + t % 2][:, D:D + NE]).then_inc(vr_free, 1)

        @block.gpsimd
        def _(pool):
            pool.sem_inc(xn_free_pool, 2)
            pool.sem_inc(lo_ready, 2)
            with pool.Fori(0, NCH // 2) as b:
                for j in range(2):
                    c = b * 2 + j
                    pool.wait_ge(xn_ready, c + 1)
                    pool.sem_inc(tick, 1)
                    nc.gpsimd.tensor_copy(rows[:, bass.ds(c * TPC, TPC), 0:D],
                                          xn[:, j, :, :]).then_inc(xn_free_pool, 1)
                    for o in range(4):
                        pool.wait_ge(mid_ready, c * 4 + o + 1)
                        nc.gpsimd.tensor_tensor(parts[:, j, o, 2, :], rest[:, o % 2, :], parts[:, j, o, 1, :],
                                                ALU.subtract).then_inc(lo_ready, 1)

        @block.vector
        def _(dve):
            dve.wait_ge(consts_in, 32)
            nc.vector.memset(zeros[:, :], 0.0).then_inc(consts_ready, 1)
            nc.vector.memset(template[:, 0:ID_COL], 0.0).then_inc(consts_ready, 1)
            nc.vector.tensor_copy(template[:, ID_COL:ROW].bitcast(I32), ids[:, NTILE:NTILE + 1]
                                  ).then_inc(consts_ready, 1)
            nc.vector.tensor_copy(ident[:, :], consts[:, 0:P]).then_inc(consts_ready, 1)
            nc.vector.tensor_copy(cb[:, :], consts[:, P:6 * P]).then_inc(consts_ready, 1)
            nc.vector.tensor_copy(rows[:, :, ID_COL].bitcast(I32), ids[:, 0:NTILE]).then_inc(consts_ready, 1)
            dve.sem_inc(rest_ready, 2)
            with dve.Fori(0, NCH // 2) as b:
                for j in range(2):
                    c = b * 2 + j
                    chain = Chain(dve, dve_a, c * 15)
                    dve.wait_ge(x_in[j], b * 16 + 16)
                    for t in range(TPC):
                        chain.done(nc.vector.bn_stats(stats[:, t, :], xin[:, j, t, :]))
                    chain.wait()
                    chain.done(nc.vector.tensor_tensor(small[:, 0, :], stats[:, :, 1], stats[:, :, 4], ALU.add))
                    chain.done(nc.vector.tensor_tensor(small[:, 1, :], stats[:, :, 1], stats[:, :, 4],
                                                       ALU.subtract))
                    chain.done(nc.vector.tensor_tensor(small[:, 2, :], stats[:, :, 2], stats[:, :, 5], ALU.add))
                    chain.wait()
                    chain.done(nc.vector.tensor_scalar(small[:, 5, :], small[:, 0, :], 0.5, None, ALU.mult))
                    chain.done(nc.vector.tensor_tensor(small[:, 1, :], small[:, 1, :], small[:, 1, :], ALU.mult))
                    chain.done(nc.vector.tensor_scalar(small[:, 2, :], small[:, 2, :], 1.0 / D, EPS,
                                                       ALU.mult, ALU.add))
                    chain.wait()
                    nc.vector.scalar_tensor_tensor(small[:, 3, :], small[:, 1, :], 0.25, small[:, 2, :],
                                                   ALU.mult, ALU.add).then_inc(var_ready, 1)
                    dve.wait_ge(std_ready, c + 1)
                    chain.done(nc.vector.reciprocal(small[:, 6, :], small[:, 4, :]))
                    chain.wait()
                    chain.done(nc.vector.tensor_tensor(small[:, 7, :], small[:, 6, :], small[:, 6, :], ALU.mult))
                    chain.wait()
                    chain.done(nc.vector.tensor_tensor(small[:, 8, :], small[:, 7, :], small[:, 3, :], ALU.mult))
                    chain.wait()
                    chain.done(nc.vector.tensor_scalar(small[:, 7, :], small[:, 8, :], -0.5, 1.5,
                                                       ALU.mult, ALU.add))
                    chain.wait()
                    chain.done(nc.vector.tensor_tensor(small[:, 9, :], small[:, 6, :], small[:, 7, :], ALU.mult))
                    chain.wait()
                    assert chain.n == 15
                    dve.wait_ge(xn_free_pool, c + 1)
                    dve.wait_ge(xn_free_pe, c + 1)
                    for t in range(TPC):
                        last = nc.vector.tensor_scalar(xn[:, j, t, :], xin[:, j, t, :], small[:, 5, t:t + 1],
                                                       small[:, 9, t:t + 1], ALU.subtract, ALU.mult)
                    last.then_inc(xn_ready, 1)
                    dve.wait_ge(vr_ready, c * 4 + XT0 - 4)
                    dve.wait_ge(xTp_ready, c + 1)
                    nc.vector.tensor_copy(xT[:, j, 1, :], banks[1][:, :]).then_inc(xT1_ready, 1)
                    for o in range(4):
                        dve.wait_ge(hi_ready, c * 4 + o + 1)
                        dve.wait_ge(lo_ready, c * 4 + o + 1)
                        nc.vector.scalar_tensor_tensor(rest[:, o % 2, :], banks[2 + o % 2][:, :],
                                                       0.25 if o < 2 else 1.0, parts[:, j, o, 0, :],
                                                       ALU.mult, ALU.subtract).then_inc(rest_ready, 1)

        @block.tensor
        def _(pe):
            pe.sem_inc(xn_free_pe, 2)
            pe.sem_inc(vr_ready, XT0)
            pe.wait_ge(consts_ready, 6)
            pe.wait_ge(weights_in, 32)

            def transposes(c, j):
                pe.wait_ge(xn_ready, c + 1)
                for t in range(TPC):
                    for h in range(2):
                        last = nc.tensor.transpose(banks[h][:, t * P:(t + 1) * P],
                                                   xn[:, j, t, h * P:(h + 1) * P], ident[:, :])
                last.then_inc(xTp_ready, 1)

            def products(c, j):
                pe.wait_ge(xT0_ready, c + 1)
                pe.wait_ge(xT1_ready, c + 1)
                pe.sem_inc(xn_free_pe, 1)
                for o in range(4):
                    pe.wait_ge(rest_ready, c * 4 + o + 1)
                    for h in range(2):
                        last = nc.tensor.matmul(banks[2 + o % 2][:, :], wqk[:, h, o * P:(o + 1) * P],
                                                xT[:, j, h, :], start=(h == 0), stop=(h == 1))
                    last.then_inc(qk_ready, 1)
                for t in range(TPC):
                    pe.wait_ge(vr_free, c * 4 + t + 1)
                    for h in range(2):
                        last = nc.tensor.matmul(banks[4 + t % 2][:, 0:D + NE], xT[:, j, h, t * P:(t + 1) * P],
                                                wvr[:, h, :], start=(h == 0), stop=(h == 1))
                    last.then_inc(vr_ready, 1)

            with pe.Fori(0, NCH // 2) as b:
                for j in range(2):
                    transposes(b * 2 + j, j)
                    products(b * 2 + j, j)

    dve_r = sem("dve_r")
    ex_ready, chosen_ready, count_ready = sem("ex_ready"), sem("chosen_ready"), sem("count_ready")
    rows_ready, rows_out, meta_ready, meta_out, meta_in, last_ready = (
        sem("rows_ready"), sem("rows_out"), sem("meta_ready"), sem("meta_out"), sem("meta_in"), sem("last_ready"))

    with nc.Block() as block:
        @block.scalar
        def _(act):
            nc.scalar.activation(aff[:, :, :], logits[:, :, :], ACT.Exp, scale=-1.0).then_inc(ex_ready, 1)

        @block.tensor
        def _(pe):
            pe.wait_ge(chosen_ready, 1)
            for k in range(4):
                m = chosen[:, 8 * k:8 * k + 8, :].rearrange("p n e -> p (n e)")
                nc.tensor.matmul(banks[4 + k][:, :], ones_b, m, start=True, stop=True)
                last = nc.tensor.matmul(banks[k][:, :], before, m, start=True, stop=True)
            last.then_inc(count_ready, 1)

        @block.sync
        def _(sp):
            sp.wait_ge(rows_ready, 1)
            sp.dma_start(rows_d.rearrange("(n p) c -> p n c", p=P), rows[:, :, :]).then_inc(rows_out, 16)
            sp.dma_start(slots_d[EMPTY * P:(EMPTY + 1) * P, :], template[:, :]).then_inc(fill_done, 16)
            sp.wait_ge(last_ready, 1)
            with sp.Fori(0, NE // 8) as i:
                last_regs, any_regs = ([sp.alloc_register(f"{name}{k}") for k in range(8)]
                                       for name in ("last_block", "any_block"))
                sp.load(last_regs, blk_table[0:1, 0, bass.ds(i * 8, 8)])
                sp.load(any_regs, blk_table[0:1, 1, bass.ds(i * 8, 8)])
                for k in range(8):
                    at = bass.RuntimeValue.of_register_unchecked(last_regs[k], min_val=0, max_val=NB_ROUTED - 1)
                    some = bass.RuntimeValue.of_register_unchecked(any_regs[k], min_val=0, max_val=1)
                    sp.dma_start(slots_d[bass.ds(at * P, P), :], template[:, :], cond=some).then_inc(fill_done, 16)
            sp.wait_ge(meta_ready, 1)
            sp.dma_start(meta_d.rearrange("f (c p) -> p f c", p=P), meta_c[:, :, :],
                         allow_slow_non_contiguous=True).then_inc(meta_out, 16)
            sp.wait_ge(meta_out, 16)
            sp.dma_start(meta[:, :, :], meta_d.unsqueeze(0)).then_inc(meta_in, 16)
            sp.wait_ge(rows_out, 16)
            sp.wait_ge(meta_in, 16)

        @block.vector
        def _(dve):
            chain = Chain(dve, dve_r)
            dve.wait_ge(ex_ready, 1)
            chain.done(nc.vector.tensor_scalar(work[:, :, :], aff[:, :, :], 1.0, None, ALU.add))
            chain.wait()
            chain.done(nc.vector.reciprocal(aff[:, :, :], work[:, :, :]))
            chain.wait()
            for n in range(NTILE):
                chain.done(nc.vector.max(top8[:, n, :], aff[:, n, :]))
            chain.wait()
            for n in range(NTILE):
                chain.done(nc.vector.match_replace(work[:, n, :], top8[:, n, :], aff[:, n, :], -1.0))
            chain.wait()
            nc.vector.tensor_scalar(chosen[:, :, :], work[:, :, :], 0.0, None, ALU.is_lt).then_inc(chosen_ready, 1)
            chain.done(nc.vector.tensor_reduce(rsum[:, :], top8[:, :, :], AX.X, ALU.add))
            chain.wait()
            chain.done(nc.vector.tensor_scalar(rsum[:, :], rsum[:, :], 1e-9, None, ALU.add))
            chain.wait()
            chain.done(nc.vector.reciprocal(junk[:, 0:NTILE], rsum[:, :]))
            dve.wait_ge(chosen_ready, 1)
            chain.done(nc.vector.tensor_tensor(work[:, :, :], aff[:, :, :], chosen[:, :, :], ALU.mult))
            chain.wait()
            nc.vector.tensor_tensor(rows[:, :, W_COL:W_COL + NE], work[:, :, :],
                                    junk[:, 0:NTILE].unsqueeze(2).to_broadcast([P, NTILE, NE]),
                                    ALU.mult).then_inc(rows_ready, 1)
            dve.wait_ge(count_ready, 1)
            chain.done(nc.vector.memset(base[:, 0, :], 0.0))
            for n in range(NTILE):
                chain.wait()
                chain.done(nc.vector.tensor_tensor(base[:, n + 1, :], base[:, n, :],
                                                   banks[4 + n // 8][:, (n % 8) * NE:(n % 8 + 1) * NE], ALU.add))
            chain.wait()
            chain.done(nc.vector.tensor_scalar(blk_i[:, :], base[:, NTILE, :], float(P - 1), None, ALU.add))
            chain.wait()
            chain.done(nc.vector.tensor_scalar(blk_i[:, :], blk_i[:, :], 7, None, ALU.logical_shift_right))
            chain.wait()
            nblk, ends, starts, some, one = (blk[:, k, :] for k in range(5))
            chain.done(nc.vector.tensor_copy(nblk, blk_i[:, :]))
            chain.done(nc.vector.memset(one, 1.0))
            chain.wait()
            chain.done(nc.vector.tensor_tensor_scan(ends, one, nblk, 0.0, ALU.mult, ALU.add))
            chain.done(nc.vector.tensor_scalar(some, nblk, 0.0, None, ALU.is_gt))
            chain.wait()
            chain.done(nc.vector.tensor_tensor(starts, ends, nblk, ALU.subtract))
            chain.done(nc.vector.tensor_scalar(blk_table[:, 0, :], ends, -1.0, 0.0, ALU.add, ALU.max))
            chain.done(nc.vector.tensor_copy(blk_table[:, 1, :], some))
            chain.wait()
            dve.sem_inc(last_ready, 1)
            chain.done(nc.vector.tensor_scalar(starts, starts, float(P), 1.0, ALU.mult, ALU.add))
            chain.wait()
            chain.done(nc.vector.tensor_tensor(base[:, 0:NTILE, :], base[:, 0:NTILE, :],
                                               starts.unsqueeze(1).to_broadcast([P, NTILE, NE]), ALU.add))
            chain.wait()
            for k in range(4):
                chain.done(nc.vector.tensor_tensor(
                    work[:, 8 * k:8 * k + 8, :].rearrange("p n e -> p (n e)"), banks[k][:, :],
                    base[:, 8 * k:8 * k + 8, :].rearrange("p n e -> p (n e)"), ALU.add))
            chain.wait()
            chain.done(nc.vector.tensor_tensor(work[:, :, :], work[:, :, :], chosen[:, :, :], ALU.mult))
            chain.wait()
            for n in range(NTILE):
                chain.done(nc.vector.max(top8[:, n, :], work[:, n, :]))
            chain.wait()
            chain.done(nc.vector.tensor_scalar(idx8[:, :, :], top8[:, :, :], -1.0, None, ALU.add))
            for c in range(MB):
                for f, of, col in ((0, one, c), (1, some, c), (2, some, MB + c)):
                    chain.done(nc.vector.scalar_tensor_tensor(
                        junk[:, :], ends, consts[:, 6 * P + col:6 * P + col + 1], of, ALU.is_le, ALU.mult,
                        accum_out=cols[:, f, c:c + 1]))
                    chain.wait()
            chain.done(nc.vector.tensor_copy(meta_c[:, E_F, :], cols[:, 0, :]))
            chain.done(nc.vector.tensor_copy(meta_c[:, AT_F, :], cols[:, 1, :]))
            chain.done(nc.vector.tensor_scalar(cols[:, 4, :], cols[:, 0, :], float(NE), None, ALU.is_lt))
            chain.done(nc.vector.tensor_tensor(cols[:, 3, :], cols[:, 1, :], cols[:, 2, :], ALU.subtract))
            chain.wait()
            chain.done(nc.vector.memset(cols[0:1, 3, 0:1], 1.0))
            chain.done(nc.vector.tensor_scalar(meta_c[:, AT_F, :], meta_c[:, AT_F, :], WR - 1, None,
                                               ALU.bitwise_and))
            chain.done(nc.vector.tensor_scalar(cols[:, 0, :], cols[:, 0, :], float(NE - 1), None, ALU.min))
            chain.done(nc.vector.tensor_scalar(cols[:, 6, :], consts[:, 6 * P:6 * P + MB], float(-EMPTY), None,
                                               ALU.add))
            chain.wait()
            chain.done(nc.vector.tensor_tensor(cols[:, 3, :], cols[:, 3, :], cols[:, 4, :], ALU.mult))
            chain.done(nc.vector.tensor_tensor(cols[:, 6, :], cols[:, 6, :], cols[:, 4, :], ALU.mult))
            chain.done(nc.vector.tensor_copy(meta_c[:, E_F, :], cols[:, 0, :]))
            chain.done(nc.vector.tensor_scalar(cols[:, 5, :], meta_c[:, AT_F, :], float(1 << PLACE_BIT), None,
                                               ALU.mult))
            chain.wait()
            chain.done(nc.vector.tensor_scalar(meta_c[:, SRC_F, :], cols[:, 6, :], float(EMPTY), None, ALU.add))
            chain.done(nc.vector.tensor_scalar(meta_c[:, AT_F, :], meta_c[:, AT_F, :], WCOLS, None, ALU.mult))
            chain.done(nc.vector.scalar_tensor_tensor(cols[:, 3, :], cols[:, 3, :], float(1 << NEW_BIT),
                                                      cols[:, 0, :], ALU.mult, ALU.add))
            chain.wait()
            chain.done(nc.vector.tensor_tensor(meta_c[:, LOAD_F, :], cols[:, 3, :], cols[:, 5, :], ALU.add))
            chain.wait()
            dve.sem_inc(meta_ready, 1)


def attend(nc, ctx, keep, onorm, x, w_proj, res, wp, m_in):
    qk_d, rows_d, slots_d, meta_d, acc_d = keep["dram"]
    ident, cb, v_sb, meta, idx8, zeros, banks, fill_done = keep["sbuf"]
    ident_b, mask_prev, mask_next = (cb[:, k * P:(k + 1) * P] for k in (0, 3, 4))

    def sb(name, shape, dt=F32):
        return ctx.enter_context(nc.sbuf_tensor(name, shape, dt))

    def sem(name):
        return ctx.enter_context(nc.semaphore(name))

    def sems(name, n):
        return [sem(f"{name}{i}") for i in range(n)]

    qk = sb("qk", [KM, 2, HG, T], BF16)
    qT, kT = qk[:, 0, :, :], qk[:, 1, :, :]
    va = sb("va", [P, HG, TT, 32])
    nmax = sb("nmax", [P, HG, TT])
    nmax_b = sb("nmax_b", [P, HG, 2, TT], BF16)
    nmaxT = sb("nmaxT", [2 * TT, HG, P], BF16)
    pT = sb("pT", [P, 4, 3 * P])
    oT = sb("oT", [P, T])
    rec = sb("rec", [P, TT // 2, HG])
    row_ring = sb("row_ring", [P, 2, ROW])
    idx_ring = sb("idx_ring", [P, 2, K], I32)

    S1, S2, OB = 0, 3, 5
    misc = banks[7]
    misc_b = misc.bitcast(BF16)
    both_o = keep["psum"][:, OB:OB + 2, :]

    va_const, va_ready = sem("va_const"), sem("va_ready")
    qk_in, nrow_in = sems("qk_in", HG), sems("nrow_in", HG)
    s1_ready, s1_free = sem("s1_ready"), sem("s1_free")
    hi_done, nmax_ready, misc_ready, misc_free, rec_ready = (
        sem("hi_done"), sem("nmax_ready"), sem("misc_ready"), sem("misc_free"), sem("rec_ready"))
    s2_ready, p_ready, pv_done, o_read = sem("s2_ready"), sem("p_ready"), sem("pv_done"), sem("o_read")
    rows_in, scattered = sems("rows_in", 2), sems("scattered", 2)
    idx_ready, pool_tick, cleared = sem("idx_ready"), sem("pool_tick"), sem("cleared")

    def is_first(g):
        return isinstance(g, int) and g == 0

    def maxima_write(g, hh):
        return 1 + hh if is_first(g) else g * 6 - 1 + (0, 2, 4, 5)[hh]

    def outputs_write(g, half):
        return g * 6 - 1 + (1, 3)[half]

    def window(i):
        return max(i - 1, 0), min(i + 2, TT)

    with nc.Block() as block:
        @block.sync
        def _(sp):
            def load(u, hh):
                for s in range(2):
                    sp.dma_start(qk[0:KS, s, hh, :], qk_d[s, :, bass.ds(u * DK, DK), :]).then_inc(qk_in[hh], 16)

            def maxima(hh, write):
                sp.wait_ge(misc_free, write + 1)
                for s in range(2):
                    dst = qT[KS + s:KS + s + 1, hh, :].rearrange("o (t q) -> o t q", t=TT)
                    sp.dma_start(dst, nmaxT[s * TT:(s + 1) * TT, hh, :]).then_inc(nrow_in[hh], 16)

            def load_rows(g, j):
                if not is_first(g):
                    sp.wait_ge(scattered[j], g * (16 * K))
                sp.dma_start(row_ring[:, j, :], rows_d[bass.ds(g * (2 * P) + j * P, P), :]).then_inc(rows_in[j], 16)

            def clear(g, k):
                sp.dma_start(acc_d[k][bass.ds(g * (NTOK // NG), NTOK // NG), :].rearrange("(p n) c -> p (n c)", p=P),
                             zeros[:, 0:NTOK // NG * D // P]).then_inc(cleared, 16)

            def group(g, last):
                for hh in range(HG):
                    clear(g, hh)
                    if hh % 2 == 1 and not last:
                        load_rows(g + 1, hh // 2)
                    if not (last and hh == HG - 1):
                        maxima((hh + 1) % HG, maxima_write(g, hh))
                    if not (last and hh > 0):
                        if not is_first(g) or hh > 0:
                            sp.wait_ge(pv_done, g * (HG * TT) + hh * TT)
                        load(g * HG + hh + 3, (hh + 3) % HG)

            for hh in range(3):
                load(hh, hh)
            for j in range(2):
                load_rows(0, j)
            maxima(0, 0)
            group(0, False)
            with sp.Fori(1, NG - 1) as g:
                group(g, False)
            group(NG - 1, True)
            for k in range(NACC):
                sp.dma_start(acc_d[k][NTOK:NTOK + P, :], zeros[:, 0:D]).then_inc(cleared, 16)
            sp.dma_start(wp[:, :, :], w_proj).then_inc(m_in, 16)
            sp.dma_start(res[:, :, :], x.rearrange("n p c -> p n c")).then_inc(m_in, 16)
            sp.wait_ge(cleared, 16 * (NG + 1) * NACC)

        @block.tensor
        def _(pe):
            pe.wait_ge(va_const, 3)

            def masks(bank, i, n):
                if i > 0:
                    last = nc.tensor.matmul(banks[bank][:, 0:P], ident_b, mask_prev, start=False,
                                            stop=(i == TT - 1), skip_group_check=True)
                if i < TT - 1:
                    last = nc.tensor.matmul(banks[bank][:, n - P:n], ident_b, mask_next, start=False, stop=True,
                                            skip_group_check=True)
                return last

            def scores_q(g, ahead, i):
                hh, n = ahead % HG, ahead * TT + i
                lo, hi = window(i)
                back = {0: 2, 1: 2, 2: 5}.get(i, 3)
                if not is_first(g) or n >= back:
                    pe.wait_ge(s1_free, g * (HG * TT) + (n - back + 1))
                nc.tensor.matmul(banks[S1 + i % 3][:, 0:(hi - lo) * P], qT[0:KS, hh, i * P:(i + 1) * P],
                                 kT[0:KS, hh, lo * P:hi * P], start=True, stop=False, skip_group_check=True)
                masks(S1 + i % 3, i, (hi - lo) * P).then_inc(s1_ready, 1)

            def scores_k(g, hh, j):
                lo, hi = window(j)
                if not is_first(g) or hh > 0 or j > 1:
                    pe.wait_ge(p_ready, g * (HG * TT) + (hh * TT + j - 1))
                nc.tensor.matmul(banks[S2 + j % 2][:, 0:(hi - lo) * P], kT[0:KM, hh, j * P:(j + 1) * P],
                                 qT[0:KM, hh, lo * P:hi * P], start=True, stop=False, skip_group_check=True)
                masks(S2 + j % 2, j, (hi - lo) * P).then_inc(s2_ready, 1)

            def values(g, hh, j):
                lo, hi = window(j)
                pe.wait_ge(p_ready, g * (HG * TT) + (hh * TT + j + 1))
                for bank in range(2):
                    a, b = max(lo, 4 * bank), min(hi, 4 * bank + 4)
                    if a < b:
                        last = nc.tensor.matmul(
                            banks[OB + bank][32 * hh:32 * hh + 32, (a - 4 * bank) * P:(b - 4 * bank) * P],
                            va[:, hh, j, :], pT[:, j % 4, (a - lo) * P:(b - lo) * P],
                            start=(j == (0, 3)[bank]), stop=(j == (4, 7)[bank]), skip_group_check=True)
                last.then_inc(pv_done, 1)

            def turn_maxima(g, ahead, write):
                pe.wait_ge(nmax_ready, g * HG + (ahead + 1))
                if not (isinstance(write, int) and write == 0):
                    pe.wait_ge(misc_free, write)
                nc.tensor.transpose(misc_b[0:2 * TT, 0:P],
                                    nmax_b[:, ahead % HG, :, :].rearrange("p s t -> p (s t)"),
                                    ident_b).then_inc(misc_ready, 1)

            def turn_outputs(g, half):
                pe.wait_ge(o_read, g)
                pe.wait_ge(misc_free, outputs_write(g, half))
                for t in range(4):
                    last = nc.tensor.transpose(misc[:, t * P:(t + 1) * P],
                                               oT[:, (4 * half + t) * P:(4 * half + t + 1) * P], ident[:, :])
                last.then_inc(misc_ready, 1)

            def group(g, last):
                for hh in range(HG):
                    if not (last and hh == HG - 1):
                        turn_maxima(g, hh + 1, maxima_write(g, hh))
                    pe.wait_ge(va_ready, g * HG + (hh + 1))
                    pe.wait_ge(nrow_in[hh], g * 32 + 32)
                    for j in range(TT):
                        scores_k(g, hh, j)
                        if j == 2 and hh == 0 and not is_first(g):
                            pe.wait_ge(o_read, g)
                        if j > 1:
                            values(g, hh, j - 2)
                        if not (last and hh > 1):
                            if j == 0:
                                pe.wait_ge(qk_in[(hh + 2) % HG], g * 32 + (32 if hh < 2 else 64))
                            scores_q(g, hh + 2, j)
                        if j == 4 and hh < 2 and not is_first(g):
                            turn_outputs(g, hh)
                    values(g, hh, TT - 2)
                    values(g, hh, TT - 1)

            for hh in range(2):
                pe.wait_ge(qk_in[hh], 32)
                for i in range(TT):
                    scores_q(0, hh, i)
            turn_maxima(0, 0, 0)
            group(0, False)
            with pe.Fori(1, NG - 1) as g:
                group(g, False)
            group(NG - 1, True)
            for half in range(2):
                pe.wait_ge(o_read, NG)
                pe.wait_ge(misc_free, NG * 6 - 2 + half)
                for t in range(4):
                    last = nc.tensor.transpose(misc[:, t * P:(t + 1) * P],
                                               oT[:, (4 * half + t) * P:(4 * half + t + 1) * P], ident[:, :])
                last.then_inc(misc_ready, 1)

        @block.scalar
        def _(act):
            def group(g, last):
                for hh in range(HG):
                    for j in range(TT):
                        lo, hi = window(j)
                        n = hh * TT + j
                        if not is_first(g) or n > 3:
                            act.wait_ge(pv_done, g * (HG * TT) + (n - 3))
                        act.wait_ge(s2_ready, g * (HG * TT) + (n + 1))
                        nc.scalar.activation(pT[:, j % 4, 0:(hi - lo) * P], banks[S2 + j % 2][:, 0:(hi - lo) * P],
                                             ACT.Exp).then_inc(p_ready, 1)
                act.wait_ge(pv_done, g * (HG * TT) + HG * TT)
                nc.scalar.copy(oT.rearrange("p (b q) -> p b q", b=2), both_o).then_inc(o_read, 1)

            group(0, False)
            with act.Fori(1, NG - 1) as g:
                group(g, False)
            group(NG - 1, True)

        @block.vector
        def _(dve):
            nc.vector.memset(va[:, :, :, DK + 1:32], 0.0).then_inc(va_const, 1)
            nc.vector.memset(va[:, :, :, DK:DK + 1], 1.0).then_inc(va_const, 1)
            nc.vector.memset(kT[KS:KM, :, :], 1.0).then_inc(va_const, 1)

            def maxima(g, ahead, i):
                hh = ahead % HG
                lo, hi = window(i)
                dve.wait_ge(s1_ready, g * (HG * TT) + (ahead * TT + i + 1))
                nc.vector.tensor_reduce(nmax[:, hh, i:i + 1], banks[S1 + i % 3][:, 0:(hi - lo) * P],
                                        AX.X, ALU.max, negate=True).then_inc(s1_free, 1)

            def split_maxima(g, ahead):
                hh = ahead % HG
                dve.wait_ge(s1_free, g * (HG * TT) + (ahead * TT + TT))
                nc.vector.tensor_copy(nmax_b[:, hh, 0, :], nmax[:, hh, :]).then_inc(hi_done, 1)
                dve.wait_ge(hi_done, g * HG + (ahead + 1))
                nc.vector.tensor_tensor(nmax_b[:, hh, 1, :], nmax[:, hh, :], nmax_b[:, hh, 0, :],
                                        ALU.subtract).then_inc(nmax_ready, 1)

            def copy_maxima(hh, write):
                dve.wait_ge(misc_ready, write + 1)
                nc.vector.tensor_copy(nmaxT[:, hh, :], misc_b[0:2 * TT, 0:P]).then_inc(misc_free, 1)

            def copy_values(g, ahead):
                nc.vector.tensor_copy(va[:, ahead % HG, :, 0:DK],
                                      v_sb[:, bass.ds(g * HG + ahead, 1), :, :].rearrange("p o t d -> p (o t) d")
                                      ).then_inc(va_ready, 1)

            def normalise(g, half, write, done):
                dve.wait_ge(misc_ready, write + 1)
                o = misc.rearrange("p (t h c) -> p t h c", t=TT // 2, h=HG)
                nc.vector.reciprocal(rec[:, :, :], o[:, :, :, DK]).then_inc(rec_ready, 1)
                dve.wait_ge(rec_ready, done)
                dst = onorm[:, bass.ds(g * TT + half * (TT // 2), TT // 2), :]
                nc.vector.tensor_tensor(dst.rearrange("p t (h d) -> p t h d", h=HG), o[:, :, :, 0:DK],
                                        rec[:, :, :].unsqueeze(3).to_broadcast([P, TT // 2, HG, DK]),
                                        ALU.mult).then_inc(misc_free, 1)

            def group(g, last):
                for hh in range(HG):
                    if not (last and hh == HG - 1):
                        copy_maxima((hh + 1) % HG, maxima_write(g, hh))
                        if not is_first(g) or hh == 3:
                            dve.wait_ge(pv_done, g * (HG * TT) + (hh - 2) * TT)
                        copy_values(g, hh + 1)
                    for i in range(TT):
                        if not (last and hh > 1):
                            maxima(g, hh + 2, i)
                        if i == 4 and hh < 2 and not is_first(g):
                            normalise(g - 1, hh, outputs_write(g, hh), g * 2 - 1 + hh)
                    if not (last and hh > 1):
                        split_maxima(g, hh + 2)

            copy_values(0, 0)
            for hh in range(2):
                for i in range(TT):
                    maxima(0, hh, i)
                split_maxima(0, hh)
            copy_maxima(0, 0)
            group(0, False)
            with dve.Fori(1, NG - 1) as g:
                group(g, False)
            group(NG - 1, True)
            for half in range(2):
                normalise(NG - 1, half, NG * 6 - 2 + half, NG * 2 - 1 + half)

        @block.gpsimd
        def _(pool):
            def step(i, j):
                n = i * 2 + j
                if not is_first(i):
                    pool.wait_ge(scattered[j], i * (16 * K))
                    pool.sem_inc(pool_tick, 1)
                pool.wait_ge(rows_in[j], i * 16 + 16)
                pool.sem_inc(pool_tick, 1)
                nc.gpsimd.tensor_copy(idx_ring[:, j, :].unsqueeze(1), idx8[:, bass.ds(n, 1), :]
                                      ).then_inc(idx_ready, 1)
                pool.wait_ge(idx_ready, n + 1)
                pool.sem_inc(pool_tick, 1)
                for k in range(K):
                    nc.gpsimd.indirect_dma_start(
                        out=slots_d, out_offset=bass.IndirectOffsetOnAxis(ap=idx_ring[:, j, k:k + 1], axis=0),
                        in_=row_ring[:, j, :], in_offset=None).then_inc(scattered[j], 16)

            pool.wait_ge(fill_done, 16 * (NE + 1))
            for j in range(2):
                step(0, j)
            with pool.Fori(1, NTILE // 2) as i:
                for j in range(2):
                    step(i, j)
            for j in range(2):
                pool.wait_ge(scattered[j], 16 * K * (NTILE // 2))


def merge(nc, ctx, keep, onorm, res, wp, m_in):
    ident, banks = keep["sbuf"][0], keep["sbuf"][6]

    def sb(name, shape, dt=F32):
        return ctx.enter_context(nc.sbuf_tensor(name, shape, dt))

    def sem(name):
        return ctx.enter_context(nc.semaphore(name))

    stage = sb("stage", [P, 2, D])
    oT2 = sb("oT2", [P, 2, 2, P])
    stage_ready, turned, turned_read, proj_ready, proj_read = (
        sem("stage_ready"), sem("turned"), sem("turned_read"), sem("proj_ready"), sem("proj_read"))

    tick = sem("merge_tick")

    with nc.Block() as block:
        @block.gpsimd
        def _(pool):
            pool.sem_inc(turned, 2)
            with pool.Fori(0, B) as b:
                for t in range(TT):
                    pool.wait_ge(turned, b * TT + t + 1)
                    pool.sem_inc(tick, 1)
                    src = onorm[:, bass.ds(b * (4 * TT), 4 * TT), :].rearrange("p (g t) c -> p g t c", g=4)[:, :, t, :]
                    nc.gpsimd.tensor_copy(stage[:, t % 2, :].rearrange("p (g c) -> p g c", g=4), src
                                          ).then_inc(stage_ready, 1)

        @block.tensor
        def _(pe):
            def turn(b, t):
                pe.wait_ge(turned_read, b * TT + t)
                pe.wait_ge(stage_ready, b * TT + t + 1)
                for h in range(2):
                    last = nc.tensor.transpose(banks[t % 2][:, h * P:(h + 1) * P],
                                               stage[:, t % 2, h * P:(h + 1) * P], ident[:, :])
                last.then_inc(turned, 1)

            def batch(b, last_batch):
                for t in range(TT):
                    n = b * TT + t
                    if not (last_batch and t == TT - 1):
                        turn(b, t + 1)
                    pe.wait_ge(turned_read, n + 2)
                    pe.wait_ge(proj_read, n + 1)
                    for h in range(2):
                        last = nc.tensor.matmul(banks[2 + t % 2][:, 0:D], oT2[:, t % 2, h, :], wp[:, h, :],
                                                start=(h == 0), stop=(h == 1))
                    last.then_inc(proj_ready, 1)

            pe.sem_inc(turned_read, 1)
            pe.wait_ge(m_in, 32)
            pe.wait_ge(stage_ready, 1)
            for h in range(2):
                last = nc.tensor.transpose(banks[0][:, h * P:(h + 1) * P], stage[:, 0, h * P:(h + 1) * P], ident[:, :])
            last.then_inc(turned, 1)
            with pe.Fori(0, B - 1) as b:
                batch(b, False)
            batch(B - 1, True)

        @block.scalar
        def _(act):
            act.sem_inc(proj_ready, 2)
            with act.Fori(0, B) as b:
                for t in range(TT):
                    act.wait_ge(turned, b * TT + t + 3)
                    act.wait_ge(proj_ready, b * TT + t + 1)
                    nc.scalar.copy(oT2[:, t % 2, :, :].rearrange("p h q -> p (h q)"), banks[t % 2][:, 0:D]
                                   ).then_inc(turned_read, 1)

        @block.vector
        def _(dve):
            dve.sem_inc(proj_read, 2)
            dve.wait_ge(m_in, 32)
            with dve.Fori(0, B) as b:
                for t in range(TT):
                    dve.wait_ge(proj_ready, b * TT + t + 3)
                    r = res[:, bass.ds(b * TT + t, 1), :].rearrange("p o c -> p (o c)")
                    nc.vector.tensor_tensor(r, banks[2 + t % 2][:, 0:D], r, ALU.add).then_inc(proj_read, 1)


def experts(nc, ctx, keep, w_exp):
    qk_d, rows_d, slots_d, meta_d, acc_d = keep["dram"]
    ident, cb, v_sb, meta, idx8, zeros, banks, fill_done = keep["sbuf"]

    def sb(name, shape, dt=F32):
        return ctx.enter_context(nc.sbuf_tensor(name, shape, dt))

    def sem(name):
        return ctx.enter_context(nc.semaphore(name))

    def sems(name, n):
        return [sem(f"{name}{i}") for i in range(n)]

    xb = sb("xb", [P, XR, ROW])
    wb = sb("wb", [P, WR * WCOLS])
    xT = sb("xTe", [P, 2, 2, P])
    gate = sb("gate", [P, 2, I])
    a_sb = sb("a_sb", [P, 2, I])
    aT = sb("aT", [P, 2, P])
    ys = sb("ys", [P, NACC, D])

    x_in, w_in, added = sems("xb_in", XR), sems("wb_in", WR), sems("added", NACC)
    px_ready, xT_ready, gu_ready, gate_ready, act_ready = (
        sem("px_ready"), sem("xTe_ready"), sem("gu_ready"), sem("gate_ready"), sem("act_ready"))
    pa_ready, aT_ready, y_ready, ys_ready = sem("pa_ready"), sem("aT_ready"), sem("y_ready"), sem("ys_ready")
    acc_free, tick = sem("acc_free"), sem("tick")
    PX, GU, PA, Y = 0, 2, 4, 6
    LAST = NB_ROUTED // XR - 1
    assert NB_ROUTED % XR == 0 and LAST > 1

    def first(i):
        return isinstance(i, int) and i == 0

    def exists(i, r):
        return not (isinstance(i, int) and i == LAST) or r < XR

    def every(engine, step):
        step(0)
        with engine.Fori(1, LAST) as i:
            step(i)
        step(LAST)

    number = count()

    def fields(engine, n, i, r, f, most):
        regs = [engine.alloc_register(f"field{f}_{next(number)}") for k in range(n)]
        engine.load(regs, meta[0:1, f, bass.ds(i * XR + r, n)])
        return [bass.RuntimeValue.of_register_unchecked(reg, min_val=0, max_val=most) for reg in regs]

    with nc.Block() as block:
        @block.sync
        def _(sp):
            def half(i, h):
                src = fields(sp, 8, i, 8 * h, SRC_F, EMPTY)
                load = fields(sp, 8, i, 8 * h, LOAD_F, (WR << PLACE_BIT) - 1)
                for k in range(8):
                    r = 8 * h + k
                    if not first(i):
                        sp.wait_ge(acc_free, i * XR + (r - XR + NACC + 1))
                    sp.dma_start(xb[:, r, :], slots_d[bass.ds(src[k] * P, P), :]).then_inc(x_in[r], 16)
                    if not first(i) or r >= WR:
                        sp.wait_ge(y_ready, i * XR + (r - WR + 1))
                    expert = (load[k] & ((1 << NEW_BIT) - 1)).with_bounds(min_val=0, max_val=NE - 1)
                    place = (load[k] >> PLACE_BIT).with_bounds(min_val=0, max_val=WR - 1)
                    sp.dma_start(wb[:, bass.ds(place * WCOLS, WCOLS)],
                                 w_exp[bass.ds(expert, 1), :, :].rearrange("e p n -> p (e n)"),
                                 cond=(load[k] >> NEW_BIT) & 1).then_inc(w_in[r % WR], 16)

            def step(i):
                for h in range(XR // 8):
                    half(i, h)

            every(sp, step)

        @block.tensor
        def _(pe):
            def turn_x(i, r):
                pe.wait_ge(x_in[r % XR], i * 16 + 16 * (r // XR + 1))
                if not first(i) or r > 1:
                    pe.wait_ge(xT_ready, i * XR + (r - 1))
                for h in range(2):
                    last = nc.tensor.transpose(banks[PX + r % 2][:, h * P:(h + 1) * P],
                                               xb[:, r % XR, h * P:(h + 1) * P], ident[:, :])
                last.then_inc(px_ready, 1)

            def gate_up(i, r, at):
                pe.wait_ge(w_in[r % WR], i * (16 * XR // WR) + 16 * (r // WR + 1))
                pe.wait_ge(xT_ready, i * XR + r + 1)
                for h in range(2):
                    last = nc.tensor.matmul(banks[GU + r % 2][:, 0:2 * I], xT[:, r % 2, h, :],
                                            wb[:, bass.ds(at + h * 2 * I, 2 * I)],
                                            start=(h == 0), stop=(h == 1))
                last.then_inc(gu_ready, 1)

            def turn_a(i, r):
                pe.wait_ge(act_ready, i * XR + r + 1)
                nc.tensor.transpose(banks[PA + r % 2][:, 0:P], a_sb[:, r % 2, :], ident[:, :]).then_inc(pa_ready, 1)

            def down(i, r, at):
                if not first(i) or r > 1:
                    pe.wait_ge(ys_ready, i * XR + (r - 1))
                pe.wait_ge(aT_ready, i * XR + r + 1)
                nc.tensor.matmul(banks[Y + r % 2][:, 0:D], aT[:, r % 2, :], wb[:, bass.ds(at + 4 * I, D)],
                                 start=True, stop=True).then_inc(y_ready, 1)

            def step(i):
                for r in range(XR):
                    k = r % 8
                    if k == 0:
                        at = fields(pe, 10 if exists(i, r + 9) else 8, i, r, AT_F, (WR - 1) * WCOLS)
                    if exists(i, r + 3):
                        turn_x(i, r + 3)
                    if exists(i, r + 2):
                        gate_up(i, r + 2, at[k + 2])
                    if exists(i, r + 1):
                        turn_a(i, r + 1)
                    down(i, r, at[k])

            at = fields(pe, 2, 0, 0, AT_F, (WR - 1) * WCOLS)
            turn_x(0, 0)
            turn_x(0, 1)
            gate_up(0, 0, at[0])
            turn_x(0, 2)
            gate_up(0, 1, at[1])
            turn_a(0, 0)
            every(pe, step)

        @block.scalar
        def _(act):
            def copy_x(i, r):
                if not first(i) or r > 1:
                    act.wait_ge(gu_ready, i * XR + (r - 1))
                act.wait_ge(px_ready, i * XR + r + 1)
                nc.scalar.copy(xT[:, r % 2, :, :].rearrange("p h q -> p (h q)"), banks[PX + r % 2][:, 0:D]
                               ).then_inc(xT_ready, 1)

            def silu(i, r):
                if not first(i) or r > 1:
                    act.wait_ge(act_ready, i * XR + (r - 1))
                act.wait_ge(gu_ready, i * XR + r + 1)
                nc.scalar.activation(gate[:, r % 2, :], banks[GU + r % 2][:, 0:I], ACT.Silu).then_inc(gate_ready, 1)

            def step(i):
                for r in range(XR):
                    if exists(i, r + 3):
                        copy_x(i, r + 3)
                    if exists(i, r + 2):
                        silu(i, r + 2)

            copy_x(0, 0)
            copy_x(0, 1)
            silu(0, 0)
            copy_x(0, 2)
            silu(0, 1)
            every(act, step)

        @block.vector
        def _(dve):
            def product(i, r, e):
                dve.wait_ge(gate_ready, i * XR + r + 1)
                if not first(i) or r > 1:
                    dve.wait_ge(pa_ready, i * XR + (r - 1))
                nc.vector.scalar_tensor_tensor(a_sb[:, r % 2, :], gate[:, r % 2, :],
                                               xb[:, r % XR, bass.ds(e + W_COL, 1)],
                                               banks[GU + r % 2][:, I:2 * I], ALU.mult, ALU.mult
                                               ).then_inc(act_ready, 1)

            def copy_a(i, r):
                if not first(i) or r > 1:
                    dve.wait_ge(y_ready, i * XR + (r - 1))
                dve.wait_ge(pa_ready, i * XR + r + 1)
                nc.vector.tensor_copy(aT[:, r % 2, :], banks[PA + r % 2][:, 0:P]).then_inc(aT_ready, 1)

            def step(i):
                for r in range(XR):
                    k = r % 8
                    if k == 0:
                        e = fields(dve, 10 if exists(i, r + 9) else 8, i, r, E_F, NE - 1)
                    if exists(i, r + 1):
                        copy_a(i, r + 1)
                    if exists(i, r + 2):
                        product(i, r + 2, e[k + 2])
                    dve.wait_ge(acc_free, i * XR + r + 1)
                    dve.wait_ge(y_ready, i * XR + r + 1)
                    nc.vector.tensor_copy(ys[:, r % NACC, :], banks[Y + r % 2][:, 0:D]).then_inc(ys_ready, 1)

            e = fields(dve, 2, 0, 0, E_F, NE - 1)
            product(0, 0, e[0])
            product(0, 1, e[1])
            copy_a(0, 0)
            every(dve, step)

        @block.gpsimd
        def _(pool):
            def step(i):
                for r in range(XR):
                    if not first(i) or r >= NACC:
                        pool.wait_ge(added[r % NACC], i * (16 * XR // NACC) + 16 * (r // NACC))
                    pool.sem_inc(acc_free, 1)
                    pool.wait_ge(ys_ready, i * XR + r + 1)
                    pool.sem_inc(tick, 1)
                    nc.gpsimd.indirect_dma_start(
                        out=acc_d[r % NACC],
                        out_offset=bass.IndirectOffsetOnAxis(ap=xb[:, r, ID_COL:ROW].bitcast(I32), axis=0),
                        in_=ys[:, r % NACC, :], in_offset=None, compute_op=ALU.add).then_inc(added[r % NACC], 16)

            every(pool, step)
            for r in range(NACC):
                pool.wait_ge(added[r], 16 * (NB_ROUTED // NACC))


def finish(nc, ctx, keep, w_exp, res, out):
    qk_d, rows_d, slots_d, meta_d, acc_d = keep["dram"]
    ident, banks = keep["sbuf"][0], keep["sbuf"][6]

    def sb(name, shape, dt=F32):
        return ctx.enter_context(nc.sbuf_tensor(name, shape, dt))

    def sem(name):
        return ctx.enter_context(nc.semaphore(name))

    def sems(name, n):
        return [sem(f"{name}{i}") for i in range(n)]

    S = 8
    NQ = NTILE // S
    w_sh = sb("w_sh", [P, WCOLS])
    xp = sb("xp", [P, 2, 2, D])
    acc = sb("acc", [P, S // 2, NACC, 2, D])
    xT = sb("xT_s", [P, 2, 2, P])
    gate = sb("gate_s", [P, 2, I])
    a_sb = sb("a_s", [P, 2, I])
    aT = sb("aT_s", [P, 2, P])

    w_in, x_in, acc_in = sem("w_sh_in"), sems("xp_in", 2), sems("acc_in", S // 2)
    px_ready, xT_ready, gu_ready, gate_ready, act_ready = (
        sem("px_s_ready"), sem("xT_s_ready"), sem("gu_s_ready"), sem("gate_s_ready"), sem("act_s_ready"))
    pa_ready, aT_ready, y_ready, y_added = (
        sem("pa_s_ready"), sem("aT_s_ready"), sem("y_s_ready"), sem("y_added"))
    half_a, half_b, both, sum_ready, stored, tick = (
        sem("half_a"), sem("half_b"), sem("both"), sem("sum_ready"), sem("stored"), sem("finish_tick"))
    PX, GU, PA, Y = 0, 2, 4, 6

    def first(q):
        return isinstance(q, int) and q == 0

    def exists(q, t):
        return (t >= 0 or not first(q)) and (t < S or not (isinstance(q, int) and q == NQ - 1))

    def every(engine, step):
        step(0)
        with engine.Fori(1, NQ - 1) as q:
            step(q)
        step(NQ - 1)

    with nc.Block() as block:
        @block.sync
        def _(sp):
            sp.dma_start(w_sh[:, :], w_exp[NE, :, :]).then_inc(w_in, 16)

            def load(q, j):
                for k in range(NACC):
                    sp.dma_start(acc[:, j, k, :, :], acc_d[k][bass.ds(q * (S * P) + j * (2 * P), 2 * P), :]
                                 .rearrange("(n p) c -> p n c", p=P)).then_inc(acc_in[j], 16)

            for j in range(S // 2):
                load(0, j)
            with sp.Fori(1, NQ) as q:
                for j in range(S // 2):
                    sp.wait_ge(sum_ready, q * (S // 2) + (j - S // 2 + 1))
                    load(q, j)

        @block.tensor
        def _(pe):
            def turn_x(q, t):
                pe.wait_ge(x_in[t // 2 % 2], q * (16 * S // 4) + 16 * (t // 4 + 1))
                if not first(q) or t > 1:
                    pe.wait_ge(xT_ready, q * S + (t - 1))
                for h in range(2):
                    last = nc.tensor.transpose(banks[PX + t % 2][:, h * P:(h + 1) * P],
                                               xp[:, t // 2 % 2, t % 2, h * P:(h + 1) * P], ident[:, :])
                last.then_inc(px_ready, 1)

            def gate_up(q, t):
                pe.wait_ge(xT_ready, q * S + t + 1)
                if not first(q) or t > 1:
                    pe.wait_ge(act_ready, q * S + (t - 1))
                for h in range(2):
                    last = nc.tensor.matmul(banks[GU + t % 2][:, 0:2 * I], xT[:, t % 2, h, :],
                                            w_sh[:, h * 2 * I:(h + 1) * 2 * I], start=(h == 0), stop=(h == 1))
                last.then_inc(gu_ready, 1)

            def turn_a(q, t):
                pe.wait_ge(act_ready, q * S + t + 1)
                if not first(q) or t > 1:
                    pe.wait_ge(aT_ready, q * S + (t - 1))
                nc.tensor.transpose(banks[PA + t % 2][:, 0:P], a_sb[:, t % 2, :], ident[:, :]).then_inc(pa_ready, 1)

            def down(q, t):
                pe.wait_ge(aT_ready, q * S + (t + 1))
                if not first(q) or t > 1:
                    pe.wait_ge(y_added, q * S + (t - 1))
                nc.tensor.matmul(banks[Y + t % 2][:, 0:D], aT[:, t % 2, :], w_sh[:, 4 * I:WCOLS],
                                 start=True, stop=True).then_inc(y_ready, 1)

            def step(q):
                for t in range(S):
                    if exists(q, t + 2):
                        turn_x(q, t + 2)
                    if exists(q, t + 1):
                        gate_up(q, t + 1)
                    turn_a(q, t)
                    if exists(q, t - 1):
                        down(q, t - 1)

            pe.wait_ge(w_in, 16)
            turn_x(0, 0)
            turn_x(0, 1)
            gate_up(0, 0)
            every(pe, step)
            down(NQ - 1, S - 1)

        @block.scalar
        def _(act):
            def load_x(q, j):
                act.dma_start(xp[:, j % 2, :, :], rows_d[bass.ds(q * (S * P) + j * (2 * P), 2 * P), 0:D]
                              .rearrange("(n p) c -> p n c", p=P)).then_inc(x_in[j % 2], 16)

            def copy_x(q, t):
                if not first(q) or t > 1:
                    act.wait_ge(gu_ready, q * S + (t - 1))
                act.wait_ge(px_ready, q * S + t + 1)
                nc.scalar.copy(xT[:, t % 2, :, :].rearrange("p h q -> p (h q)"), banks[PX + t % 2][:, 0:D]
                               ).then_inc(xT_ready, 1)
                if t % 2 == 1 and exists(q, t + 4):
                    load_x(q, t // 2 + 2)

            def silu(q, t):
                if not first(q) or t > 1:
                    act.wait_ge(act_ready, q * S + (t - 1))
                act.wait_ge(gu_ready, q * S + t + 1)
                nc.scalar.activation(gate[:, t % 2, :], banks[GU + t % 2][:, 0:I], ACT.Silu).then_inc(gate_ready, 1)

            def step(q):
                for t in range(S):
                    if exists(q, t + 2):
                        copy_x(q, t + 2)
                    if exists(q, t + 1):
                        silu(q, t + 1)
                    if t % 2 == 1 and exists(q, t - 2):
                        store(q, t // 2 - 1)

            def store(q, j):
                act.wait_ge(sum_ready, q * (S // 2) + (j + 1))
                act.dma_start(out[bass.ds(q * S + 2 * j, 2), :, :].rearrange("n p c -> p n c"),
                              res[:, bass.ds(q * S + 2 * j, 2), :]).then_inc(stored, 16)

            for j in range(2):
                load_x(0, j)
            copy_x(0, 0)
            copy_x(0, 1)
            silu(0, 0)
            every(act, step)
            store(NQ - 1, S // 2 - 1)
            act.wait_ge(stored, 16 * (NTILE // 2))

        @block.gpsimd
        def _(pool):
            with pool.Fori(0, NQ) as q:
                for j in range(S // 2):
                    pool.wait_ge(acc_in[j], q * (16 * NACC) + 16 * NACC)
                    nc.gpsimd.tensor_tensor(acc[:, j, 2, :, :], acc[:, j, 2, :, :], acc[:, j, 3, :, :],
                                            ALU.add).then_inc(half_b, 1)

        @block.vector
        def _(dve):
            def product(q, t):
                if not first(q) or t > 1:
                    dve.wait_ge(pa_ready, q * S + (t - 1))
                dve.wait_ge(gate_ready, q * S + t + 1)
                nc.vector.tensor_tensor(a_sb[:, t % 2, :], gate[:, t % 2, :], banks[GU + t % 2][:, I:2 * I],
                                        ALU.mult).then_inc(act_ready, 1)

            def copy_a(q, t):
                if not first(q) or t > 1:
                    dve.wait_ge(y_ready, q * S + (t - 1))
                dve.wait_ge(pa_ready, q * S + t + 1)
                nc.vector.tensor_copy(aT[:, t % 2, :], banks[PA + t % 2][:, 0:P]).then_inc(aT_ready, 1)

            def add_y(q, t):
                j = t // 2
                dve.wait_ge(acc_in[j], q * (16 * NACC) + 16 * NACC)
                dve.wait_ge(y_ready, q * S + (t + 1))
                nc.vector.tensor_tensor(acc[:, j, 0, t % 2, :], banks[Y + t % 2][:, 0:D], acc[:, j, 0, t % 2, :],
                                        ALU.add).then_inc(y_added, 1)

            def add_pair(q, j):
                slot = j % (S // 2)
                a0, a1, a2 = (acc[:, slot, k, :, :] for k in range(3))
                r = res[:, bass.ds(q * S + 2 * j, 2), :]
                dve.wait_ge(half_b, q * (S // 2) + (j + 1))
                nc.vector.tensor_tensor(a1, a1, a2, ALU.add).then_inc(half_a, 1)
                dve.wait_ge(y_added, q * S + (2 * j + 2))
                nc.vector.tensor_tensor(r, r, a0, ALU.add).then_inc(both, 1)
                dve.wait_ge(half_a, q * (S // 2) + (j + 1))
                dve.wait_ge(both, q * (S // 2) + (j + 1))
                nc.vector.tensor_tensor(r, r, a1, ALU.add).then_inc(sum_ready, 1)

            def step(q):
                for t in range(S):
                    copy_a(q, t)
                    if exists(q, t + 1):
                        product(q, t + 1)
                    if exists(q, t - 1):
                        add_y(q, t - 1) if t > 0 else add_y_before(q)
                    if t % 2 == 0 and exists(q, t - 2):
                        add_pair(q, t // 2 - 1)

            def add_y_before(q):
                j = S // 2 - 1
                dve.wait_ge(acc_in[j], q * (16 * NACC))
                dve.wait_ge(y_ready, q * S)
                nc.vector.tensor_tensor(acc[:, j, 0, 1, :], banks[Y + 1][:, 0:D], acc[:, j, 0, 1, :],
                                        ALU.add).then_inc(y_added, 1)

            product(0, 0)
            every(dve, step)
            add_y(NQ - 1, S - 1)
            add_pair(NQ - 1, S // 2 - 1)


def build(nc, x, w_qk, w_vr, w_proj, w_exp, c_f32, c_ids, out):
    with ExitStack() as ctx:
        def sb(name, shape, dt=F32):
            return ctx.enter_context(nc.sbuf_tensor(name, shape, dt))

        def dram(name, shape, dt=F32):
            return nc.dram_tensor(name, shape, dt, kind="Internal").ap()

        psum = ctx.enter_context(nc.psum_tensor("psum", [P, 8, 512], F32))
        keep = {
            "dram": (dram("qk_stacks", (2, KS // DK, B * D, T), BF16), dram("token_rows", (NTOK, ROW)),
                     dram("slot_rows", ((NB_ROUTED + 1) * P, ROW)), dram("block_table", (NFIELD, MB * P), I32),
                     [dram(f"acc{i}", (NTOK + P, D)) for i in range(NACC)]),
            "psum": psum,
            "sbuf": (sb("ident", [P, P]), sb("consts_bf16", [P, 5 * P], BF16), sb("v_sb", [P, NU, TT, DK]),
                     sb("block_table_row", [1, NFIELD, MB * P], I32), sb("slots_of_tokens", [P, NTILE, K], I32),
                     sb("zeros", [P, 1024]), [psum[:, i, :] for i in range(8)],
                     ctx.enter_context(nc.semaphore("fill_done"))),
        }
        with ExitStack() as inner:
            project_and_route(nc, inner, x, w_qk, w_vr, c_f32, c_ids, keep)
        res, wp = sb("res", [P, NTILE, D]), sb("wp", [P, 2, D])
        m_in = ctx.enter_context(nc.semaphore("m_in"))
        with ExitStack() as inner:
            onorm = inner.enter_context(nc.sbuf_tensor("onorm", [P, NG * TT, HG * DK], F32))
            with ExitStack() as deeper:
                attend(nc, deeper, keep, onorm, x, w_proj, res, wp, m_in)
            with ExitStack() as deeper:
                merge(nc, deeper, keep, onorm, res, wp, m_in)
        with ExitStack() as inner:
            experts(nc, inner, keep, w_exp)
        with ExitStack() as inner:
            finish(nc, inner, keep, w_exp, res, out)


def constants():
    r, c = np.arange(P)[:, None], np.arange(P)[None, :]
    f = np.zeros((P, 6 * P + 2 * MB), np.float32)
    f[:, 0:P] = r == c
    f[:, P:2 * P] = r == c
    f[:, 2 * P:3 * P] = r < c
    f[:, 3 * P:4 * P] = 1.0
    f[:, 4 * P:5 * P] = np.where(r > c, NEG, 0.0)
    f[:, 5 * P:6 * P] = np.where(c > r, NEG, 0.0)
    f[:, 6 * P:6 * P + MB] = r + P * np.arange(MB)[None, :]
    f[:, 6 * P + MB:] = f[:, 6 * P:6 * P + MB] - 1
    ids = np.zeros((P, NTILE + 1), np.int32)
    ids[:, :] = r + P * np.arange(NTILE + 1)[None, :]
    return f, ids


def kernel(L0_attn_x, L0_attn_w_qkv, L0_attn_w_proj, L0_ffn_router_w, L0_ffn_shared_gate_w,
           L0_ffn_shared_up_w, L0_ffn_shared_down_w, L0_ffn_expert_gate_k, L0_ffn_expert_up_k,
           L0_ffn_expert_down_k):
    import concourse.bacc as bacc
    from concourse.bass_utils import run_bass_kernel_spmd

    def halves(w):
        return np.ascontiguousarray(w.reshape(2, P, -1).transpose(1, 0, 2))

    w_qkv = np.asarray(L0_attn_w_qkv)
    gates = np.concatenate([np.asarray(L0_ffn_expert_gate_k), np.asarray(L0_ffn_shared_gate_w)[None]])
    ups = np.concatenate([np.asarray(L0_ffn_expert_up_k), np.asarray(L0_ffn_shared_up_w)[None]])
    downs = np.concatenate([np.asarray(L0_ffn_expert_down_k), np.asarray(L0_ffn_shared_down_w)[None]])
    gu = np.concatenate([gates, ups], axis=2).reshape(NE + 1, 2, P, 2 * I).transpose(0, 2, 1, 3)
    c_f32, c_ids = constants()
    arrays = {
        "x": np.ascontiguousarray(np.asarray(L0_attn_x).reshape(NTILE, P, D)),
        "w_qk": halves(w_qkv[0:2 * D].T),
        "w_vr": halves(np.concatenate([w_qkv[2 * D:3 * D].T, np.asarray(L0_ffn_router_w)], axis=1)),
        "w_proj": halves(np.asarray(L0_attn_w_proj).T),
        "w_exp": np.ascontiguousarray(np.concatenate([gu.reshape(NE + 1, P, 4 * I), downs], axis=2)),
        "c_f32": c_f32,
        "c_ids": c_ids,
    }
    nc = bacc.Bacc("TRN2", target_bir_lowering=False, num_devices=1)
    ins = [nc.dram_tensor("in_" + k, a.shape, mybir.dt.from_np(a.dtype), kind="ExternalInput").ap()
           for k, a in arrays.items()]
    out = nc.dram_tensor("out", (NTILE, P, D), F32, kind="ExternalOutput").ap()
    build(nc, *ins, out)
    r = run_bass_kernel_spmd(nc, [{"in_" + k: a for k, a in arrays.items()}], core_ids=[0])
    return r.results[0]["out"].reshape(B, T, D)
```

```python
from contextlib import ExitStack
from itertools import count

import numpy as np
import concourse.bass as bass
from concourse import mybir

F32 = mybir.dt.float32
BF16 = mybir.dt.bfloat16
I32 = mybir.dt.int32
ALU = mybir.AluOpType
ACT = mybir.ActivationFunctionType
AX = mybir.AxisListType

P = 128
B, T, D = 4, 1024, 256
NTOK = B * T
NTILE = NTOK // P
NH, DK = 16, 16
TT = T // P
NE, K, I = 64, 8, 128
EPS = 1e-5
MAGIC = float(0x5F3759DF)
NEG = -1.0e30

CH = 512
NCH = NTOK // CH
TPC = CH // P

NSPLIT = 3
SLOTS = ((0, 3, 0), (3, 2, 1), (5, 1, 2)), ((0, 3, 0), (3, 2, 0), (5, 1, 0))
KS = 6 * DK
KM = KS + 2
NU = B * NH
HG = 4
NG = NU // HG

NB_ROUTED = (NTOK * K) // P + NE
EMPTY = NB_ROUTED
W_COL, ID_COL = D, D + NE
ROW = D + NE + 1
WCOLS = 2 * 2 * I + D
NACC = 4
XR = 16
WR = 8
MB = 3
E_F, AT_F, LOAD_F, SRC_F = range(4)
NFIELD = 4
NEW_BIT, PLACE_BIT = 7, 8


class Chain:

    def __init__(self, engine, semaphore, base=0):
        self.engine, self.semaphore, self.base, self.n = engine, semaphore, base, 0

    def done(self, instruction):
        instruction.then_inc(self.semaphore, 1)
        self.n += 1

    def wait(self):
        self.engine.wait_ge(self.semaphore, self.base + self.n)


def project(nc, ctx, x, w_qk, w_vr, c_f32, c_ids, keep):
    qk_d, rows_d = keep["dram"][0:2]
    ident, cb, v_sb, _, _, zeros, banks = keep["sbuf"]
    before, ones_b = cb[:, P:2 * P], cb[:, 2 * P:3 * P]

    def sb(name, shape, dt=F32):
        return ctx.enter_context(nc.sbuf_tensor(name, shape, dt))

    def sem(name):
        return ctx.enter_context(nc.semaphore(name))

    wqk = sb("wqk", [P, 2, 2 * D])
    wvr = sb("wvr", [P, 2, D + NE])
    xin = sb("xin", [P, 2, TPC, D])
    xn = sb("xn", [P, 2, TPC, D])
    xT = sb("xT", [P, 2, 2, CH])
    stats = sb("stats", [P, TPC, 6])
    small = sb("small", [P, 10, TPC])
    parts = sb("parts", [P, 2, 4, NSPLIT, CH], BF16)
    rest = sb("rest", [P, 2, CH])
    rows = sb("rows", [P, 2, TPC, ROW])
    ids = sb("ids", [P, NTILE + 1], I32)
    template = keep["fill"][0]
    consts, chosen, base, slot = keep["routing"][0:4]
    ex = sb("ex", [P, 2, TPC, NE])
    aff = sb("aff", [P, 2, TPC, NE])
    marked = sb("marked", [P, TPC, NE])
    weights = sb("weights", [P, TPC, NE])
    best = sb("best", [P, TPC, K])
    rsum = sb("rsum", [P, 2, 2, TPC])

    consts_in, weights_in = sem("consts_in"), sem("weights_in")
    x_in = [sem("x_in0"), sem("x_in1")]
    consts_ready = sem("consts_ready")
    dve_a, dve_b, dve_c = sem("dve_a"), sem("dve_b"), sem("dve_c")
    VN = 22
    tick = sem("project_tick")
    xn_ready = sem("xn_ready")
    xn_copied, turned, xT_ready = sem("xn_copied"), sem("turned"), sem("xT_ready")
    qk_ready, hi_ready, rest_ready, mid_ready, lo_ready = (
        sem("qk_ready"), sem("hi_ready"), sem("rest_ready"), sem("mid_ready"), sem("lo_ready"))
    parts_out, rows_out = [sem("parts_out0"), sem("parts_out1")], [sem("rows_out0"), sem("rows_out1")]
    parts_free, rows_free = sem("parts_free"), sem("rows_free")
    vr_ready, vr_free = sem("vr_ready"), sem("vr_free")
    chosen_ready, share_ready, count_ready, count_read = (
        sem("chosen_ready"), sem("share_ready"), sem("count_ready"), sem("count_read"))
    weights_ready, rows_ready = sem("weights_ready"), sem("rows_ready")

    def chunks(engine, step):
        with engine.Fori(0, NCH // 2 - 1) as b:
            for j in range(2):
                step(b * 2 + j, b, j, False)
        for j in range(2):
            step(NCH - 2 + j, NCH // 2 - 1, j, j == 1)

    with nc.Block() as block:
        @block.sync
        def _(sp):
            def load(c, j):
                sp.dma_start(xin[:, j, :, :], x[bass.ds(c * TPC, TPC), :, :].rearrange("n p c -> p n c")
                             ).then_inc(x_in[j], 16)

            load(0, 0)
            sp.dma_start(consts[:, :], c_f32).then_inc(consts_in, 16)
            sp.dma_start(ids[:, :], c_ids).then_inc(consts_in, 16)
            sp.dma_start(wvr[:, :, :], w_vr).then_inc(weights_in, 16)
            sp.dma_start(wqk[:, :, :], w_qk).then_inc(weights_in, 16)
            load(1, 1)
            sp.sem_inc(parts_free, 2)
            sp.sem_inc(rows_free, 2)

            def step(c, b, j, last):
                if not (isinstance(c, int) and c >= NCH - 2):
                    sp.wait_ge(xn_ready, c + 1)
                    load(c + 2, j)
                for o in range(4):
                    sp.wait_ge(lo_ready, c * 4 + o + 3)
                    dst = qk_d[:, bass.ds(b * D + (o % 2) * P, P), o // 2, j * CH:(j + 1) * CH
                               ].rearrange("s p t -> p s t")
                    for first, n, part in SLOTS[o // 2]:
                        src = parts[:, j, o, part:part + 1, :].to_broadcast([P, n, CH]) if o < 2 else \
                            parts[:, j, o, part:part + n, :]
                        sp.dma_start(dst[:, first:first + n, :], src).then_inc(parts_out[j], 16)
                sp.wait_ge(rows_ready, c + 3)
                sp.dma_start(rows_d[bass.ds(c * CH, CH), :].rearrange("(n p) c -> p n c", p=P), rows[:, j, :, :]
                             ).then_inc(rows_out[j], 16)
                sp.wait_ge(parts_out[j], b * (16 * 12) + 16 * 12)
                sp.sem_inc(parts_free, 1)
                sp.wait_ge(rows_out[j], b * 16 + 16)
                sp.sem_inc(rows_free, 1)

            chunks(sp, step)

        @block.scalar
        def _(act):
            def copy_xT(c, j):
                act.wait_ge(turned, c + 2)
                nc.scalar.copy(xT[:, j, :, :], keep["psum"][:, 0:2, :]).then_inc(xT_ready, 1)

            def step(c, b, j, last):
                act.wait_ge(chosen_ready, c + 1)
                for t in range(TPC):
                    act.wait_ge(vr_ready, c * 4 + t + 1)
                    nc.scalar.copy(v_sb[:, bass.ds(b * NH, NH), j * TPC + t, :],
                                   banks[4 + t % 2][:, 0:D].rearrange("p (h d) -> p h d", h=NH))
                    nc.scalar.activation(ex[:, j, t, :], banks[4 + t % 2][:, D:D + NE], ACT.Exp, scale=-1.0
                                         ).then_inc(vr_free, 1)
                act.wait_ge(parts_free, c + 1)
                for o in range(5):
                    if o < 4:
                        act.wait_ge(qk_ready, c * 4 + o + 1)
                        nc.scalar.activation(parts[:, j, o, 0, :], banks[2 + o % 2][:, :], ACT.Copy,
                                             scale=0.25 if o < 2 else 1.0).then_inc(hi_ready, 1)
                    if o > 0:
                        act.wait_ge(rest_ready, c * 4 + o + 2)
                        nc.scalar.copy(parts[:, j, o - 1, 1, :], rest[:, (o - 1) % 2, :]).then_inc(mid_ready, 1)
                    if o == 1 and not last:
                        copy_xT(c + 1, 1 - j)

            copy_xT(0, 0)
            act.sem_inc(vr_free, 2)
            chunks(act, step)

        @block.gpsimd
        def _(pool):
            pool.sem_inc(lo_ready, 2)
            pool.sem_inc(xn_copied, 2)
            pool.wait_ge(consts_in, 32)
            pool.sem_inc(tick, 1)

            def step(c, b, j, last):
                pool.wait_ge(rows_free, c + 1)
                pool.sem_inc(tick, 1)
                pool.wait_ge(xn_ready, c + 1)
                pool.sem_inc(tick, 1)
                nc.gpsimd.tensor_copy(rows[:, j, :, 0:D], xn[:, j, :, :]).then_inc(xn_copied, 1)
                nc.gpsimd.tensor_copy(rows[:, j, :, ID_COL].bitcast(I32), ids[:, bass.ds(c * TPC, TPC)]
                                      ).then_inc(tick, 1)
                for o in range(4):
                    pool.wait_ge(mid_ready, c * 4 + o + 1)
                    nc.gpsimd.tensor_tensor(parts[:, j, o, 2, :], rest[:, o % 2, :], parts[:, j, o, 1, :],
                                            ALU.subtract).then_inc(lo_ready, 1)
                pool.wait_ge(share_ready, c + 1)
                nc.gpsimd.tensor_tensor(weights[:, :, :], aff[:, j, :, :], chosen[:, bass.ds(c * TPC + TPC, TPC), :],
                                        ALU.mult).then_inc(weights_ready, 1)
                pool.wait_ge(weights_ready, c + 1)
                nc.gpsimd.tensor_tensor(rows[:, j, :, W_COL:W_COL + NE], weights[:, :, :],
                                        rsum[:, j, 1, :].unsqueeze(2).to_broadcast([P, TPC, NE]),
                                        ALU.mult).then_inc(rows_ready, 1)

            chunks(pool, step)

        @block.vector
        def _(dve):
            def variances(c, b, j):
                chain = Chain(dve, dve_a, c * VN)
                dve.wait_ge(x_in[j], b * 16 + 16)
                for t in range(TPC):
                    chain.done(nc.vector.bn_stats(stats[:, t, :], xin[:, j, t, :]))
                chain.wait()
                chain.done(nc.vector.tensor_tensor(small[:, 0, :], stats[:, :, 1], stats[:, :, 4], ALU.add))
                chain.done(nc.vector.tensor_tensor(small[:, 1, :], stats[:, :, 1], stats[:, :, 4], ALU.subtract))
                chain.done(nc.vector.tensor_tensor(small[:, 2, :], stats[:, :, 2], stats[:, :, 5], ALU.add))
                chain.wait()
                chain.done(nc.vector.tensor_scalar(small[:, 5, :], small[:, 0, :], 0.5, None, ALU.mult))
                chain.done(nc.vector.tensor_tensor(small[:, 1, :], small[:, 1, :], small[:, 1, :], ALU.mult))
                chain.done(nc.vector.tensor_scalar(small[:, 2, :], small[:, 2, :], 1.0 / D, EPS,
                                                   ALU.mult, ALU.add))
                chain.wait()
                chain.done(nc.vector.scalar_tensor_tensor(small[:, 3, :], small[:, 1, :], 0.25, small[:, 2, :],
                                                          ALU.mult, ALU.add))
                chain.wait()
                bits, guess = small[:, 7, :].bitcast(I32), small[:, 6, :]
                chain.done(nc.vector.tensor_scalar(bits, small[:, 3, :].bitcast(I32), 1, None,
                                                   ALU.logical_shift_right))
                chain.wait()
                chain.done(nc.vector.tensor_scalar(guess.bitcast(I32), bits, -1.0, MAGIC, ALU.mult, ALU.add))
                for n, y in ((0, guess), (1, small[:, 4, :]), (2, guess)):
                    chain.wait()
                    chain.done(nc.vector.tensor_tensor(small[:, 7, :], y, y, ALU.mult))
                    chain.wait()
                    chain.done(nc.vector.scalar_tensor_tensor(small[:, 8, :], small[:, 7, :], -0.5, small[:, 3, :],
                                                              ALU.mult, ALU.mult))
                    chain.wait()
                    chain.done(nc.vector.scalar_tensor_tensor(small[:, (4, 6, 9)[n], :], small[:, 8, :], 1.5, y,
                                                              ALU.add, ALU.mult))
                assert chain.n == VN

            def normalise(c, b, j):
                dve.wait_ge(dve_a, c * VN + VN)
                dve.wait_ge(xn_copied, c + 1)
                if not (isinstance(c, int) and c == 0):
                    dve.wait_ge(turned, c)
                for t in range(TPC):
                    done = nc.vector.tensor_scalar(xn[:, j, t, :], xin[:, j, t, :], small[:, 5, t:t + 1],
                                                   small[:, 9, t:t + 1], ALU.subtract, ALU.mult)
                done.then_inc(xn_ready, 1)

            def leave(c, j, o):
                dve.wait_ge(hi_ready, c * 4 + o + 1)
                dve.wait_ge(lo_ready, c * 4 + o + 1)
                nc.vector.scalar_tensor_tensor(rest[:, o % 2, :], banks[2 + o % 2][:, :], 0.25 if o < 2 else 1.0,
                                               parts[:, j, o, 0, :], ALU.mult, ALU.subtract).then_inc(rest_ready, 1)

            def affinities(chain, c, j):
                dve.wait_ge(vr_free, c * 4 + TPC + 2)
                dve.wait_ge(rows_ready, c + 1)
                chain.done(nc.vector.tensor_scalar(ex[:, j, :, :], ex[:, j, :, :], 1.0, None, ALU.add))
                chain.wait()
                chain.done(nc.vector.reciprocal(aff[:, j, :, :], ex[:, j, :, :]))

            def choose(chain, c, j):
                chain.wait()
                dve.sem_inc(tick, 1)
                for t in range(TPC):
                    chain.done(nc.vector.max(best[:, t, :], aff[:, j, t, :]))
                chain.wait()
                dve.sem_inc(tick, 1)
                for t in range(TPC):
                    chain.done(nc.vector.match_replace(marked[:, t, :], best[:, t, :], aff[:, j, t, :], -1.0))
                chain.done(nc.vector.tensor_reduce(rsum[:, j, 0, :], best[:, :, :], AX.X, ALU.add))
                chain.wait()
                nc.vector.tensor_scalar(chosen[:, bass.ds(c * TPC + TPC, TPC), :], marked[:, :, :], 0.0, None,
                                        ALU.is_lt).then_inc(chosen_ready, 1)
                chain.done(nc.vector.tensor_scalar(rsum[:, j, 0, :], rsum[:, j, 0, :], 1e-9, None, ALU.add))
                chain.wait()
                assert chain.n == 4 + 2 * TPC
                dve.wait_ge(chosen_ready, c + 3)
                nc.vector.reciprocal(rsum[:, j, 1, :], rsum[:, j, 0, :]).then_inc(share_ready, 1)

            def count(c):
                dve.wait_ge(count_ready, c + 1)
                dve.wait_ge(dve_c, c + 1)
                nc.vector.tensor_tensor(slot[:, bass.ds(c * TPC, TPC), :],
                                        banks[6][:, 0:TPC * NE].rearrange("p (t e) -> p t e", t=TPC),
                                        base[:, bass.ds(c, 1), :].to_broadcast([P, TPC, NE]), ALU.add)
                nc.vector.tensor_tensor(base[:, bass.ds(c + 1, 1), :], base[:, bass.ds(c, 1), :],
                                        banks[7][:, 0:NE].unsqueeze(1), ALU.add).then_inc(dve_c, 1)
                dve.sem_inc(count_read, 1)

            def step(c, b, j, last):
                if not last:
                    normalise(c + 1, b + j, 1 - j)
                for o in range(2):
                    leave(c, j, o)
                count(c)
                leave(c, j, 2)
                chain = Chain(dve, dve_b, c * (4 + 2 * TPC))
                affinities(chain, c, j)
                leave(c, j, 3)
                if not (isinstance(c, int) and c >= NCH - 2):
                    variances(c + 2, b + 1, j)
                choose(chain, c, j)

            dve.sem_inc(chosen_ready, 2)
            dve.sem_inc(rows_ready, 2)
            dve.sem_inc(rest_ready, 2)
            variances(0, 0, 0)
            normalise(0, 0, 0)
            dve.wait_ge(consts_in, 32)
            nc.vector.tensor_copy(ident[:, :], consts[:, 0:P]).then_inc(consts_ready, 1)
            nc.vector.tensor_copy(cb[:, :], consts[:, P:6 * P]).then_inc(consts_ready, 1)
            nc.vector.memset(zeros[:, :], 0.0).then_inc(consts_ready, 1)
            nc.vector.memset(template[:, 0:ID_COL], 0.0).then_inc(consts_ready, 1)
            nc.vector.tensor_copy(template[:, ID_COL:ROW].bitcast(I32), ids[:, NTILE:NTILE + 1]
                                  ).then_inc(consts_ready, 1)
            nc.vector.memset(chosen[:, 0:TPC, :], 0.0).then_inc(consts_ready, 1)
            nc.vector.memset(base[:, 0, :], 0.0).then_inc(dve_c, 1)
            variances(1, 0, 1)

            chunks(dve, step)
            count(NCH)

        @block.tensor
        def _(pe):
            def transposes(c, j):
                pe.wait_ge(xn_ready, c + 1)
                for t in range(TPC):
                    for h in range(2):
                        done = nc.tensor.transpose(banks[h][:, t * P:(t + 1) * P],
                                                   xn[:, j, t, h * P:(h + 1) * P], ident[:, :])
                done.then_inc(turned, 1)

            def count(c):
                pe.wait_ge(chosen_ready, c + 2)
                pe.wait_ge(count_read, c + 1)
                def tiles(n):
                    return chosen[:, bass.ds(c * TPC, n), :].rearrange("p n e -> p (n e)")

                nc.tensor.matmul(banks[6][:, 0:TPC * NE], before, tiles(TPC), start=True, stop=False,
                                 skip_group_check=True)
                for t in range(1, TPC):
                    nc.tensor.matmul(banks[6][:, t * NE:TPC * NE], ones_b, tiles(TPC - t), start=False,
                                     stop=(t == TPC - 1), skip_group_check=True)
                for t in range(TPC):
                    done = nc.tensor.matmul(banks[7][:, 0:NE], ones_b,
                                            chosen[:, bass.ds(c * TPC + t, 1), :].rearrange("p n e -> p (n e)"),
                                            start=(t == 0), stop=(t == TPC - 1))
                done.then_inc(count_ready, 1)

            def step(c, b, j, last):
                pe.wait_ge(xT_ready, c + 1)
                for t in range(TPC):
                    pe.wait_ge(vr_free, c * 4 + t + 1)
                    for h in range(2):
                        done = nc.tensor.matmul(banks[4 + t % 2][:, 0:D + NE], xT[:, j, h, t * P:(t + 1) * P],
                                                wvr[:, h, :], start=(h == 0), stop=(h == 1))
                    done.then_inc(vr_ready, 1)
                for o in range(4):
                    if o == 2:
                        count(c)
                    if o == 2 and not last:
                        transposes(c + 1, 1 - j)
                    pe.wait_ge(rest_ready, c * 4 + o + 1)
                    for h in range(2):
                        done = nc.tensor.matmul(banks[2 + o % 2][:, :], wqk[:, h, o * P:(o + 1) * P],
                                                xT[:, j, h, :], start=(h == 0), stop=(h == 1))
                    done.then_inc(qk_ready, 1)

            pe.sem_inc(turned, 1)
            pe.sem_inc(count_read, 1)
            pe.wait_ge(consts_ready, 1)
            transposes(0, 0)
            pe.wait_ge(consts_ready, 6)
            pe.wait_ge(weights_in, 32)
            chunks(pe, step)
            count(NCH)


def end_routing(nc, dve, chain, keep, last_ready, slots_ready, meta_ready):
    consts, chosen, base, slot, blk, blk_i, junk, top8, cols, meta_c = keep["routing"]
    idx8, blk_table = keep["sbuf"][4], keep["fill"][1]
    chain.done(nc.vector.tensor_scalar(blk_i[:, :], base[:, NCH + 1, :], float(P - 1), None, ALU.add))
    chain.wait()
    chain.done(nc.vector.tensor_scalar(blk_i[:, :], blk_i[:, :], 7, None, ALU.logical_shift_right))
    chain.wait()
    nblk, ends, starts, some, one = (blk[:, k, :] for k in range(5))
    chain.done(nc.vector.tensor_copy(nblk, blk_i[:, :]))
    chain.done(nc.vector.memset(one, 1.0))
    chain.wait()
    chain.done(nc.vector.tensor_tensor_scan(ends, one, nblk, 0.0, ALU.mult, ALU.add))
    chain.done(nc.vector.tensor_scalar(some, nblk, 0.0, None, ALU.is_gt))
    chain.wait()
    chain.done(nc.vector.tensor_tensor(starts, ends, nblk, ALU.subtract))
    chain.done(nc.vector.tensor_scalar(blk_table[:, 0, :], ends, -1.0, 0.0, ALU.add, ALU.max))
    chain.done(nc.vector.tensor_copy(blk_table[:, 1, :], some))
    chain.wait()
    dve.sem_inc(last_ready, 1)
    chain.done(nc.vector.tensor_scalar(starts, starts, float(P), 1.0, ALU.mult, ALU.add))
    chain.wait()
    mine = slot[:, TPC:, :]
    chain.done(nc.vector.tensor_tensor(mine, mine, starts.unsqueeze(1).to_broadcast([P, NTILE, NE]), ALU.add))
    chain.wait()
    chain.done(nc.vector.tensor_tensor(mine, mine, chosen[:, TPC:, :], ALU.mult))
    chain.wait()
    for n in range(NTILE):
        chain.done(nc.vector.max(top8[:, n, :], slot[:, TPC + n, :]))
    chain.wait()
    nc.vector.tensor_scalar(idx8[:, :, :], top8[:, :, :], -1.0, None, ALU.add).then_inc(slots_ready, 1)
    for c in range(MB):
        for f, of, col in ((0, one, c), (1, some, c), (2, some, MB + c)):
            chain.done(nc.vector.scalar_tensor_tensor(
                junk[:, :], ends, consts[:, 6 * P + col:6 * P + col + 1], of, ALU.is_le, ALU.mult,
                accum_out=cols[:, f, c:c + 1]))
            chain.wait()
    chain.done(nc.vector.tensor_copy(meta_c[:, E_F, :], cols[:, 0, :]))
    chain.done(nc.vector.tensor_copy(meta_c[:, AT_F, :], cols[:, 1, :]))
    chain.done(nc.vector.tensor_scalar(cols[:, 4, :], cols[:, 0, :], float(NE), None, ALU.is_lt))
    chain.done(nc.vector.tensor_tensor(cols[:, 3, :], cols[:, 1, :], cols[:, 2, :], ALU.subtract))
    chain.wait()
    chain.done(nc.vector.memset(cols[0:1, 3, 0:1], 1.0))
    chain.done(nc.vector.tensor_scalar(meta_c[:, AT_F, :], meta_c[:, AT_F, :], WR - 1, None,
                                       ALU.bitwise_and))
    chain.done(nc.vector.tensor_scalar(cols[:, 0, :], cols[:, 0, :], float(NE - 1), None, ALU.min))
    chain.done(nc.vector.tensor_scalar(cols[:, 6, :], consts[:, 6 * P:6 * P + MB], float(-EMPTY), None,
                                       ALU.add))
    chain.wait()
    chain.done(nc.vector.tensor_tensor(cols[:, 3, :], cols[:, 3, :], cols[:, 4, :], ALU.mult))
    chain.done(nc.vector.tensor_tensor(cols[:, 6, :], cols[:, 6, :], cols[:, 4, :], ALU.mult))
    chain.done(nc.vector.tensor_copy(meta_c[:, E_F, :], cols[:, 0, :]))
    chain.done(nc.vector.tensor_scalar(cols[:, 5, :], meta_c[:, AT_F, :], float(1 << PLACE_BIT), None,
                                       ALU.mult))
    chain.wait()
    chain.done(nc.vector.tensor_scalar(meta_c[:, SRC_F, :], cols[:, 6, :], float(EMPTY), None, ALU.add))
    chain.done(nc.vector.tensor_scalar(meta_c[:, AT_F, :], meta_c[:, AT_F, :], WCOLS, None, ALU.mult))
    chain.done(nc.vector.scalar_tensor_tensor(cols[:, 3, :], cols[:, 3, :], float(1 << NEW_BIT),
                                              cols[:, 0, :], ALU.mult, ALU.add))
    chain.wait()
    chain.done(nc.vector.tensor_tensor(meta_c[:, LOAD_F, :], cols[:, 3, :], cols[:, 5, :], ALU.add))
    chain.wait()
    dve.sem_inc(meta_ready, 1)


def attend(nc, ctx, keep, onorm, x, w_proj, res, wp, m_in):
    qk_d, rows_d, slots_d, meta_d, acc_d = keep["dram"]
    ident, cb, v_sb, meta, idx8, zeros, banks = keep["sbuf"]
    template, blk_table = keep["fill"]
    ident_b, mask_prev, mask_next = (cb[:, k * P:(k + 1) * P] for k in (0, 3, 4))

    def sb(name, shape, dt=F32):
        return ctx.enter_context(nc.sbuf_tensor(name, shape, dt))

    def sem(name):
        return ctx.enter_context(nc.semaphore(name))

    def sems(name, n):
        return [sem(f"{name}{i}") for i in range(n)]

    RR = 4
    qk = sb("qk", [KM, HG, 2, T], BF16)
    qT, kT = qk[:, :, 0, :], qk[:, :, 1, :]
    va = sb("va", [P, HG, TT, 32])
    mask_q = sb("mask_q", [P, 3 * P])
    masked = sb("masked", [P, 2, 3 * P])
    nmax = sb("nmax", [P, HG, TT])
    nmax_b = sb("nmax_b", [P, HG, 2, TT], BF16)
    nmaxT = sb("nmaxT", [2 * TT, HG, P], BF16)
    pT = sb("pT", [P, 4, 3 * P])
    oT = sb("oT", [P, T])
    rec = sb("rec", [P, TT // 2, HG])
    row_ring = sb("row_ring", [P, RR, ROW])
    idx_ring = sb("idx_ring", [P, RR, K], I32)

    S1, S2, OB = 0, 3, 5
    misc = banks[7]
    misc_b = misc.bitcast(BF16)
    both_o = keep["psum"][:, OB:OB + 2, :]

    va_const, va_ready = sem("va_const"), sem("va_ready")
    qk_in, nrow_in = sems("qk_in", HG), sems("nrow_in", HG)
    s1_ready, s1_free = sem("s1_ready"), sem("s1_free")
    hi_done, nmax_ready, misc_ready, misc_free, rec_ready = (
        sem("hi_done"), sem("nmax_ready"), sem("misc_ready"), sem("misc_free"), sem("rec_ready"))
    s2_ready, p_ready, pv_done, o_read = sem("s2_ready"), sem("p_ready"), sem("pv_done"), sem("o_read")
    rows_in, scattered = sems("rows_in", RR), sems("scattered", RR)
    dve_tick, mask_ready, dve_r = sem("dve_tick"), sem("mask_ready"), sem("dve_r")
    last_ready, slots_ready, meta_ready, meta_out, meta_in = (
        sem("last_ready"), sem("slots_ready"), sem("meta_ready"), sem("meta_out"), sem("meta_in"))
    idx_ready, pool_tick, cleared = sem("idx_ready"), sem("pool_tick"), sem("cleared")
    empty_written, ends_filled = sem("empty_written"), sem("ends_filled")

    def is_first(g):
        return isinstance(g, int) and g == 0

    def maxima_write(g, hh):
        return 1 + hh if is_first(g) else g * 6 - 1 + (0, 2, 4, 5)[hh]

    def outputs_write(g, half):
        return g * 6 - 1 + (1, 3)[half]

    def window(i):
        return max(i - 1, 0), min(i + 2, TT)

    with nc.Block() as block:
        @block.sync
        def _(sp):
            def load(u, hh):
                sp.dma_start(qk[0:KS, hh, :, :].rearrange("p s t -> p (s t)"),
                             qk_d[:, bass.ds(u * DK, DK), :, :].rearrange("n d s t -> n d (s t)")
                             ).then_inc(qk_in[hh], 16)

            def maxima(hh, write):
                sp.wait_ge(misc_free, write + 1)
                sp.dma_start(qT[KS:KM, hh, :].rearrange("s (t q) -> s t q", t=TT), nmaxT[:, hh, :]
                             ).then_inc(nrow_in[hh], 16)

            def clear(g, k):
                sp.dma_start(acc_d[k][bass.ds(g * (NTOK // NG), NTOK // NG), :].rearrange("(p n) c -> p (n c)", p=P),
                             zeros[:, 0:NTOK // NG * D // P]).then_inc(cleared, 16)

            def group(g, last):
                for hh in range(HG):
                    if not (last and hh > 0):
                        if not is_first(g) or hh > 0:
                            sp.wait_ge(s2_ready, g * (HG * TT) + hh * TT)
                        load(g * HG + hh + 3, (hh + 3) % HG)
                    if not (last and hh == HG - 1):
                        maxima((hh + 1) % HG, maxima_write(g, hh))
                    clear(g, hh)
                    if last:
                        n = NTILE // HG
                        sp.dma_start(res[:, hh * n:(hh + 1) * n, :],
                                     x[hh * n:(hh + 1) * n, :, :].rearrange("n p c -> p n c")).then_inc(m_in, 16)

            for hh in range(3):
                load(hh, hh)
            sp.dma_start(slots_d[EMPTY * P:(EMPTY + 1) * P, :], template[:, :]).then_inc(empty_written, 16)
            maxima(0, 0)
            group(0, False)
            group(1, False)
            sp.wait_ge(meta_ready, 1)
            sp.dma_start(meta_d.rearrange("f (c p) -> p f c", p=P), keep["routing"][9][:, :, :],
                         allow_slow_non_contiguous=True).then_inc(meta_out, 16)
            with sp.Fori(2, NG - 1) as g:
                group(g, False)
            sp.wait_ge(meta_out, 16)
            sp.dma_start(meta[:, :, :], meta_d.unsqueeze(0)).then_inc(meta_in, 16)
            sp.dma_start(wp[:, :, :], w_proj).then_inc(m_in, 16)
            group(NG - 1, True)
            for k in range(NACC):
                sp.dma_start(acc_d[k][NTOK:NTOK + P, :], zeros[:, 0:D]).then_inc(cleared, 16)
            sp.wait_ge(cleared, 16 * (NG + 1) * NACC)
            sp.wait_ge(meta_in, 16)

        @block.tensor
        def _(pe):

            def masks(bank, i, n):
                if i > 0:
                    last = nc.tensor.matmul(banks[bank][:, 0:P], ident_b, mask_prev, start=False,
                                            stop=(i == TT - 1), skip_group_check=True)
                if i < TT - 1:
                    last = nc.tensor.matmul(banks[bank][:, n - P:n], ident_b, mask_next, start=False, stop=True,
                                            skip_group_check=True)
                return last

            def scores_q(g, ahead, i):
                hh, n = ahead % HG, ahead * TT + i
                lo, hi = window(i)
                back = {0: 2, 1: 2, 2: 5}.get(i, 3)
                if not is_first(g) or n >= back:
                    pe.wait_ge(s1_free, g * (HG * TT) + (n - back + 1))
                nc.tensor.matmul(banks[S1 + i % 3][:, 0:(hi - lo) * P], qT[0:KS, hh, i * P:(i + 1) * P],
                                 kT[0:KS, hh, lo * P:hi * P], start=True, stop=True).then_inc(s1_ready, 1)

            def scores_k(g, hh, j):
                lo, hi = window(j)
                if not is_first(g) or hh > 0 or j > 1:
                    pe.wait_ge(p_ready, g * (HG * TT) + (hh * TT + j - 1))
                nc.tensor.matmul(banks[S2 + j % 2][:, 0:(hi - lo) * P], kT[0:KM, hh, j * P:(j + 1) * P],
                                 qT[0:KM, hh, lo * P:hi * P], start=True, stop=False, skip_group_check=True)
                masks(S2 + j % 2, j, (hi - lo) * P).then_inc(s2_ready, 1)

            def values(g, n):
                hh, j = n // TT % HG, n % TT
                lo, hi = window(j)
                pe.wait_ge(p_ready, g * (HG * TT) + (n + 1))
                for bank in range(2):
                    a, b = max(lo, 4 * bank), min(hi, 4 * bank + 4)
                    if a < b:
                        last = nc.tensor.matmul(
                            banks[OB + bank][32 * hh:32 * hh + 32, (a - 4 * bank) * P:(b - 4 * bank) * P],
                            va[:, hh, j, :], pT[:, j % 4, (a - lo) * P:(b - lo) * P],
                            start=(j == (0, 3)[bank]), stop=(j == (4, 7)[bank]), skip_group_check=True)
                last.then_inc(pv_done, 1)

            def turn_maxima(g, ahead, write):
                pe.wait_ge(nmax_ready, g * HG + (ahead + 1))
                if not (isinstance(write, int) and write == 0):
                    pe.wait_ge(misc_free, write)
                nc.tensor.transpose(misc_b[0:2 * TT, 0:P],
                                    nmax_b[:, ahead % HG, :, :].rearrange("p s t -> p (s t)"),
                                    ident_b).then_inc(misc_ready, 1)

            def turn_outputs(g, half):
                pe.wait_ge(o_read, g)
                pe.wait_ge(misc_free, outputs_write(g, half))
                for t in range(4):
                    last = nc.tensor.transpose(misc[:, t * P:(t + 1) * P],
                                               oT[:, (4 * half + t) * P:(4 * half + t + 1) * P], ident[:, :])
                last.then_inc(misc_ready, 1)

            def group(g, last):
                for hh in range(HG):
                    pe.wait_ge(va_ready, g * HG + (hh + 1))
                    pe.wait_ge(nrow_in[hh], g * 16 + 16)
                    for j in range(TT):
                        scores_k(g, hh, j)
                        if j == 1 and not (last and hh == HG - 1):
                            turn_maxima(g, hh + 1, maxima_write(g, hh))
                        if j == 2 and hh == 0 and not is_first(g):
                            pe.wait_ge(o_read, g)
                        if hh * TT + j > 1 or not is_first(g):
                            values(g, hh * TT + j - 2)
                        if not (last and hh > 1):
                            if j == 0:
                                pe.wait_ge(qk_in[(hh + 2) % HG], g * 16 + (16 if hh < 2 else 32))
                            scores_q(g, hh + 2, j)
                        if j == 4 and hh < 2 and not is_first(g):
                            turn_outputs(g, hh)

            for hh in range(2):
                pe.wait_ge(qk_in[hh], 16)
                for i in range(TT):
                    scores_q(0, hh, i)
            pe.wait_ge(va_const, 3)
            turn_maxima(0, 0, 0)
            group(0, False)
            with pe.Fori(1, NG - 1) as g:
                group(g, False)
            group(NG - 1, True)
            for n in range(HG * TT - 2, HG * TT):
                values(NG - 1, n)
            for half in range(2):
                pe.wait_ge(o_read, NG)
                pe.wait_ge(misc_free, NG * 6 - 2 + half)
                for t in range(4):
                    last = nc.tensor.transpose(misc[:, t * P:(t + 1) * P],
                                               oT[:, (4 * half + t) * P:(4 * half + t + 1) * P], ident[:, :])
                last.then_inc(misc_ready, 1)

        @block.scalar
        def _(act):
            def group(g, last):
                for hh in range(HG):
                    for j in range(TT):
                        lo, hi = window(j)
                        n = hh * TT + j
                        if not is_first(g) or n > 3:
                            act.wait_ge(pv_done, g * (HG * TT) + (n - 3))
                        act.wait_ge(s2_ready, g * (HG * TT) + (n + 1))
                        nc.scalar.activation(pT[:, j % 4, 0:(hi - lo) * P], banks[S2 + j % 2][:, 0:(hi - lo) * P],
                                             ACT.Exp).then_inc(p_ready, 1)
                        if n == 1 and not is_first(g):
                            copy_outputs(g)

            def copy_outputs(g):
                act.wait_ge(pv_done, g * (HG * TT))
                nc.scalar.copy(oT.rearrange("p (b q) -> p b q", b=2), both_o).then_inc(o_read, 1)

            group(0, False)
            with act.Fori(1, NG - 1) as g:
                group(g, False)
            group(NG - 1, True)
            copy_outputs(NG)

        @block.vector
        def _(dve):
            nc.vector.memset(va[:, :, :, DK + 1:32], 0.0).then_inc(va_const, 1)
            nc.vector.memset(va[:, :, :, DK:DK + 1], 1.0).then_inc(va_const, 1)
            nc.vector.tensor_copy(mask_q[:, 0:P], mask_prev).then_inc(mask_ready, 1)
            nc.vector.memset(mask_q[:, P:2 * P], 0.0).then_inc(mask_ready, 1)
            nc.vector.tensor_copy(mask_q[:, 2 * P:3 * P], mask_next).then_inc(mask_ready, 1)
            dve.wait_ge(mask_ready, 3)

            def maxima(g, ahead, i):
                hh = ahead % HG
                lo, hi = window(i)
                dve.wait_ge(s1_ready, g * (HG * TT) + (ahead * TT + i + 1))
                if not is_first(g) or ahead * TT + i > 1:
                    dve.wait_ge(s1_free, g * (HG * TT) + (ahead * TT + i - 1))
                dve.sem_inc(dve_tick, 1)
                side = 0 if i > 0 else P
                nc.vector.tensor_tensor_reduce(masked[:, i % 2, 0:(hi - lo) * P], banks[S1 + i % 3][:, 0:(hi - lo) * P],
                                               mask_q[:, side:side + (hi - lo) * P], -1.0, -NEG, ALU.add, ALU.min,
                                               accum_out=nmax[:, hh, i:i + 1]).then_inc(s1_free, 1)

            def split_maxima(g, ahead):
                hh = ahead % HG
                dve.wait_ge(s1_free, g * (HG * TT) + (ahead * TT + TT))
                nc.vector.tensor_copy(nmax_b[:, hh, 0, :], nmax[:, hh, :]).then_inc(hi_done, 1)
                dve.wait_ge(hi_done, g * HG + (ahead + 1))
                nc.vector.tensor_tensor(nmax_b[:, hh, 1, :], nmax[:, hh, :], nmax_b[:, hh, 0, :],
                                        ALU.subtract).then_inc(nmax_ready, 1)

            def copy_maxima(hh, write):
                dve.wait_ge(misc_ready, write + 1)
                nc.vector.tensor_copy(nmaxT[:, hh, :], misc_b[0:2 * TT, 0:P]).then_inc(misc_free, 1)

            def copy_values(g, ahead):
                nc.vector.tensor_copy(va[:, ahead % HG, :, 0:DK],
                                      v_sb[:, bass.ds(g * HG + ahead, 1), :, :].rearrange("p o t d -> p (o t) d")
                                      ).then_inc(va_ready, 1)

            def normalise(g, half, write, done):
                dve.wait_ge(misc_ready, write + 1)
                o = misc.rearrange("p (t h c) -> p t h c", t=TT // 2, h=HG)
                nc.vector.reciprocal(rec[:, :, :], o[:, :, :, DK]).then_inc(rec_ready, 1)
                dve.wait_ge(rec_ready, done)
                dst = onorm[:, bass.ds(g * TT + half * (TT // 2), TT // 2), :]
                nc.vector.tensor_tensor(dst.rearrange("p t (h d) -> p t h d", h=HG), o[:, :, :, 0:DK],
                                        rec[:, :, :].unsqueeze(3).to_broadcast([P, TT // 2, HG, DK]),
                                        ALU.mult).then_inc(misc_free, 1)

            def group(g, last):
                for hh in range(HG):
                    if not (last and hh == HG - 1):
                        if not is_first(g) or hh == 3:
                            dve.wait_ge(pv_done, g * (HG * TT) + (hh - 2) * TT)
                        copy_values(g, hh + 1)
                    for i in range(TT):
                        if i == 1 and not (last and hh == HG - 1):
                            copy_maxima((hh + 1) % HG, maxima_write(g, hh))
                        if not (last and hh > 1):
                            maxima(g, hh + 2, i)
                        if i == 4 and hh < 2 and not is_first(g):
                            normalise(g - 1, hh, outputs_write(g, hh), g * 2 - 1 + hh)
                    if not (last and hh > 1):
                        split_maxima(g, hh + 2)

            copy_values(0, 0)
            for hh in range(2):
                for i in range(TT):
                    maxima(0, hh, i)
                split_maxima(0, hh)
            copy_maxima(0, 0)
            end_routing(nc, dve, Chain(dve, dve_r), keep, last_ready, slots_ready, meta_ready)
            group(0, False)
            with dve.Fori(1, NG - 1) as g:
                group(g, False)
            group(NG - 1, True)
            for half in range(2):
                normalise(NG - 1, half, NG * 6 - 2 + half, NG * 2 - 1 + half)

        @block.gpsimd
        def _(pool):
            def fill(i):
                last_regs, any_regs = ([pool.alloc_register(f"{name}{8 * i + k}") for k in range(8)]
                                       for name in ("last_block", "any_block"))
                pool.load(last_regs, blk_table[0:1, 0, 8 * i:8 * i + 8])
                pool.load(any_regs, blk_table[0:1, 1, 8 * i:8 * i + 8])
                for k in range(8):
                    at = bass.RuntimeValue.of_register_unchecked(last_regs[k], min_val=0, max_val=NB_ROUTED - 1)
                    some = bass.RuntimeValue.of_register_unchecked(any_regs[k], min_val=0, max_val=1)
                    pool.dma_start(slots_d[bass.ds(at * P, P), :], template[:, :], cond=some).then_inc(ends_filled, 16)

            def load(i, j):
                if not is_first(i) or j >= RR:
                    pool.wait_ge(scattered[j % RR], i * (16 * K) + (16 * K) * (j // RR))
                    pool.sem_inc(pool_tick, 1)
                pool.dma_start(row_ring[:, j % RR, :], rows_d[bass.ds(i * (RR * P) + j * P, P), :]
                               ).then_inc(rows_in[j % RR], 16)

            def scatter(i, j):
                pool.wait_ge(rows_in[j], i * 16 + 16)
                pool.sem_inc(pool_tick, 1)
                nc.gpsimd.tensor_copy(idx_ring[:, j, :].unsqueeze(1), idx8[:, bass.ds(i * RR + j, 1), :]
                                      ).then_inc(idx_ready, 1)
                pool.wait_ge(idx_ready, i * RR + (j + 1))
                pool.sem_inc(pool_tick, 1)
                for k in range(K):
                    nc.gpsimd.indirect_dma_start(
                        out=slots_d, out_offset=bass.IndirectOffsetOnAxis(ap=idx_ring[:, j, k:k + 1], axis=0),
                        in_=row_ring[:, j, :], in_offset=None).then_inc(scattered[j], 16)

            def step(i, last):
                for j in range(RR):
                    if not last or j + 2 < RR:
                        load(i, j + 2)
                    scatter(i, j)

            nc.gpsimd.memset(kT[KS:KM, :, :], 1.0).then_inc(va_const, 1)
            for j in range(2):
                load(0, j)
            pool.wait_ge(last_ready, 1)
            for i in range(NE // 8):
                fill(i)
            pool.wait_ge(slots_ready, 1)
            pool.wait_ge(empty_written, 16)
            pool.wait_ge(ends_filled, 16 * NE)
            step(0, False)
            with pool.Fori(1, NTILE // RR - 1) as i:
                step(i, False)
            step(NTILE // RR - 1, True)
            for j in range(RR):
                pool.wait_ge(scattered[j], 16 * K * (NTILE // RR))


def merge(nc, ctx, keep, onorm, res, wp, m_in, loads):
    ident, banks = keep["sbuf"][0], keep["sbuf"][6]

    def sb(name, shape, dt=F32):
        return ctx.enter_context(nc.sbuf_tensor(name, shape, dt))

    def sem(name):
        return ctx.enter_context(nc.semaphore(name))

    stage = sb("stage", [P, 2, D])
    oT2 = sb("oT2", [P, 2, 2, P])
    stage_ready, turned, turned_read, proj_ready, proj_read = (
        sem("stage_ready"), sem("turned"), sem("turned_read"), sem("proj_ready"), sem("proj_read"))

    tick = sem("merge_tick")

    with nc.Block() as block:
        @block.sync
        def _(sp):
            loads["half"](sp, 0, 0)

        @block.gpsimd
        def _(pool):
            pool.sem_inc(turned, 2)
            with pool.Fori(0, B) as b:
                for t in range(TT):
                    pool.wait_ge(turned, b * TT + t + 1)
                    pool.sem_inc(tick, 1)
                    src = onorm[:, bass.ds(b * (4 * TT), 4 * TT), :].rearrange("p (g t) c -> p g t c", g=4)[:, :, t, :]
                    nc.gpsimd.tensor_copy(stage[:, t % 2, :].rearrange("p (g c) -> p g c", g=4), src
                                          ).then_inc(stage_ready, 1)

        @block.tensor
        def _(pe):
            def turn(b, t):
                pe.wait_ge(turned_read, b * TT + t)
                pe.wait_ge(stage_ready, b * TT + t + 1)
                for h in range(2):
                    last = nc.tensor.transpose(banks[t % 2][:, h * P:(h + 1) * P],
                                               stage[:, t % 2, h * P:(h + 1) * P], ident[:, :])
                last.then_inc(turned, 1)

            def batch(b, last_batch):
                for t in range(TT):
                    n = b * TT + t
                    if not (last_batch and t == TT - 1):
                        turn(b, t + 1)
                    pe.wait_ge(turned_read, n + 2)
                    pe.wait_ge(proj_read, n + 1)
                    for h in range(2):
                        last = nc.tensor.matmul(banks[2 + t % 2][:, 0:D], oT2[:, t % 2, h, :], wp[:, h, :],
                                                start=(h == 0), stop=(h == 1))
                    last.then_inc(proj_ready, 1)

            pe.sem_inc(turned_read, 1)
            pe.wait_ge(m_in, 16 * (1 + HG))
            pe.wait_ge(stage_ready, 1)
            for h in range(2):
                last = nc.tensor.transpose(banks[0][:, h * P:(h + 1) * P], stage[:, 0, h * P:(h + 1) * P], ident[:, :])
            last.then_inc(turned, 1)
            with pe.Fori(0, B - 1) as b:
                batch(b, False)
            batch(B - 1, True)

        @block.scalar
        def _(act):
            act.sem_inc(proj_ready, 2)
            with act.Fori(0, B) as b:
                for t in range(TT):
                    act.wait_ge(turned, b * TT + t + 3)
                    act.wait_ge(proj_ready, b * TT + t + 1)
                    nc.scalar.copy(oT2[:, t % 2, :, :].rearrange("p h q -> p (h q)"), banks[t % 2][:, 0:D]
                                   ).then_inc(turned_read, 1)

        @block.vector
        def _(dve):
            dve.sem_inc(proj_read, 2)
            dve.wait_ge(m_in, 16 * (1 + HG))
            with dve.Fori(0, B) as b:
                for t in range(TT):
                    dve.wait_ge(proj_ready, b * TT + t + 3)
                    r = res[:, bass.ds(b * TT + t, 1), :].rearrange("p o c -> p (o c)")
                    nc.vector.tensor_tensor(r, banks[2 + t % 2][:, 0:D], r, ALU.add).then_inc(proj_read, 1)


def expert_loads(nc, ctx, keep, w_exp):
    slots_d, meta = keep["dram"][2], keep["sbuf"][3]
    xb = ctx.enter_context(nc.sbuf_tensor("xb", [P, XR, ROW], F32))
    wb = ctx.enter_context(nc.sbuf_tensor("wb", [P, WR * WCOLS], F32))
    x_in = [ctx.enter_context(nc.semaphore(f"xb_in{i}")) for i in range(XR)]
    w_in = [ctx.enter_context(nc.semaphore(f"wb_in{i}")) for i in range(WR)]
    acc_free, y_ready = ctx.enter_context(nc.semaphore("acc_free")), ctx.enter_context(nc.semaphore("y_ready"))
    number = count()

    def fields(engine, n, i, r, f, most):
        regs = [engine.alloc_register(f"field{f}_{next(number)}") for k in range(n)]
        engine.load(regs, meta[0:1, f, bass.ds(i * XR + r, n)])
        return [bass.RuntimeValue.of_register_unchecked(reg, min_val=0, max_val=most) for reg in regs]

    def half(sp, i, h):
        first = isinstance(i, int) and i == 0
        src = fields(sp, 8, i, 8 * h, SRC_F, EMPTY)
        load = fields(sp, 8, i, 8 * h, LOAD_F, (WR << PLACE_BIT) - 1)
        for k in range(8):
            r = 8 * h + k
            if not first:
                sp.wait_ge(acc_free, i * XR + (r - XR + NACC + 1))
            sp.dma_start(xb[:, r, :], slots_d[bass.ds(src[k] * P, P), :]).then_inc(x_in[r], 16)
            if not first or r >= WR:
                sp.wait_ge(y_ready, i * XR + (r - WR + 1))
            expert = (load[k] & ((1 << NEW_BIT) - 1)).with_bounds(min_val=0, max_val=NE - 1)
            place = (load[k] >> PLACE_BIT).with_bounds(min_val=0, max_val=WR - 1)
            sp.dma_start(wb[:, bass.ds(place * WCOLS, WCOLS)],
                         w_exp[bass.ds(expert, 1), :, :].rearrange("e p n -> p (e n)"),
                         cond=(load[k] >> NEW_BIT) & 1).then_inc(w_in[r % WR], 16)

    return {"xb": xb, "wb": wb, "x_in": x_in, "w_in": w_in, "acc_free": acc_free, "y_ready": y_ready,
            "fields": fields, "half": half}


def experts(nc, ctx, keep, loads, w_exp):
    rows_d, acc_d = keep["dram"][1], keep["dram"][4]
    ident, v_sb, banks = (keep["sbuf"][k] for k in (0, 2, 6))

    def sb(name, shape, dt=F32):
        return ctx.enter_context(nc.sbuf_tensor(name, shape, dt))

    def sem(name):
        return ctx.enter_context(nc.semaphore(name))

    def sems(name, n):
        return [sem(f"{name}{i}") for i in range(n)]

    xb, wb, x_in, w_in, acc_free, y_ready, fields = (
        loads[name] for name in ("xb", "wb", "x_in", "w_in", "acc_free", "y_ready", "fields"))
    w_sh, shared_in = keep["shared"]
    x_all = v_sb.rearrange("p u t d -> p (u t d)").rearrange("p (n c) -> p n c", c=D)
    xT = sb("xTe", [P, 2, 2, P])
    gate = sb("gate", [P, 2, I])
    a_sb = sb("a_sb", [P, 2, I])
    aT = sb("aT", [P, 2, P])
    ys = sb("ys", [P, NACC, D])

    added = sems("added", NACC)
    px_ready, xT_ready, gu_ready, gate_ready, act_ready = (
        sem("px_ready"), sem("xTe_ready"), sem("gu_ready"), sem("gate_ready"), sem("act_ready"))
    pa_ready, aT_ready, ys_ready, tick = sem("pa_ready"), sem("aT_ready"), sem("ys_ready"), sem("tick")
    PX, GU, PA, Y = 0, 2, 4, 6
    LAST = NB_ROUTED // XR - 1
    assert NB_ROUTED % XR == 0 and LAST > 1

    def first(i):
        return isinstance(i, int) and i == 0

    def exists(i, r):
        return not (isinstance(i, int) and i == LAST) or r < XR

    def every(engine, step):
        step(0)
        with engine.Fori(1, LAST) as i:
            step(i)
        step(LAST)

    with nc.Block() as block:
        @block.sync
        def _(sp):
            def load_shared(part):
                n = NTILE // 4
                sp.dma_start(x_all[:, part * n:(part + 1) * n, :],
                             rows_d[part * n * P:(part + 1) * n * P, 0:D].rearrange("(n p) c -> p n c", p=P)
                             ).then_inc(shared_in, 16)

            def step(i):
                for h in range(XR // 8):
                    if not first(i) or h > 0:
                        loads["half"](sp, i, h)
                    if isinstance(i, int):
                        load_shared((2 if i == LAST else 0) + h)

            sp.dma_start(w_sh[:, :], w_exp[NE, :, :]).then_inc(shared_in, 16)
            every(sp, step)
            sp.wait_ge(shared_in, 16 * 5)

        @block.tensor
        def _(pe):
            def turn_x(i, r):
                pe.wait_ge(x_in[r % XR], i * 16 + 16 * (r // XR + 1))
                if not first(i) or r > 1:
                    pe.wait_ge(xT_ready, i * XR + (r - 1))
                for h in range(2):
                    last = nc.tensor.transpose(banks[PX + r % 2][:, h * P:(h + 1) * P],
                                               xb[:, r % XR, h * P:(h + 1) * P], ident[:, :])
                last.then_inc(px_ready, 1)

            def gate_up(i, r, at):
                pe.wait_ge(w_in[r % WR], i * (16 * XR // WR) + 16 * (r // WR + 1))
                pe.wait_ge(xT_ready, i * XR + r + 1)
                for h in range(2):
                    last = nc.tensor.matmul(banks[GU + r % 2][:, 0:2 * I], xT[:, r % 2, h, :],
                                            wb[:, bass.ds(at + h * 2 * I, 2 * I)],
                                            start=(h == 0), stop=(h == 1))
                last.then_inc(gu_ready, 1)

            def turn_a(i, r):
                pe.wait_ge(act_ready, i * XR + r + 1)
                nc.tensor.transpose(banks[PA + r % 2][:, 0:P], a_sb[:, r % 2, :], ident[:, :]).then_inc(pa_ready, 1)

            def down(i, r, at):
                if not first(i) or r > 1:
                    pe.wait_ge(ys_ready, i * XR + (r - 1))
                pe.wait_ge(aT_ready, i * XR + r + 1)
                nc.tensor.matmul(banks[Y + r % 2][:, 0:D], aT[:, r % 2, :], wb[:, bass.ds(at + 4 * I, D)],
                                 start=True, stop=True).then_inc(y_ready, 1)

            def step(i):
                for r in range(XR):
                    k = r % 8
                    if k == 0:
                        at = fields(pe, 10 if exists(i, r + 9) else 8, i, r, AT_F, (WR - 1) * WCOLS)
                    if exists(i, r + 3):
                        turn_x(i, r + 3)
                    if exists(i, r + 2):
                        gate_up(i, r + 2, at[k + 2])
                    if exists(i, r + 1):
                        turn_a(i, r + 1)
                    down(i, r, at[k])

            at = fields(pe, 2, 0, 0, AT_F, (WR - 1) * WCOLS)
            turn_x(0, 0)
            turn_x(0, 1)
            gate_up(0, 0, at[0])
            turn_x(0, 2)
            gate_up(0, 1, at[1])
            turn_a(0, 0)
            every(pe, step)

        @block.scalar
        def _(act):
            def copy_x(i, r):
                if not first(i) or r > 1:
                    act.wait_ge(gu_ready, i * XR + (r - 1))
                act.wait_ge(px_ready, i * XR + r + 1)
                nc.scalar.copy(xT[:, r % 2, :, :].rearrange("p h q -> p (h q)"), banks[PX + r % 2][:, 0:D]
                               ).then_inc(xT_ready, 1)

            def silu(i, r):
                if not first(i) or r > 1:
                    act.wait_ge(act_ready, i * XR + (r - 1))
                act.wait_ge(gu_ready, i * XR + r + 1)
                nc.scalar.activation(gate[:, r % 2, :], banks[GU + r % 2][:, 0:I], ACT.Silu).then_inc(gate_ready, 1)

            def step(i):
                for r in range(XR):
                    if exists(i, r + 3):
                        copy_x(i, r + 3)
                    if exists(i, r + 2):
                        silu(i, r + 2)

            copy_x(0, 0)
            copy_x(0, 1)
            silu(0, 0)
            copy_x(0, 2)
            silu(0, 1)
            every(act, step)

        @block.vector
        def _(dve):
            def product(i, r, e):
                dve.wait_ge(gate_ready, i * XR + r + 1)
                if not first(i) or r > 1:
                    dve.wait_ge(pa_ready, i * XR + (r - 1))
                nc.vector.scalar_tensor_tensor(a_sb[:, r % 2, :], gate[:, r % 2, :],
                                               xb[:, r % XR, bass.ds(e + W_COL, 1)],
                                               banks[GU + r % 2][:, I:2 * I], ALU.mult, ALU.mult
                                               ).then_inc(act_ready, 1)

            def copy_a(i, r):
                if not first(i) or r > 1:
                    dve.wait_ge(y_ready, i * XR + (r - 1))
                dve.wait_ge(pa_ready, i * XR + r + 1)
                nc.vector.tensor_copy(aT[:, r % 2, :], banks[PA + r % 2][:, 0:P]).then_inc(aT_ready, 1)

            def step(i):
                for r in range(XR):
                    k = r % 8
                    if k == 0:
                        e = fields(dve, 10 if exists(i, r + 9) else 8, i, r, E_F, NE - 1)
                    if exists(i, r + 1):
                        copy_a(i, r + 1)
                    if exists(i, r + 2):
                        product(i, r + 2, e[k + 2])
                    dve.wait_ge(acc_free, i * XR + r + 1)
                    dve.wait_ge(y_ready, i * XR + r + 1)
                    nc.vector.tensor_copy(ys[:, r % NACC, :], banks[Y + r % 2][:, 0:D]).then_inc(ys_ready, 1)

            e = fields(dve, 2, 0, 0, E_F, NE - 1)
            product(0, 0, e[0])
            product(0, 1, e[1])
            copy_a(0, 0)
            every(dve, step)

        @block.gpsimd
        def _(pool):
            def step(i):
                for r in range(XR):
                    if not first(i) or r >= NACC:
                        pool.wait_ge(added[r % NACC], i * (16 * XR // NACC) + 16 * (r // NACC))
                    pool.sem_inc(acc_free, 1)
                    pool.wait_ge(ys_ready, i * XR + r + 1)
                    pool.sem_inc(tick, 1)
                    nc.gpsimd.indirect_dma_start(
                        out=acc_d[r % NACC],
                        out_offset=bass.IndirectOffsetOnAxis(ap=xb[:, r, ID_COL:ROW].bitcast(I32), axis=0),
                        in_=ys[:, r % NACC, :], in_offset=None, compute_op=ALU.add).then_inc(added[r % NACC], 16)

            every(pool, step)
            for r in range(NACC):
                pool.wait_ge(added[r], 16 * (NB_ROUTED // NACC))


def finish(nc, ctx, keep, res, out):
    acc_d = keep["dram"][4]
    ident, banks = keep["sbuf"][0], keep["sbuf"][6]

    def sb(name, shape, dt=F32):
        return ctx.enter_context(nc.sbuf_tensor(name, shape, dt))

    def sem(name):
        return ctx.enter_context(nc.semaphore(name))

    def sems(name, n):
        return [sem(f"{name}{i}") for i in range(n)]

    S = 8
    NQ = NTILE // S
    w_sh, shared_in = keep["shared"]
    x_all = keep["sbuf"][2].rearrange("p u t d -> p (u t d)").rearrange("p (n c) -> p n c", c=D)
    xp = sb("xp", [P, 2, 2, D])
    acc = sb("acc", [P, S // 2, NACC, 2, D])
    xT = sb("xT_s", [P, 2, 2, P])
    gate = sb("gate_s", [P, 2, I])
    a_sb = sb("a_s", [P, 2, I])
    aT = sb("aT_s", [P, 2, P])

    x_placed, acc_in = sem("x_placed"), sems("acc_in", S // 2)
    px_ready, xT_ready, gu_ready, gate_ready, act_ready = (
        sem("px_s_ready"), sem("xT_s_ready"), sem("gu_s_ready"), sem("gate_s_ready"), sem("act_s_ready"))
    pa_ready, aT_ready, y_ready, y_added = (
        sem("pa_s_ready"), sem("aT_s_ready"), sem("y_s_ready"), sem("y_added"))
    half_a, half_b, both, sum_ready, stored = (
        sem("half_a"), sem("half_b"), sem("both"), sem("sum_ready"), sem("stored"))
    PX, GU, PA, Y = 0, 2, 4, 6

    def first(q):
        return isinstance(q, int) and q == 0

    def exists(q, t):
        return (t >= 0 or not first(q)) and (t < S or not (isinstance(q, int) and q == NQ - 1))

    def every(engine, step):
        step(0)
        with engine.Fori(1, NQ - 1) as q:
            step(q)
        step(NQ - 1)

    with nc.Block() as block:
        @block.sync
        def _(sp):
            def load(q, j):
                for k in range(NACC):
                    sp.dma_start(acc[:, j, k, :, :], acc_d[k][bass.ds(q * (S * P) + j * (2 * P), 2 * P), :]
                                 .rearrange("(n p) c -> p n c", p=P)).then_inc(acc_in[j], 16)

            for j in range(S // 2):
                load(0, j)
            with sp.Fori(1, NQ) as q:
                for j in range(S // 2):
                    sp.wait_ge(sum_ready, q * (S // 2) + (j - S // 2 + 1))
                    load(q, j)

        @block.tensor
        def _(pe):
            def turn_x(q, t):
                pe.wait_ge(x_placed, q * (S // 2) + (t // 2 + 1))
                if not first(q) or t > 1:
                    pe.wait_ge(xT_ready, q * S + (t - 1))
                for h in range(2):
                    last = nc.tensor.transpose(banks[PX + t % 2][:, h * P:(h + 1) * P],
                                               xp[:, t // 2 % 2, t % 2, h * P:(h + 1) * P], ident[:, :])
                last.then_inc(px_ready, 1)

            def gate_up(q, t):
                pe.wait_ge(xT_ready, q * S + t + 1)
                if not first(q) or t > 1:
                    pe.wait_ge(act_ready, q * S + (t - 1))
                for h in range(2):
                    last = nc.tensor.matmul(banks[GU + t % 2][:, 0:2 * I], xT[:, t % 2, h, :],
                                            w_sh[:, h * 2 * I:(h + 1) * 2 * I], start=(h == 0), stop=(h == 1))
                last.then_inc(gu_ready, 1)

            def turn_a(q, t):
                pe.wait_ge(act_ready, q * S + t + 1)
                if not first(q) or t > 1:
                    pe.wait_ge(aT_ready, q * S + (t - 1))
                nc.tensor.transpose(banks[PA + t % 2][:, 0:P], a_sb[:, t % 2, :], ident[:, :]).then_inc(pa_ready, 1)

            def down(q, t):
                pe.wait_ge(aT_ready, q * S + (t + 1))
                if not first(q) or t > 1:
                    pe.wait_ge(y_added, q * S + (t - 1))
                nc.tensor.matmul(banks[Y + t % 2][:, 0:D], aT[:, t % 2, :], w_sh[:, 4 * I:WCOLS],
                                 start=True, stop=True).then_inc(y_ready, 1)

            def step(q):
                for t in range(S):
                    if exists(q, t + 2):
                        turn_x(q, t + 2)
                    if exists(q, t + 1):
                        gate_up(q, t + 1)
                    turn_a(q, t)
                    if exists(q, t - 1):
                        down(q, t - 1)

            pe.wait_ge(shared_in, 16 * 5)
            turn_x(0, 0)
            turn_x(0, 1)
            gate_up(0, 0)
            every(pe, step)
            down(NQ - 1, S - 1)

        @block.scalar
        def _(act):
            def place(q, j):
                nc.scalar.copy(xp[:, j % 2, :, :], x_all[:, bass.ds(q * S + 2 * j, 2), :]
                               ).then_inc(x_placed, 1)

            def copy_x(q, t):
                if not first(q) or t > 1:
                    act.wait_ge(gu_ready, q * S + (t - 1))
                act.wait_ge(px_ready, q * S + t + 1)
                nc.scalar.copy(xT[:, t % 2, :, :].rearrange("p h q -> p (h q)"), banks[PX + t % 2][:, 0:D]
                               ).then_inc(xT_ready, 1)
                if t % 2 == 1 and exists(q, t + 4):
                    place(q, t // 2 + 2)

            def silu(q, t):
                if not first(q) or t > 1:
                    act.wait_ge(act_ready, q * S + (t - 1))
                act.wait_ge(gu_ready, q * S + t + 1)
                nc.scalar.activation(gate[:, t % 2, :], banks[GU + t % 2][:, 0:I], ACT.Silu).then_inc(gate_ready, 1)

            def step(q):
                for t in range(S):
                    if exists(q, t + 2):
                        copy_x(q, t + 2)
                    if exists(q, t + 1):
                        silu(q, t + 1)
                    if t % 2 == 1 and exists(q, t - 2):
                        store(q, t // 2 - 1)

            def store(q, j):
                act.wait_ge(sum_ready, q * (S // 2) + (j + 1))
                act.dma_start(out[bass.ds(q * S + 2 * j, 2), :, :].rearrange("n p c -> p n c"),
                              res[:, bass.ds(q * S + 2 * j, 2), :]).then_inc(stored, 16)

            act.wait_ge(shared_in, 16 * 5)
            for j in range(2):
                place(0, j)
            copy_x(0, 0)
            copy_x(0, 1)
            silu(0, 0)
            every(act, step)
            store(NQ - 1, S // 2 - 1)
            act.wait_ge(stored, 16 * (NTILE // 2))

        @block.gpsimd
        def _(pool):
            with pool.Fori(0, NQ) as q:
                for j in range(S // 2):
                    pool.wait_ge(acc_in[j], q * (16 * NACC) + 16 * NACC)
                    nc.gpsimd.tensor_tensor(acc[:, j, 2, :, :], acc[:, j, 2, :, :], acc[:, j, 3, :, :],
                                            ALU.add).then_inc(half_b, 1)

        @block.vector
        def _(dve):
            def product(q, t):
                if not first(q) or t > 1:
                    dve.wait_ge(pa_ready, q * S + (t - 1))
                dve.wait_ge(gate_ready, q * S + t + 1)
                nc.vector.tensor_tensor(a_sb[:, t % 2, :], gate[:, t % 2, :], banks[GU + t % 2][:, I:2 * I],
                                        ALU.mult).then_inc(act_ready, 1)

            def copy_a(q, t):
                if not first(q) or t > 1:
                    dve.wait_ge(y_ready, q * S + (t - 1))
                dve.wait_ge(pa_ready, q * S + t + 1)
                nc.vector.tensor_copy(aT[:, t % 2, :], banks[PA + t % 2][:, 0:P]).then_inc(aT_ready, 1)

            def add_y(q, t):
                j = t // 2
                dve.wait_ge(acc_in[j], q * (16 * NACC) + 16 * NACC)
                dve.wait_ge(y_ready, q * S + (t + 1))
                nc.vector.tensor_tensor(acc[:, j, 0, t % 2, :], banks[Y + t % 2][:, 0:D], acc[:, j, 0, t % 2, :],
                                        ALU.add).then_inc(y_added, 1)

            def add_pair(q, j):
                slot = j % (S // 2)
                a0, a1, a2 = (acc[:, slot, k, :, :] for k in range(3))
                r = res[:, bass.ds(q * S + 2 * j, 2), :]
                dve.wait_ge(half_b, q * (S // 2) + (j + 1))
                nc.vector.tensor_tensor(a1, a1, a2, ALU.add).then_inc(half_a, 1)
                dve.wait_ge(y_added, q * S + (2 * j + 2))
                nc.vector.tensor_tensor(r, r, a0, ALU.add).then_inc(both, 1)
                dve.wait_ge(half_a, q * (S // 2) + (j + 1))
                dve.wait_ge(both, q * (S // 2) + (j + 1))
                nc.vector.tensor_tensor(r, r, a1, ALU.add).then_inc(sum_ready, 1)

            def step(q):
                for t in range(S):
                    copy_a(q, t)
                    if exists(q, t + 1):
                        product(q, t + 1)
                    if exists(q, t - 1):
                        add_y(q, t - 1) if t > 0 else add_y_before(q)
                    if t % 2 == 0 and exists(q, t - 2):
                        add_pair(q, t // 2 - 1)

            def add_y_before(q):
                j = S // 2 - 1
                dve.wait_ge(acc_in[j], q * (16 * NACC))
                dve.wait_ge(y_ready, q * S)
                nc.vector.tensor_tensor(acc[:, j, 0, 1, :], banks[Y + 1][:, 0:D], acc[:, j, 0, 1, :],
                                        ALU.add).then_inc(y_added, 1)

            product(0, 0)
            every(dve, step)
            add_y(NQ - 1, S - 1)
            add_pair(NQ - 1, S // 2 - 1)


def build(nc, x, w_qk, w_vr, w_proj, w_exp, c_f32, c_ids, out):
    with ExitStack() as ctx:
        def sb(name, shape, dt=F32):
            return ctx.enter_context(nc.sbuf_tensor(name, shape, dt))

        def dram(name, shape, dt=F32):
            return nc.dram_tensor(name, shape, dt, kind="Internal").ap()

        psum = ctx.enter_context(nc.psum_tensor("psum", [P, 8, 512], F32))
        keep = {
            "dram": (dram("qk_stacks", (KS // DK, B * D, 2, T), BF16), dram("token_rows", (NTOK, ROW)),
                     dram("slot_rows", ((NB_ROUTED + 1) * P, ROW)), dram("block_table", (NFIELD, MB * P), I32),
                     [dram(f"acc{i}", (NTOK + P, D)) for i in range(NACC)]),
            "psum": psum,
            "shared": (sb("w_sh", [P, WCOLS]), ctx.enter_context(nc.semaphore("shared_in"))),
            "fill": (sb("template", [P, ROW]), sb("blk_table", [P, 2, NE], I32)),
            "routing": (sb("consts_f32", [P, 6 * P + 2 * MB]), sb("chosen", [P, TPC + NTILE, NE], BF16),
                        sb("base", [P, NCH + 2, NE]), sb("slot", [P, TPC + NTILE, NE]),
                        sb("blk", [P, 5, NE]), sb("blk_i", [P, NE], I32), sb("junk", [P, NE]),
                        sb("top8", [P, NTILE, K]), sb("cols", [P, 7, MB]), sb("meta_c", [P, NFIELD, MB], I32)),
            "sbuf": (sb("ident", [P, P]), sb("consts_bf16", [P, 5 * P], BF16), sb("v_sb", [P, NU, TT, DK]),
                     sb("block_table_row", [1, NFIELD, MB * P], I32), sb("slots_of_tokens", [P, NTILE, K], I32),
                     sb("zeros", [P, 1024]), [psum[:, i, :] for i in range(8)]),
        }
        with ExitStack() as inner:
            project(nc, inner, x, w_qk, w_vr, c_f32, c_ids, keep)
        res, wp = sb("res", [P, NTILE, D]), sb("wp", [P, 2, D])
        m_in = ctx.enter_context(nc.semaphore("m_in"))
        with ExitStack() as inner:
            onorm = inner.enter_context(nc.sbuf_tensor("onorm", [P, NG * TT, HG * DK], F32))
            with ExitStack() as deeper:
                attend(nc, deeper, keep, onorm, x, w_proj, res, wp, m_in)
            loads = expert_loads(nc, inner, keep, w_exp)
            with ExitStack() as deeper:
                merge(nc, deeper, keep, onorm, res, wp, m_in, loads)
            with ExitStack() as deeper:
                experts(nc, deeper, keep, loads, w_exp)
        with ExitStack() as inner:
            finish(nc, inner, keep, res, out)


def constants():
    r, c = np.arange(P)[:, None], np.arange(P)[None, :]
    f = np.zeros((P, 6 * P + 2 * MB), np.float32)
    f[:, 0:P] = r == c
    f[:, P:2 * P] = r == c
    f[:, 2 * P:3 * P] = r < c
    f[:, 3 * P:4 * P] = 1.0
    f[:, 4 * P:5 * P] = np.where(r > c, NEG, 0.0)
    f[:, 5 * P:6 * P] = np.where(c > r, NEG, 0.0)
    f[:, 6 * P:6 * P + MB] = r + P * np.arange(MB)[None, :]
    f[:, 6 * P + MB:] = f[:, 6 * P:6 * P + MB] - 1
    ids = np.zeros((P, NTILE + 1), np.int32)
    ids[:, :] = r + P * np.arange(NTILE + 1)[None, :]
    return f, ids


def kernel(L0_attn_x, L0_attn_w_qkv, L0_attn_w_proj, L0_ffn_router_w, L0_ffn_shared_gate_w,
           L0_ffn_shared_up_w, L0_ffn_shared_down_w, L0_ffn_expert_gate_k, L0_ffn_expert_up_k,
           L0_ffn_expert_down_k):
    import concourse.bacc as bacc
    from concourse.bass_utils import run_bass_kernel_spmd

    def halves(w):
        return np.ascontiguousarray(w.reshape(2, P, -1).transpose(1, 0, 2))

    w_qkv = np.asarray(L0_attn_w_qkv)
    gates = np.concatenate([np.asarray(L0_ffn_expert_gate_k), np.asarray(L0_ffn_shared_gate_w)[None]])
    ups = np.concatenate([np.asarray(L0_ffn_expert_up_k), np.asarray(L0_ffn_shared_up_w)[None]])
    downs = np.concatenate([np.asarray(L0_ffn_expert_down_k), np.asarray(L0_ffn_shared_down_w)[None]])
    gu = np.concatenate([gates, ups], axis=2).reshape(NE + 1, 2, P, 2 * I).transpose(0, 2, 1, 3)
    c_f32, c_ids = constants()
    arrays = {
        "x": np.ascontiguousarray(np.asarray(L0_attn_x).reshape(NTILE, P, D)),
        "w_qk": halves(w_qkv[0:2 * D].T),
        "w_vr": halves(np.concatenate([w_qkv[2 * D:3 * D].T, np.asarray(L0_ffn_router_w)], axis=1)),
        "w_proj": halves(np.asarray(L0_attn_w_proj).T),
        "w_exp": np.ascontiguousarray(np.concatenate([gu.reshape(NE + 1, P, 4 * I), downs], axis=2)),
        "c_f32": c_f32,
        "c_ids": c_ids,
    }
    nc = bacc.Bacc("TRN2", target_bir_lowering=False, num_devices=1)
    ins = [nc.dram_tensor("in_" + k, a.shape, mybir.dt.from_np(a.dtype), kind="ExternalInput").ap()
           for k, a in arrays.items()]
    out = nc.dram_tensor("out", (NTILE, P, D), F32, kind="ExternalOutput").ap()
    build(nc, *ins, out)
    r = run_bass_kernel_spmd(nc, [{"in_" + k: a for k, a in arrays.items()}], core_ids=[0])
    return r.results[0]["out"].reshape(B, T, D)
```
